# Optimizing a Trainium2 kernel written in Bass

```python
import numpy as np
import jax
import jax.numpy as jnp

def _softmax(x, axis=-1):
    return jax.nn.softmax(x, axis=axis)

def _gelu(x):
    return jax.nn.gelu(x, approximate=True)

def _silu(x):
    return jax.nn.silu(x)

def _sigmoid(x):
    return jax.nn.sigmoid(x)

def _layernorm(x, axis=-1, eps=1e-05):
    m = jnp.mean(x, axis=axis, keepdims=True)
    v = jnp.var(x, axis=axis, keepdims=True)
    return (x - m) / jnp.sqrt(v + eps)

def _scatter_add(tgt, idx, src, axis=0):
    return tgt.at[idx].add(src)

def _segment_sum(src, seg, n):
    return jax.ops.segment_sum(src, seg, n)
kernel_name = 'mk_adaln_d1_jaxref_r4_6a7c77'

def setup_inputs(seed: int=0):
    np.random.seed(seed)
    _w = jnp.asarray

    def _L0_attn_setup():
        import jax, jax.numpy as jnp
        import numpy as np
        N_HEAD = 32
        ROPE_BASE = 10000.0

        def _rope_cos_sin(T, n_elem, dtype):
            theta = 1.0 / ROPE_BASE ** (jnp.arange(0, n_elem, 2, dtype=dtype) / n_elem)
            seq_idx = jnp.arange(T, dtype=dtype)
            idx_theta = jnp.outer(seq_idx, theta)
            idx_theta2 = jnp.concatenate([idx_theta, idx_theta], axis=-1)
            return (jnp.cos(idx_theta2), jnp.sin(idx_theta2))

        def _apply_rope(x, cos, sin):
            d2 = x.shape[-1] // 2
            rot = jnp.concatenate([-x[..., d2:], x[..., :d2]], axis=-1)
            return x * cos + rot * sin
        key = jax.random.key(seed)
        k1, k2, k3, k4 = jax.random.split(key, 4)
        B, T, C = (1, 512, 1024)
        s_in = 1.0 / np.sqrt(C)
        return {'x': jax.random.normal(k1, (B, T, C), jnp.float32), 'w_attn': jax.random.normal(k2, (3 * C, C), jnp.float32) * s_in, 'w_proj': jax.random.normal(k3, (C, C), jnp.float32) * s_in, 'adapter_wte': jax.random.normal(k4, (10, C), jnp.float32), 'gating': jnp.ones((1,), jnp.float32)}
    _L0_attn_in = _L0_attn_setup()

    def _L0_ffn_setup():
        import jax, jax.numpy as jnp
        import numpy as np
        TOP_K = 2
        key = jax.random.key(seed)
        k1, k2, k3 = jax.random.split(key, 3)
        B, S, H, O, E = (2048, 1, 1024, 1024, 8)
        x = jax.random.normal(k1, (B, S, H), dtype=jnp.float32)
        gate_w = jax.random.normal(k2, (H, E), dtype=jnp.float32) * 0.02
        expert_w = jax.random.normal(k3, (E, H, O), dtype=jnp.float32) * 0.02
        return {'x': x, 'gate_w': gate_w, 'expert_w': expert_w}
    _L0_ffn_in = _L0_ffn_setup()
    _L0_c = _w((lambda *s: np.random.randn(*s).astype(np.float32) * 0.05)(1, 1024))
    _L0_wmod = _w((lambda *s: np.random.randn(*s).astype(np.float32) * 0.05)(1024, 6 * 1024) * 1024 ** (-0.5))
    _d = {'L0_attn_x': _L0_attn_in['x'], 'L0_attn_w_attn': _L0_attn_in['w_attn'], 'L0_attn_w_proj': _L0_attn_in['w_proj'], 'L0_attn_adapter_wte': _L0_attn_in['adapter_wte'], 'L0_attn_gating': _L0_attn_in['gating'], 'L0_ffn_gate_w': _L0_ffn_in['gate_w'], 'L0_ffn_expert_w': _L0_ffn_in['expert_w'], 'L0_c': _L0_c, 'L0_wmod': _L0_wmod}
    _x0 = _d['L0_attn_x']
    _d['L0_attn_x'] = jax.random.normal(jax.random.fold_in(jax.random.key(seed), 1), (1, 2048, 1024), dtype=_x0.dtype)
    del _x0
    return _d

def reference(L0_attn_x, L0_attn_w_attn, L0_attn_w_proj, L0_attn_adapter_wte, L0_attn_gating, L0_ffn_gate_w, L0_ffn_expert_w, L0_c, L0_wmod):

    def _L0_attn_ref(x, w_attn, w_proj, adapter_wte, gating):
        import jax, jax.numpy as jnp
        import numpy as np
        N_HEAD = 32
        ROPE_BASE = 10000.0

        def _rope_cos_sin(T, n_elem, dtype):
            theta = 1.0 / ROPE_BASE ** (jnp.arange(0, n_elem, 2, dtype=dtype) / n_elem)
            seq_idx = jnp.arange(T, dtype=dtype)
            idx_theta = jnp.outer(seq_idx, theta)
            idx_theta2 = jnp.concatenate([idx_theta, idx_theta], axis=-1)
            return (jnp.cos(idx_theta2), jnp.sin(idx_theta2))

        def _apply_rope(x, cos, sin):
            d2 = x.shape[-1] // 2
            rot = jnp.concatenate([-x[..., d2:], x[..., :d2]], axis=-1)
            return x * cos + rot * sin
        B, T, C = x.shape
        H = N_HEAD
        hd = C // H
        qkv = jnp.einsum('btc,oc->bto', x, w_attn)
        q, k, v = jnp.split(qkv, 3, axis=-1)
        q = q.reshape(B, T, H, hd).transpose(0, 2, 1, 3)
        k = k.reshape(B, T, H, hd).transpose(0, 2, 1, 3)
        v = v.reshape(B, T, H, hd).transpose(0, 2, 1, 3)
        cos, sin = _rope_cos_sin(T, hd, x.dtype)
        q = _apply_rope(q, cos, sin)
        k = _apply_rope(k, cos, sin)
        scores = jnp.einsum('bhqd,bhkd->bhqk', q, k) / jnp.sqrt(jnp.asarray(hd, x.dtype))
        causal = jnp.tril(jnp.ones((T, T), bool))
        scores = jnp.where(causal, scores, jnp.asarray(-jnp.inf, x.dtype))
        attn = jax.nn.softmax(scores, axis=-1)
        y = jnp.einsum('bhqk,bhkd->bhqd', attn, v)
        aT = adapter_wte.shape[0]
        prefix = adapter_wte[None]
        aqkv = jnp.einsum('btc,oc->bto', prefix, w_attn)
        _, ak, av = jnp.split(aqkv, 3, axis=-1)
        ak = ak.reshape(1, aT, H, hd).transpose(0, 2, 1, 3)
        av = av.reshape(1, aT, H, hd).transpose(0, 2, 1, 3)
        ascores = jnp.einsum('bhqd,xhkd->bhqk', q, ak) / jnp.sqrt(jnp.asarray(C, x.dtype))
        ascores = gating[0] * jax.nn.softmax(ascores.astype(jnp.float32), axis=-1).astype(q.dtype)
        y = y + jnp.einsum('bhqk,xhkd->bhqd', ascores, av)
        y = y.transpose(0, 2, 1, 3).reshape(B, T, C)
        return jnp.einsum('btc,oc->bto', y, w_proj)

    def _L0_ffn_ref(x, gate_w, expert_w):
        import jax, jax.numpy as jnp
        import numpy as np
        TOP_K = 2
        E = gate_w.shape[-1]
        logits = jnp.einsum('bsh,he->bse', x, gate_w)
        topv, topi = jax.lax.top_k(logits, TOP_K)
        w = jax.nn.softmax(topv, axis=-1)
        onehot = jax.nn.one_hot(topi, E, dtype=x.dtype)
        w_e = jnp.einsum('bske,bsk->bse', onehot, w)
        out = jnp.einsum('bsh,eho,bse->bso', x, expert_w, w_e)
        return out
    x = L0_attn_x
    mod = (_silu(L0_c) @ L0_wmod).reshape(L0_c.shape[0], 6, 1, -1)
    sa, ca, ga, sb, cb, gb = (mod[:, 0], mod[:, 1], mod[:, 2], mod[:, 3], mod[:, 4], mod[:, 5])
    ga = (2 * (ga >= 0) - 1) * jnp.maximum(jnp.abs(ga), 0.25)
    gb = (2 * (gb >= 0) - 1) * jnp.maximum(jnp.abs(gb), 0.25)
    h = _layernorm(x, axis=-1) * (1 + ca) + sa
    x = x + ga * _L0_attn_ref(h, L0_attn_w_attn, L0_attn_w_proj, L0_attn_adapter_wte, L0_attn_gating)
    h = _layernorm(x, axis=-1) * (1 + cb) + sb
    x = x + gb * _L0_ffn_ref(h, L0_ffn_gate_w, L0_ffn_expert_w)
    return x

_drawn_inputs = setup_inputs


def setup_inputs(seed=0):
    import zlib

    import numpy as np

    out = dict(_drawn_inputs(seed))
    spreads = {}
    factors = {}
    for name, (base, spread) in spreads.items():
        noise = np.random.default_rng([zlib.crc32(name.encode()), seed]).standard_normal(out[name].shape)
        drawn = base * np.exp(spread * noise) if base else spread * noise
        out[name] = jnp.asarray(drawn.astype(out[name].dtype))
    for name, factor in factors.items():
        out[name] = (out[name] * factor).astype(out[name].dtype)
    return out
```

```python
import math
from contextlib import ExitStack, contextmanager

import concourse.bass as bass
from concourse import mybir

ALU = mybir.AluOpType
ACT = mybir.ActivationFunctionType
AX = mybir.AxisListType
F32 = mybir.dt.float32
F32R = mybir.dt.float32r
I32 = mybir.dt.int32
U32 = mybir.dt.uint32

P = 128
T, C = 2048, 1024
H, D = 32, 32
E = 8
A = 10
CH = 512
KC = C // P
NT = T // P
NQ = T // CH
TPC = CH // P
HG = P // D
G = H // HG
EPS = 1e-5
LOOKS = 2


def ds(i, n=1):
    return bass.ds(i, n)


class Steps:

    def __init__(self, eng, sem, base=0):
        self.eng, self.sem, self.base, self.n = eng, sem, base, 0

    def link(self, ins):
        self.n += 1
        ins.then_inc(self.sem, 1)
        self.eng.wait_ge(self.sem, self.base + self.n)


def modulation(nc, sem, c, wmod, mod_rows):
    with ExitStack() as ctx:
        sb = lambda name, shape, dt: ctx.enter_context(nc.sbuf_tensor(name, shape, dt))
        UN = 6
        c_col = sb("c_col", [P, KC], F32)
        c_sig = sb("c_sig", [P, KC], F32)
        silu = sb("silu", [P, KC], F32)
        wbuf = sb("wmod_buf", [P, 3, KC, CH], F32)
        row = sb("mod_row", [1, 2, 3 * C], F32)
        gate = sb("gate", [1, CH], F32)
        gate_sign = sb("gate_sign", [1, CH], F32)
        gate_size = sb("gate_size", [1, CH], F32)
        acc = ctx.enter_context(nc.psum_tensor("mod_acc", [1, 2, CH], F32))
        c_loaded, silu_step, silu_ready = sem("c_loaded"), sem("silu_step"), sem("silu_ready")
        sig_ready = sem("sig_ready")
        w_loaded = [sem(f"wmod_loaded{b}") for b in range(3)]
        mod_acc_ready, mod_acc_free = sem("mod_acc_ready"), sem("mod_acc_free")
        mod_step, row_done, mod_stored = sem("mod_step"), sem("mod_row_done"), sem("mod_stored")
        w_view = wmod.rearrange("(k p) (n j) -> n p k j", p=P, j=CH)
        block = ctx.enter_context(nc.Block())

        @block.sync
        def _(sp):
            sp.dma_start(c_col[:, :], c).then_inc(c_loaded, 16)
            with sp.Fori(0, 2) as i:
                for u in range(UN):
                    sp.wait_ge(mod_acc_free, i * UN + u + 1)
                    sp.dma_start(wbuf[:, u % 3], w_view[ds(i * UN + u)].rearrange("a p k j -> (a p) k j")).then_inc(w_loaded[u % 3], 16)
            sp.wait_ge(row_done, 2 * UN)
            sp.dma_start(mod_rows.rearrange("(a n) -> a n", a=1), row[:, :, :].rearrange("a b n -> a (b n)")).then_inc(mod_stored, 16)
            sp.wait_ge(mod_stored, 16)

        @block.scalar
        def _(act):
            nc.scalar.preload_act_table(ACT.Exp)
            act.wait_ge(c_loaded, 16)
            nc.scalar.activation(c_sig[:, :], c_col[:, :], ACT.Exp, scale=-1.0).then_inc(sig_ready, 1)

        @block.vector
        def _(dve):
            dve.sem_inc(mod_acc_free, 3)
            dve.wait_ge(sig_ready, 1)
            s = Steps(dve, silu_step)
            s.link(nc.vector.tensor_scalar(silu[:, :], c_sig[:, :], 1.0, None, ALU.add))
            s.link(nc.vector.reciprocal(c_sig[:, :], silu[:, :]))
            nc.vector.tensor_tensor(silu[:, :], c_col[:, :], c_sig[:, :], ALU.mult).then_inc(silu_ready, 1)
            with dve.Fori(0, 2) as i:
                s = Steps(dve, mod_step, i * 8)
                for u in range(UN):
                    dst = row[:, ds(i), u * CH:(u + 1) * CH].rearrange("a b n -> a (b n)")
                    src = acc[:, u % 2]
                    dve.wait_ge(mod_acc_ready, i * UN + u + 1)
                    if u // 2 == 0:
                        last = nc.vector.tensor_copy(dst, src)
                    elif u // 2 == 1:
                        last = nc.vector.tensor_scalar(dst, src, 1.0, None, ALU.add)
                    else:
                        s.link(nc.vector.tensor_copy(gate[:, :], src))
                        s.link(nc.vector.tensor_scalar(gate_sign[:, :], gate[:, :], 0.0, 2.0, ALU.is_ge, ALU.mult))
                        s.link(nc.vector.scalar_tensor_tensor(out=gate_size[:, :], in0=gate[:, :], scalar=-1.0, in1=gate[:, :],
                                                              op0=ALU.mult, op1=ALU.max))
                        s.link(nc.vector.tensor_scalar(gate_size[:, :], gate_size[:, :], 0.25, None, ALU.max))
                        last = nc.vector.scalar_tensor_tensor(out=dst, in0=gate_sign[:, :], scalar=-1.0, in1=gate_size[:, :],
                                                              op0=ALU.add, op1=ALU.mult)
                    last.then_inc(row_done, 1)
                    dve.wait_ge(row_done, i * UN + u + 1)
                    nc.vector.sem_inc(mod_acc_free, 1)

        @block.tensor
        def _(pe):
            pe.wait_ge(silu_ready, 1)
            with pe.Fori(0, 2) as i:
                for u in range(UN):
                    pe.wait_ge(w_loaded[u % 3], i * 32 + 16 * (u // 3 + 1))
                    pe.wait_ge(mod_acc_free, i * UN + u + 2)
                    for k in range(KC):
                        last = nc.tensor.matmul(acc[:, u % 2], silu[:, k:k + 1], wbuf[:, u % 3, k], start=(k == 0), stop=(k == KC - 1))
                    last.then_inc(mod_acc_ready, 1)


def norm_in(nc, sem, x, mod_rows, identity, hT_hi, hT_lo):
    with ExitStack() as ctx:
        sb = lambda name, shape, dt: ctx.enter_context(nc.sbuf_tensor(name, shape, dt))
        ident = sb("n_ident", [P, P], F32)
        scale_b = sb("n_scale", [P, C], F32)
        shift_b = sb("n_shift", [P, C], F32)
        xt = sb("n_x", [P, TPC, C], F32)
        ht = sb("n_h", [P, TPC, C], F32)
        stats = sb("n_stats", [P, TPC, 2, 6], F32)
        mv = sb("n_mv", [P, TPC, 2], F32)
        std = sb("n_std", [P, TPC], F32)
        rstd = sb("n_rstd", [P, TPC], F32)
        newton = sb("n_newton", [P, TPC], F32)
        turned = ctx.enter_context(nc.psum_tensor("n_turned", [P, KC, CH], F32))
        const_loaded = sem("n_const_loaded")
        x_loaded = [sem(f"n_x_loaded{j}") for j in range(TPC)]
        x_free, h_free, bank_free = sem("n_x_free"), sem("n_h_free"), sem("n_bank_free")
        stat_step, var_ready, std_ready, xn_ready = sem("n_stat_step"), sem("n_var_ready"), sem("n_std_ready"), sem("n_xn_ready")
        stats_in = sem("n_stats_in")
        scaled, h_ready, bank_ready, hi_done = sem("n_scaled"), sem("n_h_ready"), sem("n_bank_ready"), sem("n_hi_done")
        block = ctx.enter_context(nc.Block())

        @block.sync
        def _(sp):
            sp.dma_start(ident[:, :], identity).then_inc(const_loaded, 16)
            sp.dma_start(shift_b[:, :], mod_rows[0:C].rearrange("(a n) -> a n", a=1).broadcast_to([P, C])).then_inc(const_loaded, 16)
            sp.dma_start(scale_b[:, :], mod_rows[C:2 * C].rearrange("(a n) -> a n", a=1).broadcast_to([P, C])).then_inc(const_loaded, 16)
            with sp.Fori(0, NQ) as i:
                for j in range(TPC):
                    sp.wait_ge(x_free, i * TPC + j + 1)
                    sp.dma_start(xt[:, j], x[ds((i * TPC + j) * P, P), :]).then_inc(x_loaded[j], 16)

        @block.vector
        def _(dve):
            dve.sem_inc(bank_free, KC)
            with dve.Fori(0, NQ) as i:
                s = Steps(dve, stat_step, i * (2 * TPC + 6))
                for j in range(TPC):
                    dve.wait_ge(x_loaded[j], i * 16 + 16)
                    nc.vector.bn_stats(stats[:, j, 0], xt[:, j, 0:CH])
                    s.link(nc.vector.bn_stats(stats[:, j, 1], xt[:, j, CH:C]))
                    nc.vector.sem_inc(stats_in, 1)
                    s.link(nc.vector.bn_aggr(mv[:, j], stats[:, j].rearrange("p a b -> p (a b)")))
                s.link(nc.vector.tensor_scalar(mv[:, :, 1], mv[:, :, 1], EPS, None, ALU.add))
                nc.vector.sem_inc(var_ready, 1)
                dve.wait_ge(std_ready, i + 1)
                s.link(nc.vector.reciprocal(rstd[:, :], std[:, :]))
                s.link(nc.vector.tensor_tensor(newton[:, :], rstd[:, :], rstd[:, :], ALU.mult))
                s.link(nc.vector.tensor_tensor(newton[:, :], newton[:, :], mv[:, :, 1], ALU.mult))
                s.link(nc.vector.tensor_scalar(newton[:, :], newton[:, :], -0.5, 1.5, ALU.mult, ALU.add))
                s.link(nc.vector.tensor_tensor(rstd[:, :], rstd[:, :], newton[:, :], ALU.mult))
                for j in range(TPC):
                    nc.vector.tensor_scalar(xt[:, j], xt[:, j], mv[:, j, 0:1], rstd[:, j:j + 1], ALU.subtract, ALU.mult).then_inc(xn_ready, 1)
                for k in range(KC):
                    dve.wait_ge(hi_done, i * KC + k + 1)
                    col = ds(i * CH, CH)
                    nc.vector.tensor_tensor(hT_lo[:, k, col], turned[:, k], hT_hi[:, k, col], ALU.subtract).then_inc(bank_free, 1)

        @block.gpsimd
        def _(pool):
            pool.sem_inc(x_free, TPC)
            pool.sem_inc(h_free, TPC)
            pool.wait_ge(const_loaded, 48)
            with pool.Fori(0, NQ) as i:
                for j in range(TPC):
                    pool.wait_ge(xn_ready, i * TPC + j + 1)
                    pool.wait_ge(h_free, i * TPC + j + 1)
                    nc.gpsimd.tensor_tensor(ht[:, j], xt[:, j], scale_b[:, :], ALU.mult).then_inc(scaled, 1)
                    pool.wait_ge(scaled, i * TPC + j + 1)
                    nc.gpsimd.tensor_tensor(ht[:, j], ht[:, j], shift_b[:, :], ALU.add).then_inc(h_ready, 1)
                    nc.gpsimd.sem_inc(x_free, 1)

        @block.tensor
        def _(pe):
            pe.wait_ge(const_loaded, 48)
            with pe.Fori(0, NQ) as i:
                for j in range(TPC):
                    pe.wait_ge(h_ready, i * TPC + j + 1)
                    for k in range(KC):
                        if j == 0:
                            pe.wait_ge(bank_free, i * KC + k + 1)
                        last = nc.tensor.transpose(turned[:, k, j * P:(j + 1) * P], ht[:, j, k * P:(k + 1) * P], ident[:, :])
                        if j == TPC - 1:
                            last.then_inc(bank_ready, 1)
                    if j < TPC - 1:
                        last.then_inc(h_free, 1)
                    else:
                        pe.wait_ge(bank_ready, i * KC + KC)
                        nc.tensor.sem_inc(h_free, 1)

        @block.scalar
        def _(act):
            nc.scalar.preload_act_table(ACT.Sqrt)
            with act.Fori(0, NQ) as i:
                act.wait_ge(var_ready, i + 1)
                nc.scalar.activation(std[:, :], mv[:, :, 1], ACT.Sqrt).then_inc(std_ready, 1)
                for k in range(KC):
                    act.wait_ge(bank_ready, i * KC + k + 1)
                    nc.scalar.activation(hT_hi[:, k, ds(i * CH, CH)], turned[:, k], ACT.Copy).then_inc(hi_done, 1)

BODY = 2 * NQ


def product(nc, acc, lhs, rhs):
    for k in range(KC):
        nc.tensor.matmul(acc, lhs(0, k), rhs(0, k), start=(k == 0), stop=False)
        nc.tensor.matmul(acc, lhs(0, k), rhs(1, k), start=False, stop=False)
        last = nc.tensor.matmul(acc, lhs(1, k), rhs(0, k), start=False, stop=(k == KC - 1))
    return last


def project(nc, sem, kind, w_tiles, first, hT, consts, ad, outs):
    rope, adapted = kind != "v", kind != "q"
    with ExitStack() as ctx:
        sb = lambda name, shape, dt=F32: ctx.enter_context(nc.sbuf_tensor(f"{kind}_{name}", shape, dt))
        pb = lambda name, shape: ctx.enter_context(nc.psum_tensor(f"{kind}_{name}_psum", shape, F32))
        sm = lambda name: sem(f"{kind}_{name}")
        w_raw = sb("w_raw", [P, 2, C])
        w_hi = sb("w_hi", [P, 2, C], F32R)
        w_lo = sb("w_lo", [P, 2, C], F32R)
        acc = pb("acc", [P, 2, CH])
        if rope:
            cos = sb("cos", [P, T])
            sin = sb("sin", [P, T])
            x_cos = sb("x_cos", [P, CH])
            x_rot = sb("x_rot", [P, CH])
            y = sb("y", [P, 2, CH])
            y_hi = sb("y_hi", [P, 2, CH], F32R)
            y_lo = sb("y_lo", [P, 2, CH], F32R)
        else:
            ident = sb("ident", [P, P])
            vT = sb("vT", [P, 2, CH])
            v_out = sb("v_out", [P, 2, CH])
            turned = pb("turned", [P, 2, CH])
        if adapted:
            a_rep = sb("a_rep", [P, KC, HG, D])
            block_mask = sb("block_mask", [P, P])
            a_acc = pb("a_acc", [P, P])

        consts_loaded, w_raw_free = sm("consts_loaded"), sm("w_raw_free")
        w_loaded = [sm("w_loaded0"), sm("w_loaded1")]
        w_hi_done, w_ready, w_free = sm("w_hi_done"), sm("w_ready"), sm("w_free")
        acc_ready, acc_free = sm("acc_ready"), sm("acc_free")
        stored = [sm("stored0"), sm("stored1")]
        rep_cleared, rep_loaded, a_acc_ready, a_kept = sm("rep_cleared"), sm("rep_loaded"), sm("a_acc_ready"), sm("a_kept")
        rot_step, y_ready, y_hi_done, y_lo_done = sm("rot_step"), sm("y_ready"), sm("y_hi_done"), sm("y_lo_done")
        marks = sm("marks")
        vT_ready, turned_ready, v_out_ready = sm("vT_ready"), sm("turned_ready"), sm("v_out_ready")
        n_const = {"k": 3, "v": 2, "q": 2}[kind]
        STORES = 32 if rope else 16
        block = ctx.enter_context(nc.Block())

        @block.sync
        def _(sp):
            if rope:
                sp.dma_start(cos[:, :], consts["cos"]).then_inc(consts_loaded, 16)
                sp.dma_start(sin[:, :], consts["sin"]).then_inc(consts_loaded, 16)
            else:
                sp.dma_start(ident[:, :], consts["ident"]).then_inc(consts_loaded, 16)
            if adapted:
                sp.dma_start(block_mask[:, :], consts["block_mask"]).then_inc(consts_loaded, 16)
                sp.wait_ge(rep_cleared, 1)
                for h in range(HG):
                    sp.dma_start(a_rep[:, :, h, 0:A], consts["adapter"]).then_inc(rep_loaded, 16)
            with sp.Fori(0, G // 2) as i:
                for v in range(2):
                    sp.wait_ge(w_raw_free, i * 2 + v + 1)
                    sp.dma_start(w_raw[:, v], w_tiles[ds(i * 2 + (first + v))].rearrange("a p n -> (a p) n")).then_inc(w_loaded[v], 16)

        @block.gpsimd
        def _(pool):
            pool.sem_inc(w_raw_free, 2)
            if adapted:
                nc.gpsimd.memset(a_rep[:, :, :, :], 0.0).then_inc(rep_cleared, 1)
            with pool.Fori(0, G // 2) as i:
                for v in range(2):
                    pool.wait_ge(w_free, i * 2 + v + 1)
                    pool.wait_ge(w_loaded[v], i * 16 + 16)
                    pool.sem_inc(marks, 1)
                    nc.gpsimd.tensor_copy(w_hi[:, v], w_raw[:, v]).then_inc(w_hi_done, 1)
                    pool.wait_ge(w_hi_done, i * 2 + v + 1)
                    nc.gpsimd.tensor_tensor(w_lo[:, v], w_raw[:, v], w_hi[:, v], ALU.subtract).then_inc(w_ready, 1)
                    if not adapted:
                        pool.wait_ge(w_ready, i * 2 + v + 1)
                        pool.sem_inc(w_raw_free, 1)

        @block.tensor
        def _(pe):
            pe.sem_inc(w_free, 2)

            def turn_v(i, u):
                pe.wait_ge(vT_ready, i * BODY + u + 1)
                pe.wait_ge(v_out_ready, i * BODY + u + 1)
                for j in range(TPC):
                    last = nc.tensor.transpose(turned[:, u % 2, j * P:(j + 1) * P], vT[:, u % 2, j * P:(j + 1) * P], ident[:, :])
                last.then_inc(turned_ready, 1)

            if adapted:
                pe.wait_ge(rep_loaded, 16 * HG)
            pe.wait_ge(consts_loaded, 16 * n_const)
            with pe.Fori(0, G // 2) as i:
                for u in range(BODY):
                    v = u // NQ
                    if u % NQ == 0:
                        pe.wait_ge(w_ready, i * 2 + v + 1)
                        if adapted:
                            pe.wait_ge(a_kept, i * 2 + v + 1)
                            for k in range(KC):
                                rep = a_rep[:, k].rearrange("p h a -> p (h a)")
                                w = w_raw[:, v, k * P:(k + 1) * P]
                                last = nc.tensor.matmul(a_acc[:, :], *((w, rep) if kind == "k" else (rep, w)), start=(k == 0), stop=(k == KC - 1))
                            last.then_inc(a_acc_ready, 1)
                            pe.wait_ge(a_acc_ready, i * 2 + v + 1)
                            pe.sem_inc(w_raw_free, 1)
                    pe.wait_ge(acc_free, i * BODY + u + 1)
                    col = slice(u % NQ * CH, (u % NQ + 1) * CH)
                    product(nc, acc[:, u % 2],
                            lambda part, k: (w_hi, w_lo)[part][:, v, k * P:(k + 1) * P],
                            lambda part, k: hT[part][:, k, col]).then_inc(acc_ready, 1)
                    if kind == "v" and u >= 1:
                        turn_v(i, u - 1)
                    if u % NQ == NQ - 1:
                        pe.wait_ge(acc_ready, i * BODY + u + 1)
                        pe.sem_inc(w_free, 1)
                if kind == "v":
                    turn_v(i, BODY - 1)

        @block.scalar
        def _(act):
            nc.scalar.preload_act_table(ACT.Exp)
            with act.Fori(0, G // 2) as i:
                for u in range(BODY):
                    v, rows, n = u // NQ, ds((i * 2 + u // NQ)), i * BODY + u
                    if kind == "v":
                        act.wait_ge(acc_ready, n + 1)
                        act.wait_ge(turned_ready, n + 1)
                        nc.scalar.activation(vT[:, u % 2], acc[:, u % 2], ACT.Copy).then_inc(vT_ready, 1)
                        act.wait_ge(vT_ready, n + 1)
                        act.sem_inc(acc_free, 1)
                    else:
                        act.wait_ge(y_ready, n + 1)
                        act.wait_ge(stored[u % 2], i * (STORES * NQ) + STORES * (u // 2 + 1))
                        nc.scalar.activation(y_hi[:, u % 2], y[:, u % 2], ACT.Copy).then_inc(y_hi_done, 1)
                    for b in ([u - 1] if u else []) + ([u] if u == BODY - 1 else []):
                        g = ds(i * 2 + b // NQ)
                        if kind == "v":
                            act.wait_ge(v_out_ready, i * BODY + b + 3)
                            t0 = b % NQ * TPC
                            act.dma_start(outs[0][g, :, t0:t0 + TPC, :].rearrange("g p k n -> (g p) (k n)"), v_out[:, b % 2]).then_inc(stored[b % 2], 16)
                        else:
                            col = slice(b % NQ * CH, (b % NQ + 1) * CH)
                            act.wait_ge(y_lo_done, i * BODY + b + 1)
                            for part, src in ((0, y_hi), (1, y_lo)):
                                act.dma_start(outs[part][g, :, col].rearrange("g p n -> (g p) n"), src[:, b % 2].bitcast(F32)).then_inc(stored[b % 2], 16)
            for b in range(2):
                act.wait_ge(stored[b], STORES * (G * NQ // 2 + 1))

        @block.vector
        def _(dve):
            dve.sem_inc(acc_free, 2)
            for b in range(2):
                dve.sem_inc(stored[b], STORES)
            if kind == "v":
                dve.sem_inc(turned_ready, 2)
                dve.sem_inc(v_out_ready, 2)
            if adapted:
                dve.sem_inc(a_kept, 1)
            dve.wait_ge(consts_loaded, 16 * n_const)
            swap = [(d + D // 2) % D for d in range(D)]

            def keep_adapter(i, v):
                dve.wait_ge(a_acc_ready, i * 2 + v + 1)
                nc.vector.tensor_tensor(ad[:, ds(i * 2 + v)].rearrange("p a n -> p (a n)"), a_acc[:, :], block_mask[:, :],
                                        ALU.mult).then_inc(a_kept, 1)

            def rotate(i, u):
                s = Steps(dve, rot_step, i * (3 * BODY) + 3 * u)
                col = slice(u % NQ * CH, (u % NQ + 1) * CH)
                dve.wait_ge(acc_ready, i * BODY + u + 1)
                dve.sem_inc(marks, 1)
                nc.vector.stream_shuffle(x_rot[:, :], acc[:, u % 2], swap)
                s.link(nc.vector.tensor_tensor(x_cos[:, :], acc[:, u % 2], cos[:, col], ALU.mult))
                dve.sem_inc(acc_free, 1)
                s.link(nc.vector.tensor_tensor(x_rot[:, :], x_rot[:, :], sin[:, col], ALU.mult))
                dve.wait_ge(stored[u % 2], i * (STORES * NQ) + STORES * (u // 2 + 1))
                s.link(nc.vector.tensor_tensor(y[:, u % 2], x_cos[:, :], x_rot[:, :], ALU.add))
                dve.sem_inc(y_ready, 1)

            def split(i, u):
                dve.wait_ge(y_hi_done, i * BODY + u + 1)
                nc.vector.tensor_tensor(y_lo[:, u % 2], y[:, u % 2], y_hi[:, u % 2], ALU.subtract).then_inc(y_lo_done, 1)

            def out_v(i, u):
                dve.wait_ge(turned_ready, i * BODY + u + 3)
                dve.wait_ge(stored[u % 2], i * (STORES * NQ) + STORES * (u // 2 + 1))
                nc.vector.tensor_copy(v_out[:, u % 2], turned[:, u % 2]).then_inc(v_out_ready, 1)

            with dve.Fori(0, G // 2) as i:
                for u in range(BODY):
                    if adapted and u % NQ == 0:
                        keep_adapter(i, u // NQ)
                    if rope:
                        rotate(i, u)
                    if u >= 1:
                        (split if rope else out_v)(i, u - 1)
                (split if rope else out_v)(i, BODY - 1)


def adapter_attention(nc, sem, consts, ak, av, q_hi_d, q_lo_d, out):
    UN = NQ
    with ExitStack() as ctx:
        sb = lambda name, shape, dt=F32: ctx.enter_context(nc.sbuf_tensor(f"a_{name}", shape, dt))
        pb = lambda name, shape: ctx.enter_context(nc.psum_tensor(f"a_{name}_psum", shape, F32))
        sm = lambda name: sem(f"a_{name}")
        M = TPC * HG
        ident = sb("ident", [P, P])
        gating = sb("gating", [P, 1])
        q_hi, q_lo, q = sb("q_hi", [P, UN, CH]), sb("q_lo", [P, UN, CH]), sb("q", [P, UN, CH])
        av_cur = sb("av_cur", [P, P])
        top, total, inv = sb("top", [P, M]), sb("total", [P, M]), sb("inv", [P, M])
        weight = sb("weight", [P, UN, M, A])
        prob = sb("prob", [P, UN, M, D])
        probT = sb("probT", [P, 2, CH])
        y = sb("y", [P, UN, CH])
        scores, turned, acc = pb("scores", [P, 2, CH]), pb("turned", [P, 2, CH]), pb("acc", [P, 2, CH])
        consts_loaded, cleared = sm("consts_loaded"), sm("cleared")
        q_loaded = [sm(f"q_loaded{u}") for u in range(UN)]
        q_ready, q_used, scores_ready, step, shifted, exp_done = sm("q_ready"), sm("q_used"), sm("scores_ready"), sm("step"), sm("shifted"), sm("exp_done")
        prob_ready, turned_ready, probT_ready, av_ready, acc_ready, y_ready = (
            sm("prob_ready"), sm("turned_ready"), sm("probT_ready"), sm("av_ready"), sm("acc_ready"), sm("y_ready"))
        stored, marks = [sm(f"stored{u}") for u in range(UN)], sm("marks")
        block = ctx.enter_context(nc.Block())

        @block.sync
        def _(sp):
            sp.dma_start(ident[:, :], consts["ident"]).then_inc(consts_loaded, 16)
            sp.dma_start(gating[:, :], consts["gating"].rearrange("(a n) -> a n", a=1).broadcast_to([P, 1])).then_inc(consts_loaded, 16)
            with sp.Fori(0, G) as i:
                for u in range(UN):
                    sp.wait_ge(q_ready, i * UN + u + 1)
                    for src, dst in ((q_hi_d, q_hi), (q_lo_d, q_lo)):
                        sp.dma_start(dst[:, u], src[ds(i), :, u * CH:(u + 1) * CH].rearrange("g p n -> (g p) n")).then_inc(q_loaded[u], 16)

        @block.gpsimd
        def _(pool):
            pool.sem_inc(q_ready, UN)
            pool.sem_inc(acc_ready, UN)
            nc.gpsimd.memset(prob[:, :, :, :], 0.0).then_inc(cleared, 1)
            with pool.Fori(0, G) as i:
                pool.wait_ge(acc_ready, i * UN + UN)
                pool.sem_inc(marks, 1)
                nc.gpsimd.tensor_copy(av_cur[:, :], av[:, ds(i)].rearrange("p a n -> p (a n)")).then_inc(av_ready, 1)
                for u in range(UN):
                    pool.wait_ge(q_loaded[u], i * 32 + 32)
                    pool.wait_ge(q_used, i * UN + u + 1)
                    nc.gpsimd.tensor_tensor(q[:, u], q_hi[:, u], q_lo[:, u], ALU.add).then_inc(q_ready, 1)

        @block.tensor
        def _(pe):
            pe.sem_inc(q_used, UN)
            pe.wait_ge(consts_loaded, 32)

            def score(i, u):
                pe.wait_ge(q_ready, i * UN + u + 1 + UN)
                pe.wait_ge(shifted, i * UN + u + 1)
                for j in range(TPC):
                    last = nc.tensor.matmul(scores[:, u % 2, j * P:(j + 1) * P], q[:, u, j * P:(j + 1) * P],
                                            ak[:, ds(i)].rearrange("p a n -> p (a n)"), start=True, stop=True)
                last.then_inc(scores_ready, 1)
                pe.wait_ge(scores_ready, i * UN + u + 1)
                pe.sem_inc(q_used, 1)

            def turn(i, u):
                pe.wait_ge(prob_ready, i * UN + u + 1)
                pe.wait_ge(probT_ready, i * UN + u + 1)
                for j in range(TPC):
                    last = nc.tensor.transpose(turned[:, u % 2, j * P:(j + 1) * P],
                                               prob[:, u, j * HG:(j + 1) * HG, :].rearrange("p h a -> p (h a)"), ident[:, :])
                last.then_inc(turned_ready, 1)

            def multiply(i, u):
                pe.wait_ge(probT_ready, i * UN + u + 3)
                pe.wait_ge(av_ready, i + 1)
                pe.wait_ge(y_ready, i * UN + u + 1)
                nc.tensor.matmul(acc[:, u % 2], av_cur[:, :], probT[:, u % 2], start=True, stop=True).then_inc(acc_ready, 1)

            with pe.Fori(0, G) as i:
                for u in range(UN + 2):
                    if u < UN:
                        score(i, u)
                    if 1 <= u <= UN:
                        turn(i, u - 1)
                    if u >= 2:
                        multiply(i, u - 2)

        @block.vector
        def _(dve):
            dve.sem_inc(shifted, 2)
            dve.wait_ge(consts_loaded, 32)
            dve.wait_ge(cleared, 1)

            def shift(i, u, s):
                dve.wait_ge(scores_ready, i * UN + u + 1)
                dve.wait_ge(shifted, i * UN + u + 2)
                view = scores[:, u % 2].rearrange("p (m a) -> p m a", a=D)[:, :, 0:A]
                s.link(nc.vector.tensor_reduce(top[:, :], view, AX.X, ALU.max))
                nc.vector.tensor_tensor(weight[:, u], view, top[:, :].rearrange("p (m a) -> p m a", a=1).broadcast_to([P, M, A]),
                                        ALU.subtract).then_inc(shifted, 1)

            def norm(i, u, s):
                dve.wait_ge(exp_done, i * UN + u + 1)
                s.link(nc.vector.tensor_reduce(total[:, :], weight[:, u], AX.X, ALU.add))
                s.link(nc.vector.reciprocal(inv[:, :], total[:, :]))
                s.link(nc.vector.tensor_scalar(inv[:, :], inv[:, :], gating[:, 0:1], None, ALU.mult))
                s.link(nc.vector.tensor_tensor(prob[:, u, :, 0:A], weight[:, u],
                                               inv[:, :].rearrange("p (m a) -> p m a", a=1).broadcast_to([P, M, A]), ALU.mult))
                dve.sem_inc(prob_ready, 1)

            dve.sem_inc(prob_ready, 0) if False else None
            with dve.Fori(0, G) as i:
                s = Steps(dve, step, i * (5 * UN))
                for u in range(UN + 1):
                    if u < UN:
                        shift(i, u, s)
                    if u >= 1:
                        norm(i, u - 1, s)

        @block.scalar
        def _(act):
            nc.scalar.preload_act_table(ACT.Exp)
            act.sem_inc(probT_ready, 2)
            act.sem_inc(y_ready, 2)
            for u in range(UN):
                act.sem_inc(stored[u], 16)
            with act.Fori(0, G) as i:
                for u in range(UN + 2):
                    if u < UN:
                        act.wait_ge(shifted, i * UN + u + 3)
                        nc.scalar.activation(weight[:, u], weight[:, u], ACT.Exp, scale=1.0 / math.sqrt(C)).then_inc(exp_done, 1)
                    if 1 <= u <= UN:
                        b = u - 1
                        act.wait_ge(turned_ready, i * UN + b + 1)
                        act.wait_ge(acc_ready, i * UN + b + UN - 1)
                        nc.scalar.activation(probT[:, b % 2], turned[:, b % 2], ACT.Copy).then_inc(probT_ready, 1)
                    if u >= 2:
                        b = u - 2
                        act.wait_ge(acc_ready, i * UN + b + UN + 1)
                        act.wait_ge(stored[b], i * 16 + 16)
                        nc.scalar.activation(y[:, b], acc[:, b % 2], ACT.Copy).then_inc(y_ready, 1)
                        act.wait_ge(y_ready, i * UN + b + 3)
                        act.dma_start(out[ds(i), :, b * CH:(b + 1) * CH].rearrange("g p n -> (g p) n"), y[:, b]).then_inc(stored[b], 16)
            for u in range(UN):
                act.wait_ge(stored[u], 16 * (G + 1))

MASKED = -1.0e38
HALF = HG // 2
STACK = 3 * D


def attention(nc, sem, consts, q_parts, k_parts, v_d, a_d, out_parts, rows_d):
    UNITS = [(par, qc) for par in range(2) for qc in range(NQ)]
    W = len(UNITS)
    steps_of = lambda qc: TPC * (qc + 1)
    STEPS = sum(steps_of(qc) for _, qc in UNITS)
    items_of = lambda qc: HG * TPC * (qc + 1)
    ITEMS = sum(items_of(qc) for _, qc in UNITS) + W
    HEAD = items_of(0) + 1
    LOADS = 7 * 16
    ROW = HG * 16
    with ExitStack() as ctx:
        sb = lambda name, shape, dt=F32: ctx.enter_context(nc.sbuf_tensor(f"t_{name}", shape, dt))
        pb = lambda name, shape: ctx.enter_context(nc.psum_tensor(f"t_{name}_psum", shape, F32))
        sm = lambda name: sem(f"t_{name}")
        q_stack = [sb(f"q_stack{b}", [P, HG, T], F32R) for b in range(2)]
        k_stack = [sb(f"k_stack{b}", [P, HG, T], F32R) for b in range(2)]
        v = [sb(f"v{b}", [P, NT, P]) for b in range(2)]
        zeros = sb("zeros", [P, C])
        ident = sb("ident", [P, P])
        causal = sb("causal", [P, CH])
        ones = sb("ones", [P, D])
        unused = sb("unused", [P, CH])
        part = sb("part", [P, HG * TPC, NQ])
        top = sb("top", [P, HG * TPC])
        minus_top = sb("minus_top", [HG * TPC, 2, P], F32R)
        prob = sb("prob", [P, 2, 2, HALF, CH])
        total_inv, y_own = sb("total_inv", [P, CH]), sb("y_own", [P, CH])
        a_part = sb("a_part", [P, 2, CH])
        y = sb("y", [P, 2, CH])
        y_hi, y_lo = sb("y_hi", [P, 2, CH], F32R), sb("y_lo", [P, 2, CH], F32R)
        seen = pb("seen", [P, 2, CH])
        scores = pb("scores", [P, 2, HALF, CH])
        y_acc, total = pb("y_acc", [P, CH]), pb("total", [P, CH])

        consts_loaded, ones_set = sm("consts_loaded"), sm("ones_set")
        loaded, group_done = [sm("loaded0"), sm("loaded1")], sm("group_done")
        seen_ready, seen_free, top_ready, minus_ready = sm("seen_ready"), sm("seen_free"), sm("top_ready"), sm("minus_ready")
        row_loaded = [sm("row_loaded0"), sm("row_loaded1")]
        scores_ready, exp_done, masked, pv_done, acc_free = sm("scores_ready"), sm("exp_done"), sm("masked"), sm("pv_done"), sm("acc_free")
        a_loaded = [sm("a_loaded0"), sm("a_loaded1")]
        norm_step, y_ready, y_hi_done, y_lo_done = sm("norm_step"), sm("y_ready"), sm("y_hi_done"), sm("y_lo_done")
        stored = [sm("stored0"), sm("stored1")]
        marks, zeros_set, zeroed = sm("marks"), sm("zeros_set"), sm("zeroed")
        block = ctx.enter_context(nc.Block())

        def following(wi):
            return UNITS[(wi + 1) % W]

        def items(qc):
            return [(c, h, j) for c in range(qc + 1) for h in range(HG) for j in range(TPC)]

        def first_item(wi):
            return sum(items_of(following(w)[1]) + 1 for w in range(wi))

        def first_step(wi):
            return sum(steps_of(UNITS[w][1]) for w in range(wi))

        def spread(wi):
            n, m = steps_of(UNITS[wi][1]), items_of(following(wi)[1])
            until = max(n - 1, 1)
            return [m * min(s + 1, until) // until - m * min(s, until) // until for s in range(n)]

        def load_group(eng, par, g):
            for src, dst, rows in ((q_parts[0], q_stack, 0), (q_parts[1], q_stack, 1), (q_parts[0], q_stack, 2),
                                   (k_parts[0], k_stack, 0), (k_parts[0], k_stack, 1), (k_parts[1], k_stack, 2)):
                eng.dma_start(dst[par][rows * D:(rows + 1) * D, :, :].bitcast(F32),
                              src[g].rearrange("g (h d) n -> d (g h) n", d=D)).then_inc(loaded[par], 16)
            eng.dma_start(v[par][:, :, :], v_d[g].rearrange("g p k n -> (g p) k n")).then_inc(loaded[par], 16)

        def load_row(eng, par, qc, b):
            for h in range(HG):
                dst = q_stack[par][STACK:STACK + 1, h, qc * CH:(qc + 1) * CH].bitcast(F32)
                eng.dma_start(dst.rearrange("a (j c) -> a j c", c=P), minus_top[h * TPC:(h + 1) * TPC, b].bitcast(F32)).then_inc(row_loaded[b], 16)

        def store(eng, i, wi):
            par, qc = UNITS[wi]
            eng.wait_ge(y_lo_done, i * W + wi + 3)
            for dst, src in zip(out_parts, (y_hi, y_lo)):
                eng.dma_start(dst[ds(i * 2 + par), :, qc * CH:(qc + 1) * CH].rearrange("g p n -> (g p) n"),
                              src[:, wi % 2].bitcast(F32)).then_inc(stored[wi % 2], 16)

        @block.sync
        def _(sp):
            sp.dma_start(ident[:, :], consts["ident"]).then_inc(consts_loaded, 16)
            sp.dma_start(causal[:, :], consts["causal"]).then_inc(consts_loaded, 16)
            load_group(sp, 0, ds(0))
            sp.wait_ge(minus_ready, 1)
            load_row(sp, 0, 0, 0)
            with sp.Fori(0, G // 2) as i:
                for wi, (par, qc) in enumerate(UNITS):
                    b = wi % 2
                    if wi == 0:
                        sp.wait_ge(group_done, i * 2 + 1)
                        load_group(sp, 1, ds(i * 2 + 1))
                    if wi == NQ:
                        sp.wait_ge(group_done, i * 2 + 2)
                        load_group(sp, 0, ds((i * 2 + 2) % G))
                    sp.wait_ge(y_ready, i * W + wi + 1)
                    sp.dma_start(a_part[:, b], a_d[ds(i * 2 + par), :, qc * CH:(qc + 1) * CH].rearrange("g p n -> (g p) n")).then_inc(a_loaded[b], 16)
                    if wi >= 1:
                        store(sp, i, wi - 1)
                    sp.wait_ge(minus_ready, i * W + wi + 2)
                    load_row(sp, following(wi)[0], following(wi)[1], 1 - b)
                store(sp, i, W - 1)
            for b in range(2):
                sp.wait_ge(stored[b], 32 * (G * NQ // 2 + 1))
                sp.wait_ge(row_loaded[b], ROW * (G * NQ // 2 + (b == 0) + 1))

        @block.tensor
        def _(pe):
            pe.sem_inc(group_done, 1)
            pe.sem_inc(pv_done, 2)

            def see(base, n, par, qc, c, h, j):
                width = CH if c < qc else (j + 1) * P
                pe.wait_ge(seen_free, base + n + 1)
                t0 = qc * CH + j * P
                nc.tensor.matmul(seen[:, n % 2, 0:width], q_stack[par][0:STACK, h, t0:t0 + P],
                                 k_stack[par][0:STACK, h, c * CH:c * CH + width], start=True, stop=True).then_inc(seen_ready, 1)

            def turn_top(base, n, w):
                pe.wait_ge(top_ready, w + 1)
                pe.wait_ge(seen_free, base + n + 1)
                nc.tensor.transpose(seen[0:HG * TPC, n % 2, 0:P], top[:, :], ident[:, :]).then_inc(seen_ready, 1)

            def score(n, par, qc, kt, pair):
                c0 = max(kt - qc * TPC, 0) * P
                pe.wait_ge(exp_done, n + 1)
                for x in range(HALF):
                    h = pair * HALF + x
                    last = nc.tensor.matmul(scores[:, pair, x, c0:CH], k_stack[par][0:STACK + 1, h, kt * P:(kt + 1) * P],
                                            q_stack[par][0:STACK + 1, h, qc * CH + c0:(qc + 1) * CH], start=True, stop=True)
                last.then_inc(scores_ready, 1)

            def multiply(i, wi, kt, what):
                par, qc = UNITS[wi]
                c0 = max(kt - qc * TPC, 0) * P
                step = first_step(wi) + kt
                pe.wait_ge(exp_done, i * (2 * STEPS) + 2 * step + 4)
                if kt >= qc * TPC:
                    pe.wait_ge(masked, (i * W + wi) * TPC + kt - qc * TPC + 1)
                if kt == 0:
                    pe.wait_ge(acc_free, i * W + wi + 1)
                ends = kt == steps_of(qc) - 1
                for h in range(HG):
                    acc, lhs = (y_acc, v[par][:, kt, h * D:(h + 1) * D]) if what == "y" else (total, ones[:, :])
                    last = nc.tensor.matmul(acc[h * D:(h + 1) * D, c0:CH], lhs, prob[:, step % 2, h // HALF, h % HALF, c0:CH],
                                            start=(kt == 0), stop=ends)
                if what == "y":
                    return
                last.then_inc(pv_done, 1)
                if ends and qc == NQ - 1:
                    pe.wait_ge(pv_done, i * STEPS + step + 3)
                    pe.sem_inc(group_done, 1)

            pe.wait_ge(consts_loaded, 32)
            pe.wait_ge(ones_set, 3)
            pe.wait_ge(loaded[0], LOADS)
            n = 0
            for c, h, j in items(0):
                see(0, n, 0, 0, c, h, j)
                n += 1
            turn_top(0, n, 0)
            with pe.Fori(0, G // 2) as i:
                pending = None
                for wi, (par, qc) in enumerate(UNITS):
                    npar, nqc = following(wi)
                    todo = items(nqc)
                    n = HEAD + first_item(wi)
                    pe.wait_ge(row_loaded[wi % 2], i * (ROW * W // 2) + ROW * (wi // 2 + 2))
                    for s, count in enumerate(spread(wi)):
                        if s == 0 and nqc == 0:
                            pe.wait_ge(loaded[npar], i * LOADS + LOADS * (1 + (npar == 0)))
                        for quarter in range(4):
                            if quarter < 2:
                                score(i * (2 * STEPS) + 2 * (first_step(wi) + s) + quarter, par, qc, s, quarter)
                            elif pending is not None:
                                multiply(i, *pending, "y" if quarter == 2 else "total")
                            for _ in range(count * (quarter + 1) // 4 - count * quarter // 4):
                                see(i * ITEMS, n, npar, nqc, *todo.pop(0))
                                n += 1
                        pending = (wi, s)
                    turn_top(i * ITEMS, n, i * W + wi + 1)
                    assert not todo
                multiply(i, *pending, "y")
                multiply(i, *pending, "total")

        @block.scalar
        def _(act):
            nc.scalar.preload_act_table(ACT.Exp)
            act.sem_inc(exp_done, 2)
            def split(i, wi):
                act.wait_ge(y_ready, i * W + wi + 3)
                act.wait_ge(stored[wi % 2], i * (16 * W) + 32 * (wi // 2 + 1))
                nc.scalar.activation(y_hi[:, wi % 2], y[:, wi % 2], ACT.Copy).then_inc(y_hi_done, 1)

            with act.Fori(0, G // 2) as i:
                for wi, (par, qc) in enumerate(UNITS):
                    for s in range(steps_of(qc)):
                        c0 = max(s - qc * TPC, 0) * P
                        step = first_step(wi) + s
                        act.wait_ge(pv_done, i * STEPS + step + 1)
                        for pair in range(2):
                            act.wait_ge(scores_ready, i * (2 * STEPS) + 2 * step + pair + 1)
                            nc.scalar.activation(prob[:, step % 2, pair, :, c0:CH], scores[:, pair, :, c0:CH], ACT.Exp,
                                                 scale=1.0 / math.sqrt(D)).then_inc(exp_done, 1)
                        if s == 3 and wi >= 1:
                            split(i, wi - 1)
                split(i, W - 1)

        @block.vector
        def _(dve):
            dve.sem_inc(seen_free, 2)
            dve.sem_inc(y_ready, 2)
            dve.sem_inc(acc_free, 1)
            for b in range(2):
                dve.sem_inc(stored[b], 32)
                dve.sem_inc(row_loaded[b], ROW)
            nc.vector.memset(ones[:, :], 1.0).then_inc(ones_set, 1)
            for b in range(2):
                nc.vector.memset(k_stack[b][STACK:STACK + 1, :, :].bitcast(F32), 1.0).then_inc(ones_set, 1)
            dve.wait_ge(consts_loaded, 32)

            def largest(base, n, qc, c, h, j):
                dve.wait_ge(seen_ready, base + n + 1)
                dst = part[:, h * TPC + j, c:c + 1]
                if c < qc:
                    nc.vector.tensor_reduce(dst, seen[:, n % 2], AX.X, ALU.max).then_inc(seen_free, 1)
                else:
                    dve.wait_ge(seen_free, base + n + 2)
                    dve.sem_inc(marks, 1)
                    width = (j + 1) * P
                    nc.vector.tensor_tensor_reduce(out=unused[:, 0:width], in0=seen[:, n % 2, 0:width], in1=causal[:, CH - width:CH],
                                                   scale=1.0, scalar=MASKED, op0=ALU.add, op1=ALU.max, accum_out=dst).then_inc(seen_free, 1)

            def whole(base, n, w, rows, qc, b):
                dve.wait_ge(seen_free, base + n + 2)
                nc.vector.tensor_reduce(top[:, :], part[:, :, 0:qc + 1], AX.X, ALU.max).then_inc(top_ready, 1)
                dve.wait_ge(seen_ready, base + n + 1)
                dve.wait_ge(row_loaded[b], rows * ROW + ROW)
                nc.vector.tensor_scalar(minus_top[:, b], seen[0:HG * TPC, n % 2, 0:P], -1.0, None, ALU.mult).then_inc(minus_ready, 1)
                dve.wait_ge(minus_ready, w + 1)
                dve.sem_inc(seen_free, 1)

            def norm(i, wi):
                s = Steps(dve, norm_step, i * (2 * W) + 2 * wi)
                qc = UNITS[wi][1]
                dve.wait_ge(pv_done, i * STEPS + first_step(wi) + steps_of(qc) + 2)
                dve.wait_ge(y_ready, i * W + wi + 2)
                s.link(nc.vector.reciprocal(total_inv[:, :], total[:, :]))
                s.link(nc.vector.tensor_tensor(y_own[:, :], y_acc[:, :], total_inv[:, :], ALU.mult))
                dve.sem_inc(acc_free, 1)
                dve.wait_ge(a_loaded[wi % 2], i * (16 * W // 2) + 16 * (wi // 2 + 1))
                dve.wait_ge(y_lo_done, i * W + wi + 1)
                nc.vector.tensor_tensor(y[:, wi % 2], y_own[:, :], a_part[:, wi % 2], ALU.add).then_inc(y_ready, 1)

            for n, (c, h, j) in enumerate(items(0)):
                largest(0, n, 0, c, h, j)
            whole(0, HEAD - 1, 0, 0, 0, 0)
            with dve.Fori(0, G // 2) as i:
                for wi, (par, qc) in enumerate(UNITS):
                    npar, nqc = following(wi)
                    todo = items(nqc)
                    n = HEAD + first_item(wi)
                    for s, count in enumerate(spread(wi)):
                        for _ in range(count):
                            largest(i * ITEMS, n, nqc, *todo.pop(0))
                            n += 1
                        if s == 0 and wi >= 1:
                            norm(i, wi - 1)
                    whole(i * ITEMS, n, i * W + wi + 1, i * (W // 2) + (wi + 1) // 2, nqc, (wi + 1) % 2)
                norm(i, W - 1)

        @block.gpsimd
        def _(pool):
            def split(i, wi):
                pool.wait_ge(y_hi_done, i * W + wi + 1)
                nc.gpsimd.tensor_tensor(y_lo[:, wi % 2], y[:, wi % 2], y_hi[:, wi % 2], ALU.subtract).then_inc(y_lo_done, 1)

            pool.sem_inc(y_lo_done, 2)
            nc.gpsimd.memset(zeros[:, :], 0.0).then_inc(zeros_set, 1)
            pool.wait_ge(zeros_set, 1)
            for n in range(rows_d.shape[0] // P):
                pool.dma_start(rows_d[n * P:(n + 1) * P, :], zeros[:, :]).then_inc(zeroed, 16)
            with pool.Fori(0, G // 2) as i:
                for wi, (par, qc) in enumerate(UNITS):
                    if wi >= 1 and qc > 0:
                        split(i, wi - 1)
                    for r in range(TPC):
                        step = first_step(wi) + qc * TPC + r
                        pool.wait_ge(exp_done, i * (2 * STEPS) + 2 * step + 4)
                        pool.sem_inc(marks, 1)
                        tile = prob[:, step % 2, :, :, r * P:(r + 1) * P].rearrange("p a b n -> p (a b) n")
                        nc.gpsimd.affine_select(out=tile, in_=tile, compare_op=ALU.is_ge, fill=0.0, base=0,
                                                pattern=[[0, HG], [1, P]], channel_multiplier=-1).then_inc(masked, 1)
                    if wi >= 1 and qc == 0:
                        split(i, wi - 1)
                split(i, W - 1)
            pool.wait_ge(zeroed, 16 * (rows_d.shape[0] // P))

MT = 2
MROWS = MT * P
MAX_MACRO = 2 * T // MROWS + E - 1
LAG = 2


def proj_out(nc, sem, consts, mod_rows, w_proj, y_parts, x, x1_d, h2, logitsT):
    with ExitStack() as ctx:
        sb = lambda name, shape, dt=F32: ctx.enter_context(nc.sbuf_tensor(f"o_{name}", shape, dt))
        pb = lambda name, shape: ctx.enter_context(nc.psum_tensor(f"o_{name}_psum", shape, F32))
        sm = lambda name: sem(f"o_{name}")
        w_raw = sb("w_raw", [P, 2, C])
        w_hi, w_lo = sb("w_hi", [P, KC, C], F32R), sb("w_lo", [P, KC, C], F32R)
        ident = sb("ident", [P, P])
        gate_w = sb("gate_w", [P, KC, E])
        ga, shift_b, scale_b = sb("ga", [P, C]), sb("shift", [P, C]), sb("scale", [P, C])
        y_hi, y_lo = sb("y_hi", [P, 2, G, P], F32R), sb("y_lo", [P, 2, G, P], F32R)
        xt, x1, xn = sb("x", [P, 2, C]), sb("x1", [P, 2, C]), sb("xn", [P, C])
        stats, mv = sb("stats", [P, 2, 6]), sb("mv", [P, 2])
        std, rstd, newton = sb("std", [P, 1]), sb("rstd", [P, 1]), sb("newton", [P, 1])
        h = sb("h", [P, 2, C])
        h2T = sb("h2T", [P, KC, P])
        acc, turned, logits = pb("acc", [P, 2, C]), pb("turned", [P, KC, P]), pb("logits", [E, P])
        consts_loaded, w_hi_done, w_ready = sm("consts_loaded"), sm("w_hi_done"), sm("w_ready")
        w_loaded = [sm("w_loaded0"), sm("w_loaded1")]
        y_loaded, x_loaded = [sm("y_loaded0"), sm("y_loaded1")], [sm("x_loaded0"), sm("x_loaded1")]
        acc_ready, x1_ready, step, var_ready, std_ready, xn_ready, scaled, h_ready = (
            sm("acc_ready"), sm("x1_ready"), sm("step"), sm("var_ready"), sm("std_ready"), sm("xn_ready"), sm("scaled"), sm("h_ready"))
        turned_ready, h2T_ready, logits_ready, logits_kept = sm("turned_ready"), sm("h2T_ready"), sm("logits_ready"), sm("logits_kept")
        stored, kept, marks = [sm("stored0"), sm("stored1")], [sm("kept0"), sm("kept1")], sm("marks")
        block = ctx.enter_context(nc.Block())

        @block.sync
        def _(sp):
            sp.dma_start(ident[:, :], consts["ident"]).then_inc(consts_loaded, 16)
            sp.dma_start(gate_w[:, :, :], consts["gate_w"].rearrange("(k p) e -> p k e", p=P)).then_inc(consts_loaded, 16)
            for j, dst in ((2, ga), (3, shift_b), (4, scale_b)):
                sp.dma_start(dst[:, :], mod_rows[j * C:(j + 1) * C].rearrange("(a n) -> a n", a=1).broadcast_to([P, C])).then_inc(consts_loaded, 16)
            for k in range(KC):
                if k >= 2:
                    sp.wait_ge(w_ready, k - 1)
                sp.dma_start(w_raw[:, k % 2], w_proj[k * P:(k + 1) * P, :]).then_inc(w_loaded[k % 2], 16)
            with sp.Fori(0, NT // 2) as i:
                for b in range(2):
                    n = i * 2 + b
                    sp.wait_ge(acc_ready, n + 1)
                    for src, dst in zip(y_parts, (y_hi, y_lo)):
                        sp.dma_start(dst[:, b].bitcast(F32), src[:, :, ds(n * P, P)].rearrange("g p n -> p g n")).then_inc(y_loaded[b], 16)
                    sp.wait_ge(x1_ready, n + 1)
                    sp.dma_start(xt[:, b], x[ds(n * P, P), :]).then_inc(x_loaded[b], 16)

        @block.tensor
        def _(pe):
            pe.sem_inc(acc_ready, 2)
            pe.wait_ge(consts_loaded, 16 * 5)
            pe.wait_ge(w_ready, KC)

            def turn(n, b):
                pe.wait_ge(h_ready, n + 1)
                pe.wait_ge(h2T_ready, n + 1)
                for k in range(KC):
                    last = nc.tensor.transpose(turned[:, k], h[:, b, k * P:(k + 1) * P], ident[:, :])
                last.then_inc(turned_ready, 1)

            def gate(n):
                pe.wait_ge(h2T_ready, n + 2)
                pe.wait_ge(logits_kept, n + 1)
                for k in range(KC):
                    last = nc.tensor.matmul(logits[:, :], gate_w[:, k], h2T[:, k], start=(k == 0), stop=(k == KC - 1))
                last.then_inc(logits_ready, 1)

            def project(i, b):
                pe.wait_ge(y_loaded[b], i * 32 + 32)
                pe.wait_ge(x1_ready, i * 2 + b + 1)
                for o in range(2):
                    col = slice(o * CH, (o + 1) * CH)
                    last = product(nc, acc[:, b, col], lambda part, k: (y_hi, y_lo)[part][:, b, k],
                                   lambda part, k: (w_hi, w_lo)[part][:, k, col])
                last.then_inc(acc_ready, 1)

            with pe.Fori(0, NT // 2) as i:
                for b in range(2):
                    turn(i * 2 + b, b)
                    project(i, b)
                    gate(i * 2 + b)
            for n in range(NT, NT + LAG):
                turn(n, n % 2)
                gate(n)

        @block.scalar
        def _(act):
            nc.scalar.preload_act_table(ACT.Sqrt)
            act.sem_inc(h2T_ready, 1)
            act.sem_inc(logits_kept, 1)
            for k in range(KC):
                act.wait_ge(w_loaded[k % 2], 16 * (k // 2 + 1))
                nc.scalar.activation(w_hi[:, k], w_raw[:, k % 2], ACT.Copy).then_inc(w_hi_done, 1)

            def keep(n, col):
                act.wait_ge(turned_ready, n + 1)
                act.wait_ge(logits_ready, n + 1)
                nc.scalar.activation(h2T[:, :, :], turned[:, :, :], ACT.Copy).then_inc(h2T_ready, 1)
                act.wait_ge(logits_ready, n + 2)
                nc.scalar.activation(logitsT[:, col], logits[:, :], ACT.Copy).then_inc(logits_kept, 1)

            act.sem_inc(logits_ready, 1)
            with act.Fori(0, NT // 2) as i:
                for b in range(2):
                    keep(i * 2 + b, ds((i * 2 + b) * P, P))
                    act.wait_ge(var_ready, i * 2 + b + 1)
                    nc.scalar.activation(std[:, :], mv[:, 1:2], ACT.Sqrt).then_inc(std_ready, 1)
                    n = i * 2 + b
                    act.wait_ge(h_ready, n + LAG + 1)
                    act.dma_start(h2[:, ds(n)].rearrange("p a n -> p (a n)"), h[:, b]).then_inc(kept[b], 16)
                    act.dma_start(x1_d[ds(n * P, P), :], x1[:, b]).then_inc(stored[b], 16)
            for n in range(NT, NT + LAG):
                keep(n, slice(n * P, (n + 1) * P))
            for b in range(2):
                act.wait_ge(kept[b], 16 * (NT // 2 + 1))
                act.wait_ge(stored[b], 16 * (NT // 2 + 1))

        @block.vector
        def _(dve):
            dve.sem_inc(x1_ready, 2)
            for b in range(2):
                dve.sem_inc(stored[b], 16)
            for k in range(KC):
                dve.wait_ge(w_hi_done, k + 1)
                nc.vector.tensor_tensor(w_lo[:, k], w_raw[:, k % 2], w_hi[:, k], ALU.subtract).then_inc(w_ready, 1)
            dve.wait_ge(consts_loaded, 16 * 5)
            with dve.Fori(0, NT // 2) as i:
                s = Steps(dve, step, i * (2 * 9))
                for b in range(2):
                    n = i * 2 + b
                    dve.wait_ge(acc_ready, n + 3)
                    dve.wait_ge(stored[b], i * 16 + 16)
                    dve.wait_ge(xn_ready, n + 1)
                    s.link(nc.vector.tensor_tensor(x1[:, b], acc[:, b], ga[:, :], ALU.mult))
                    dve.wait_ge(x_loaded[b], i * 16 + 16)
                    s.link(nc.vector.tensor_tensor(x1[:, b], x1[:, b], xt[:, b], ALU.add))
                    dve.sem_inc(x1_ready, 1)
                    nc.vector.bn_stats(stats[:, 0], x1[:, b, 0:CH])
                    s.link(nc.vector.bn_stats(stats[:, 1], x1[:, b, CH:C]))
                    dve.sem_inc(marks, 1)
                    s.link(nc.vector.bn_aggr(mv[:, :], stats[:, :, :].rearrange("p a b -> p (a b)")))
                    nc.vector.tensor_scalar(mv[:, 1:2], mv[:, 1:2], EPS, None, ALU.add).then_inc(var_ready, 1)
                    dve.wait_ge(std_ready, n + 1)
                    s.link(nc.vector.reciprocal(rstd[:, :], std[:, :]))
                    s.link(nc.vector.tensor_tensor(newton[:, :], rstd[:, :], rstd[:, :], ALU.mult))
                    s.link(nc.vector.tensor_tensor(newton[:, :], newton[:, :], mv[:, 1:2], ALU.mult))
                    s.link(nc.vector.tensor_scalar(newton[:, :], newton[:, :], -0.5, 1.5, ALU.mult, ALU.add))
                    s.link(nc.vector.tensor_tensor(rstd[:, :], rstd[:, :], newton[:, :], ALU.mult))
                    dve.wait_ge(scaled, n + 1)
                    nc.vector.tensor_scalar(xn[:, :], x1[:, b], mv[:, 0:1], rstd[:, 0:1], ALU.subtract, ALU.mult).then_inc(xn_ready, 1)

        @block.gpsimd
        def _(pool):
            pool.sem_inc(scaled, 1)
            pool.sem_inc(xn_ready, 1)
            nc.gpsimd.memset(h[:, :, :], 0.0).then_inc(h_ready, LAG)
            for b in range(2):
                pool.sem_inc(kept[b], 16)
            pool.wait_ge(consts_loaded, 16 * 5)
            with pool.Fori(0, NT // 2) as i:
                for b in range(2):
                    n = i * 2 + b
                    pool.wait_ge(turned_ready, n + 1)
                    pool.wait_ge(kept[b], i * 16 + 16)
                    pool.wait_ge(xn_ready, n + 2)
                    nc.gpsimd.tensor_tensor(h[:, b], xn[:, :], scale_b[:, :], ALU.mult).then_inc(scaled, 1)
                    pool.wait_ge(scaled, n + 2)
                    nc.gpsimd.tensor_tensor(h[:, b], h[:, b], shift_b[:, :], ALU.add).then_inc(h_ready, 1)


def route(nc, sem, consts, h2, logitsT, slots, weights, bounds, rows_d):
    NTH = T // MROWS - 1
    with ExitStack() as ctx:
        sb = lambda name, shape, dt=F32: ctx.enter_context(nc.sbuf_tensor(f"r_{name}", shape, dt))
        pb = lambda name, shape: ctx.enter_context(nc.psum_tensor(f"r_{name}_psum", shape, F32))
        sm = lambda name: sem(f"r_{name}")
        ident, before, ones = sb("ident", [P, P]), sb("before", [P, P]), sb("ones", [P, P])
        numbers, limits = sb("numbers", [P, E]), sb("limits", [P, NTH])
        logits, best, index = sb("logits", [P, NT, E]), sb("best", [P, NT, 8]), sb("index", [P, NT, 8], U32)
        indexf = sb("indexf", [P, NT, 8])
        first, second, both = sb("first", [P, NT, E]), sb("second", [P, NT, E]), sb("both", [P, NT, E])
        gap, denom = sb("gap", [P, NT]), sb("denom", [P, NT])
        ahead, over = sb("ahead", [P, NT + 1, E]), sb("over", [P, E, NTH])
        macros, start = sb("macros", [P, E]), sb("start", [P, E + 1])
        row, picked, slotf = sb("row", [P, NT, E]), sb("picked", [P, NT, E]), sb("slotf", [P, 2, NT])
        p_logits, p_rank, p_count = pb("logits", [P, CH]), pb("rank", [P, CH]), pb("count", [P, CH])
        consts_loaded, turned_ready, both_ready, ranks_ready = sm("consts_loaded"), sm("turned_ready"), sm("both_ready"), sm("ranks_ready")
        step, gap_ready, exp_done, slots_ready, scattered = sm("step"), sm("gap_ready"), sm("exp_done"), sm("slots_ready"), sm("scattered")
        block = ctx.enter_context(nc.Block())

        @block.sync
        def _(sp):
            for dst, name in ((ident[:, :], "ident"), (before[:, :], "before"), (numbers[:, :], "numbers"), (limits[:, :], "limits")):
                sp.dma_start(dst, consts[name]).then_inc(consts_loaded, 16)

        @block.tensor
        def _(pe):
            pe.wait_ge(consts_loaded, 64)
            for i in range(NT):
                last = nc.tensor.transpose(p_logits[:, i * E:(i + 1) * E], logitsT[:, (i + LAG) * P:(i + LAG + 1) * P], ident[0:E, 0:E])
            last.then_inc(turned_ready, 1)
            pe.wait_ge(both_ready, 1)
            m = both[:, :, :].rearrange("p i e -> p (i e)")
            nc.tensor.matmul(p_rank[:, 0:P], before[:, :], m, start=True, stop=True)
            nc.tensor.matmul(p_count[:, 0:P], ones[:, :], m, start=True, stop=True).then_inc(ranks_ready, 1)

        @block.scalar
        def _(act):
            nc.scalar.preload_act_table(ACT.Exp)
            act.wait_ge(gap_ready, 1)
            nc.scalar.activation(gap[:, :], gap[:, :], ACT.Exp).then_inc(exp_done, 1)

        @block.vector
        def _(dve):
            s = Steps(dve, step)
            wide = lambda ap, shape: ap.broadcast_to(shape)
            s.link(nc.vector.memset(ones[:, :], 1.0))
            s.link(nc.vector.memset(ahead[:, 0], 0.0))
            s.link(nc.vector.memset(start[:, 0:1], 0.0))
            dve.wait_ge(consts_loaded, 64)
            dve.wait_ge(turned_ready, 1)
            s.link(nc.vector.tensor_copy(logits[:, :, :].rearrange("p i e -> p (i e)"), p_logits[:, 0:NT * E]))
            for i in range(NT):
                last = nc.vector.max(best[:, i], logits[:, i])
            s.link(last)
            for i in range(NT):
                last = nc.vector.max_index(index[:, i], best[:, i], logits[:, i])
            s.link(last)
            s.link(nc.vector.tensor_copy(indexf[:, :, :], index[:, :, :]))
            numbers_w = wide(numbers[:, :].rearrange("p (a e) -> p a e", a=1), [P, NT, E])
            for c, mask in ((0, first), (1, second)):
                s.link(nc.vector.tensor_tensor(mask[:, :, :], wide(indexf[:, :, c:c + 1], [P, NT, E]), numbers_w, ALU.is_equal))
            nc.vector.tensor_tensor(both[:, :, :], first[:, :, :], second[:, :, :], ALU.add).then_inc(both_ready, 1)
            nc.vector.tensor_tensor(gap[:, :], best[:, :, 1], best[:, :, 0], ALU.subtract).then_inc(gap_ready, 1)
            dve.wait_ge(exp_done, 1)
            s.link(nc.vector.tensor_scalar(denom[:, :], gap[:, :], 1.0, None, ALU.add))
            s.link(nc.vector.reciprocal(weights[:, 0], denom[:, :]))
            s.link(nc.vector.tensor_tensor(weights[:, 1], gap[:, :], weights[:, 0], ALU.mult))
            dve.wait_ge(ranks_ready, 1)
            for i in range(NT):
                s.link(nc.vector.tensor_tensor(ahead[:, i + 1], p_count[:, i * E:(i + 1) * E], ahead[:, i], ALU.add))
            s.link(nc.vector.tensor_tensor(over[:, :, :], wide(ahead[:, NT].rearrange("p (e a) -> p e a", a=1), [P, E, NTH]),
                                           wide(limits[:, :].rearrange("p (a l) -> p a l", a=1), [P, E, NTH]), ALU.is_gt))
            s.link(nc.vector.tensor_reduce(macros[:, :], over[:, :, :], AX.X, ALU.add))
            s.link(nc.vector.tensor_scalar(macros[:, :], macros[:, :], 1.0, None, ALU.add))
            for e in range(E):
                s.link(nc.vector.tensor_tensor(start[:, e + 1:e + 2], start[:, e:e + 1], macros[:, e:e + 1], ALU.add))
            s.link(nc.vector.tensor_copy(bounds[:, :], start[0:1, :]))
            s.link(nc.vector.tensor_tensor(row[:, :, :].rearrange("p i e -> p (i e)"), p_rank[:, 0:P],
                                           ahead[:, 0:NT].rearrange("p i e -> p (i e)"), ALU.add))
            s.link(nc.vector.tensor_scalar(macros[:, :], start[:, 0:E], float(MROWS), None, ALU.mult))
            s.link(nc.vector.tensor_tensor(row[:, :, :], row[:, :, :], wide(macros[:, :].rearrange("p (a e) -> p a e", a=1), [P, NT, E]), ALU.add))
            for c, mask in ((0, first), (1, second)):
                s.link(nc.vector.tensor_tensor(picked[:, :, :], mask[:, :, :], row[:, :, :], ALU.mult))
                s.link(nc.vector.tensor_reduce(slotf[:, c], picked[:, :, :], AX.X, ALU.add))
            nc.vector.tensor_copy(slots[:, :, :], slotf[:, :, :]).then_inc(slots_ready, 1)

        @block.gpsimd
        def _(pool):
            pool.wait_ge(slots_ready, 1)
            for i in range(NT):
                for c in range(2):
                    nc.gpsimd.indirect_dma_start(rows_d, bass.IndirectOffsetOnAxis(ap=slots[:, c, i:i + 1], axis=0),
                                                 h2[:, i], None).then_inc(scattered, 16)
            pool.wait_ge(scattered, 16 * 2 * NT)


def experts(nc, sem, consts, mod_rows, expert_w, bounds, rows_d):
    RAWS = 4
    with ExitStack() as ctx:
        sb = lambda name, shape, dt=F32: ctx.enter_context(nc.sbuf_tensor(f"e_{name}", shape, dt))
        pb = lambda name, shape: ctx.enter_context(nc.psum_tensor(f"e_{name}_psum", shape, F32))
        sm = lambda name: sem(f"e_{name}")
        ident, gb = sb("ident", [P, P]), sb("gb", [P, C])
        w_raw = sb("w_raw", [P, RAWS, C])
        w_hi = [sb(f"w_hi{b}", [P, KC, C], F32R) for b in range(2)]
        w_lo = [sb(f"w_lo{b}", [P, KC, C], F32R) for b in range(2)]
        xt = sb("x", [P, MT, C])
        x_hi, x_lo = sb("x_hi", [P, MT, KC, P], F32R), sb("x_lo", [P, MT, KC, P], F32R)
        y = sb("y", [P, MT, C])
        turned, acc = pb("turned", [P, C]), pb("acc", [P, MT, C])
        consts_loaded = sm("consts_loaded")
        w_loaded, w_hi_done, w_ready, w_free = [sm(f"w_loaded{r}") for r in range(RAWS)], sm("w_hi_done"), sm("w_ready"), sm("w_free")
        x_loaded, turned_ready, x_hi_done, x_ready = [sm(f"x_loaded{s}") for s in range(MT)], sm("turned_ready"), sm("x_hi_done"), sm("x_ready")
        acc_ready, y_ready, stored, marks = sm("acc_ready"), sm("y_ready"), [sm(f"stored{s}") for s in range(MT)], sm("marks")
        block = ctx.enter_context(nc.Block())

        def bound(eng, e):
            return eng.value_load(bounds[0:1, e:e + 1], min_val=0, max_val=MAX_MACRO) if isinstance(e, int) else eng.value_load(bounds[0:1, ds(e)], min_val=0, max_val=MAX_MACRO)

        @block.sync
        def _(sp):
            sp.dma_start(ident[:, :], consts["ident"]).then_inc(consts_loaded, 16)
            sp.dma_start(gb[:, :], mod_rows[5 * C:6 * C].rearrange("(a n) -> a n", a=1).broadcast_to([P, C])).then_inc(consts_loaded, 16)
            sp.dma_start(xt[:, 0], rows_d[0:P, :]).then_inc(x_loaded[0], 16)
            total = bound(sp, E)
            with sp.Fori(0, total) as g:
                for s in range(MT):
                    sp.wait_ge(turned_ready, g * MT + s + 1)
                    sp.dma_start(xt[:, (s + 1) % MT], rows_d[ds((g * MT + (s + 1)) * P, P), :]).then_inc(x_loaded[(s + 1) % MT], 16)
                    sp.wait_ge(y_ready, g * MT + s + 3)
                    sp.dma_start(rows_d[ds((g * MT + s) * P, P), :], y[:, s]).then_inc(stored[s], 16)
            for s in range(MT):
                sp.wait_ge(stored[s], total * 16 + 16)
                sp.wait_ge(x_loaded[s], total * 16 + (16 if s == 0 else 0))
            sp.sem_inc(marks, 1)

        @block.gpsimd
        def _(pool):
            def load(src, c):
                pool.dma_start(w_raw[:, c % RAWS], src).then_inc(w_loaded[c % RAWS], 16)

            for c in range(RAWS):
                load(expert_w[0, c * P:(c + 1) * P, :], c)
            with pool.Fori(0, E // 2) as j:
                for b in range(2):
                    pool.wait_ge(w_free, j * 2 + b + 1)
                    for c in range(KC):
                        n = (j * 2 + b) * KC + c
                        pool.wait_ge(w_loaded[c % RAWS], (j * 2 + b) * (16 * KC // RAWS) + 16 * (c // RAWS + 1))
                        pool.sem_inc(marks, 1)
                        nc.gpsimd.tensor_copy(w_hi[b][:, c], w_raw[:, c % RAWS]).then_inc(w_hi_done, 1)
                        pool.wait_ge(w_hi_done, n + 1)
                        nc.gpsimd.tensor_tensor(w_lo[b][:, c], w_raw[:, c % RAWS], w_hi[b][:, c], ALU.subtract).then_inc(w_ready, 1)
                        pool.wait_ge(w_ready, n + 1)
                        nxt = c + RAWS
                        e = (j * 2 + (b + nxt // KC)) % E if nxt >= KC else j * 2 + b
                        load(expert_w[ds(e), nxt % KC * P:(nxt % KC + 1) * P, :].rearrange("a p n -> (a p) n"), c)
            for c in range(RAWS):
                pool.wait_ge(w_loaded[c], 16 * (E * KC // RAWS + 1))

        @block.tensor
        def _(pe):
            pe.sem_inc(w_free, 2)
            pe.sem_inc(turned_ready, 1)
            pe.sem_inc(acc_ready, 1)
            pe.wait_ge(consts_loaded, 32)

            def turn(n, s, loads):
                pe.wait_ge(x_loaded[s], loads)
                pe.wait_ge(x_ready, n + 1)
                for k in range(KC):
                    last = nc.tensor.transpose(turned[:, k * P:(k + 1) * P], xt[:, s, k * P:(k + 1) * P], ident[:, :])
                last.then_inc(turned_ready, 1)

            turn(0, 0, 16)
            with pe.Fori(0, E // 2) as j:
                for b in range(2):
                    lo, hi = bound(pe, j * 2 + b), bound(pe, j * 2 + (b + 1))
                    pe.wait_ge(w_ready, (j * 2 + b) * KC + KC)
                    pe.sem_inc(marks, 1)
                    with pe.Fori(lo, hi) as g:
                        for s in range(MT):
                            turn(g * MT + (s + 1), (s + 1) % MT, g * 16 + 16 * (1 + s))
                            pe.wait_ge(x_ready, g * MT + s + 2)
                            pe.wait_ge(y_ready, g * MT + s + 1)
                            for o in range(2):
                                col = slice(o * CH, (o + 1) * CH)
                                last = product(nc, acc[:, s, col], lambda part, k: (x_hi, x_lo)[part][:, s, k],
                                               lambda part, k: (w_hi, w_lo)[part][b][:, k, col])
                            last.then_inc(acc_ready, 1)
                    pe.wait_ge(acc_ready, hi * MT + 1)
                    pe.sem_inc(w_free, 1)

        @block.scalar
        def _(act):
            nc.scalar.preload_act_table(ACT.Exp)
            total = bound(act, E)
            act.wait_ge(turned_ready, 2)
            nc.scalar.activation(x_hi[:, 0].rearrange("p k n -> p (k n)"), turned[:, :], ACT.Copy).then_inc(x_hi_done, 1)
            with act.Fori(0, total) as g:
                for s in range(MT):
                    act.wait_ge(turned_ready, g * MT + s + 3)
                    act.wait_ge(acc_ready, g * MT + s + 1)
                    nc.scalar.activation(x_hi[:, (s + 1) % MT].rearrange("p k n -> p (k n)"), turned[:, :], ACT.Copy).then_inc(x_hi_done, 1)

        @block.vector
        def _(dve):
            dve.sem_inc(x_ready, 1)
            dve.sem_inc(y_ready, 2)
            for s in range(MT):
                dve.sem_inc(stored[s], 16)
            dve.wait_ge(consts_loaded, 32)
            total = bound(dve, E)

            def split(n, s):
                dve.wait_ge(x_hi_done, n + 1)
                nc.vector.tensor_tensor(x_lo[:, s].rearrange("p k n -> p (k n)"), turned[:, :],
                                        x_hi[:, s].rearrange("p k n -> p (k n)"), ALU.subtract).then_inc(x_ready, 1)

            split(0, 0)
            with dve.Fori(0, total) as g:
                for s in range(MT):
                    split(g * MT + (s + 1), (s + 1) % MT)
                    dve.wait_ge(acc_ready, g * MT + s + 2)
                    dve.wait_ge(stored[s], g * 16 + 16)
                    nc.vector.tensor_tensor(y[:, s], acc[:, s], gb[:, :], ALU.mult).then_inc(y_ready, 1)


def combine(nc, sem, slots, weights, out_rows_d, x1_d, out):
    with ExitStack() as ctx:
        sb = lambda name, shape, dt=F32: ctx.enter_context(nc.sbuf_tensor(f"c_{name}", shape, dt))
        sm = lambda name: sem(f"c_{name}")
        B = 4
        rows, x1, res = sb("rows", [P, B, 2, C]), sb("x1", [P, B, C]), sb("res", [P, B, C])
        gathered, x1_loaded = [sm(f"gathered{b}") for b in range(B)], [sm(f"x1_loaded{b}") for b in range(B)]
        half, done, stored = sm("half"), sm("done"), [sm(f"stored{b}") for b in range(B)]
        block = ctx.enter_context(nc.Block())

        @block.gpsimd
        def _(pool):
            for i in range(NT):
                b = i % B
                if i >= B:
                    pool.wait_ge(done, i - B + 1)
                for c in range(2):
                    nc.gpsimd.indirect_dma_start(rows[:, b, c], None, out_rows_d,
                                                 bass.IndirectOffsetOnAxis(ap=slots[:, c, i:i + 1], axis=0)).then_inc(gathered[b], 16)

        @block.sync
        def _(sp):
            for i in range(NT + 2):
                if i < NT:
                    if i >= B:
                        sp.wait_ge(done, i - B + 1)
                    sp.dma_start(x1[:, i % B], x1_d[i * P:(i + 1) * P, :]).then_inc(x1_loaded[i % B], 16)
                if i >= 2:
                    n = i - 2
                    sp.wait_ge(done, n + 1)
                    sp.dma_start(out[n * P:(n + 1) * P, :], res[:, n % B]).then_inc(stored[n % B], 16)
            for b in range(B):
                sp.wait_ge(stored[b], 16 * (NT // B))

        @block.vector
        def _(dve):
            for i in range(NT):
                b = i % B
                dve.wait_ge(gathered[b], 32 * (i // B + 1))
                dve.wait_ge(x1_loaded[b], 16 * (i // B + 1))
                if i >= B:
                    dve.wait_ge(stored[b], 16 * (i // B))
                nc.vector.scalar_tensor_tensor(out=res[:, b], in0=rows[:, b, 0], scalar=weights[:, 0, i:i + 1], in1=x1[:, b],
                                               op0=ALU.mult, op1=ALU.add).then_inc(half, 1)
                dve.wait_ge(half, i + 1)
                nc.vector.scalar_tensor_tensor(out=res[:, b], in0=rows[:, b, 1], scalar=weights[:, 1, i:i + 1], in1=res[:, b],
                                               op0=ALU.mult, op1=ALU.add).then_inc(done, 1)


@contextmanager
def semaphores(nc):
    taken = []

    def sem(name):
        taken.append(nc.alloc_semaphore(name=name))
        return taken[-1]

    yield sem
    nc.clear_and_free_semaphores(taken)
    nc.all_engine_barrier()


def adaln_block(nc, x, w_attn, w_proj, adapter, gating, gate_w, expert_w, c, wmod, consts, out):
    def scratch(name, shape):
        return nc.dram_tensor(f"scratch_{name}", shape, F32).ap()

    mod_rows = scratch("mod_rows", [6 * C])
    q_hi, q_lo, k_hi, k_lo = (scratch(n, [G, P, T]) for n in ("q_hi", "q_lo", "k_hi", "k_lo"))
    v, a_y = scratch("v", [G, P, NT, P]), scratch("a_y", [G, P, T])
    y_hi, y_lo = scratch("y_hi", [G, P, T]), scratch("y_lo", [G, P, T])
    x1 = scratch("x1", [T, C])
    rows = scratch("rows", [(MAX_MACRO + 1) * MROWS, C])
    consts = dict(consts, adapter=adapter, gating=gating, gate_w=gate_w)
    with ExitStack() as ctx:
        with semaphores(nc) as sem:
            modulation(nc, sem, c, wmod, mod_rows)
        with semaphores(nc) as sem, ExitStack() as stage:
            ak = stage.enter_context(nc.sbuf_tensor("ak", [P, G, P], F32))
            av = stage.enter_context(nc.sbuf_tensor("av", [P, G, P], F32))
            with ExitStack() as inner:
                hT = [inner.enter_context(nc.sbuf_tensor(n, [P, KC, T], F32R)) for n in ("hT_hi", "hT_lo")]
                norm_in(nc, sem, x, mod_rows, consts["ident"], *hT)
                project(nc, sem, "k", w_attn, G, hT, consts, ak, (k_hi, k_lo))
                project(nc, sem, "v", w_attn, 2 * G, hT, consts, av, (v,))
                project(nc, sem, "q", w_attn, 0, hT, consts, None, (q_hi, q_lo))
            adapter_attention(nc, sem, consts, ak, av, q_hi, q_lo, a_y)
        with semaphores(nc) as sem:
            attention(nc, sem, consts, (q_hi, q_lo), (k_hi, k_lo), v, a_y, (y_hi, y_lo), rows)
        slots = ctx.enter_context(nc.sbuf_tensor("slots", [P, 2, NT], I32))
        weights = ctx.enter_context(nc.sbuf_tensor("weights", [P, 2, NT], F32))
        bounds = ctx.enter_context(nc.sbuf_tensor("bounds", [1, E + 1], I32))
        with semaphores(nc) as sem, ExitStack() as stage:
            h2 = stage.enter_context(nc.sbuf_tensor("h2", [P, NT, C], F32))
            logitsT = stage.enter_context(nc.sbuf_tensor("logitsT", [E, (NT + LAG) * P], F32))
            proj_out(nc, sem, consts, mod_rows, w_proj, (y_hi, y_lo), x, x1, h2, logitsT)
            route(nc, sem, consts, h2, logitsT, slots, weights, bounds, rows)
        with semaphores(nc) as sem:
            experts(nc, sem, consts, mod_rows, expert_w, bounds, rows)
            combine(nc, sem, slots, weights, rows, x1, out)


def _constants():
    import numpy as np

    theta = np.float32(1.0) / np.float32(10000.0) ** (np.arange(0, D, 2, dtype=np.float32) / np.float32(D))
    angle = np.outer(np.arange(T, dtype=np.float32), theta.astype(np.float32)).astype(np.float32)
    d = np.arange(P) % D
    sign = np.where(d < D // 2, np.float32(-1), np.float32(1))[:, None]
    p = np.arange(P)
    causal = np.zeros((P, CH), np.float32)
    causal[:, CH - P:] = np.where(p[None, :] > p[:, None], np.float32(MASKED), np.float32(0))
    return {
        "ident": np.eye(P, dtype=np.float32),
        "block_mask": np.kron(np.eye(HG, dtype=np.float32), np.ones((D, D), np.float32)),
        "cos": np.ascontiguousarray(np.cos(angle).astype(np.float32).T[d % (D // 2)]),
        "sin": np.ascontiguousarray(np.sin(angle).astype(np.float32).T[d % (D // 2)] * sign),
        "causal": causal,
        "before": np.ascontiguousarray((p[:, None] < p[None, :]).astype(np.float32)),
        "numbers": np.tile(np.arange(E, dtype=np.float32), (P, 1)),
        "limits": np.tile(np.arange(1, T // MROWS, dtype=np.float32) * MROWS, (P, 1)),
    }


def kernel(**inputs):
    import numpy as np
    import concourse.bacc as bacc
    from concourse.bass_utils import run_bass_kernel_spmd

    a = {k: np.asarray(v) for k, v in inputs.items()}
    lay = {
        "x": a["L0_attn_x"].reshape(T, C),
        "w_attn": a["L0_attn_w_attn"].reshape(3 * G, P, KC, P).transpose(0, 3, 2, 1).reshape(3 * G, P, C),
        "w_proj": a["L0_attn_w_proj"].T,
        "adapter": a["L0_attn_adapter_wte"].T.reshape(KC, P, A).transpose(1, 0, 2),
        "gating": a["L0_attn_gating"],
        "gate_w": a["L0_ffn_gate_w"],
        "expert_w": a["L0_ffn_expert_w"],
        "c": a["L0_c"].reshape(KC, P).T,
        "wmod": a["L0_wmod"],
    }
    nc = bacc.Bacc("TRN2", target_bir_lowering=False, num_devices=1)
    arrays, aps = {}, {}
    for name, value in {**lay, **_constants()}.items():
        arrays[f"in_{name}"] = np.ascontiguousarray(value)
        aps[name] = nc.dram_tensor(f"in_{name}", list(value.shape), F32, kind="ExternalInput").ap()
    out = nc.dram_tensor("out", [T, C], F32, kind="ExternalOutput").ap()
    adaln_block(nc, *(aps[name] for name in lay), {name: aps[name] for name in _constants()}, out)
    r = run_bass_kernel_spmd(nc, [arrays], core_ids=[0])
    return r.results[0]["out"].reshape(1, T, C)
```

```python
import math
from contextlib import ExitStack, contextmanager

import concourse.bass as bass
from concourse import mybir

ALU = mybir.AluOpType
ACT = mybir.ActivationFunctionType
AX = mybir.AxisListType
F32 = mybir.dt.float32
F32R = mybir.dt.float32r
I32 = mybir.dt.int32
U32 = mybir.dt.uint32

P = 128
T, C = 2048, 1024
H, D = 32, 32
E = 8
A = 10
CH = 512
KC = C // P
NT = T // P
NQ = T // CH
TPC = CH // P
HG = P // D
G = H // HG
EPS = 1e-5
LOOKS = 2


def ds(i, n=1):
    return bass.ds(i, n)


class Steps:

    def __init__(self, eng, sem, base=0):
        self.eng, self.sem, self.base, self.n = eng, sem, base, 0

    def link(self, ins):
        self.n += 1
        ins.then_inc(self.sem, 1)
        self.eng.wait_ge(self.sem, self.base + self.n)


def modulation(nc, sem, c, wmod, mod_rows):
    with ExitStack() as ctx:
        sb = lambda name, shape, dt: ctx.enter_context(nc.sbuf_tensor(name, shape, dt))
        UN = 6
        c_col = sb("c_col", [P, KC], F32)
        c_sig = sb("c_sig", [P, KC], F32)
        silu = sb("silu", [P, KC], F32)
        wbuf = sb("wmod_buf", [P, 3, KC, CH], F32)
        row = sb("mod_row", [1, 2, 3 * C], F32)
        gate = sb("gate", [1, CH], F32)
        gate_sign = sb("gate_sign", [1, CH], F32)
        gate_size = sb("gate_size", [1, CH], F32)
        acc = ctx.enter_context(nc.psum_tensor("mod_acc", [1, 2, CH], F32))
        c_loaded, silu_step, silu_ready = sem("c_loaded"), sem("silu_step"), sem("silu_ready")
        sig_ready = sem("sig_ready")
        w_loaded = [sem(f"wmod_loaded{b}") for b in range(3)]
        mod_acc_ready, mod_acc_free = sem("mod_acc_ready"), sem("mod_acc_free")
        mod_step, row_done, mod_stored = sem("mod_step"), sem("mod_row_done"), sem("mod_stored")
        w_view = wmod.rearrange("(k p) (n j) -> n p k j", p=P, j=CH)
        block = ctx.enter_context(nc.Block())

        @block.sync
        def _(sp):
            sp.dma_start(c_col[:, :], c).then_inc(c_loaded, 16)
            with sp.Fori(0, 2) as i:
                for u in range(UN):
                    sp.wait_ge(mod_acc_free, i * UN + u + 1)
                    sp.dma_start(wbuf[:, u % 3], w_view[ds(i * UN + u)].rearrange("a p k j -> (a p) k j")).then_inc(w_loaded[u % 3], 16)
            sp.wait_ge(row_done, 2 * UN)
            sp.dma_start(mod_rows.rearrange("(a n) -> a n", a=1), row[:, :, :].rearrange("a b n -> a (b n)")).then_inc(mod_stored, 16)
            sp.wait_ge(mod_stored, 16)

        @block.scalar
        def _(act):
            nc.scalar.preload_act_table(ACT.Exp)
            act.wait_ge(c_loaded, 16)
            nc.scalar.activation(c_sig[:, :], c_col[:, :], ACT.Exp, scale=-1.0).then_inc(sig_ready, 1)

        @block.vector
        def _(dve):
            dve.sem_inc(mod_acc_free, 3)
            dve.wait_ge(sig_ready, 1)
            s = Steps(dve, silu_step)
            s.link(nc.vector.tensor_scalar(silu[:, :], c_sig[:, :], 1.0, None, ALU.add))
            s.link(nc.vector.reciprocal(c_sig[:, :], silu[:, :]))
            nc.vector.tensor_tensor(silu[:, :], c_col[:, :], c_sig[:, :], ALU.mult).then_inc(silu_ready, 1)
            with dve.Fori(0, 2) as i:
                s = Steps(dve, mod_step, i * 8)
                for u in range(UN):
                    dst = row[:, ds(i), u * CH:(u + 1) * CH].rearrange("a b n -> a (b n)")
                    src = acc[:, u % 2]
                    dve.wait_ge(mod_acc_ready, i * UN + u + 1)
                    if u // 2 == 0:
                        last = nc.vector.tensor_copy(dst, src)
                    elif u // 2 == 1:
                        last = nc.vector.tensor_scalar(dst, src, 1.0, None, ALU.add)
                    else:
                        s.link(nc.vector.tensor_copy(gate[:, :], src))
                        s.link(nc.vector.tensor_scalar(gate_sign[:, :], gate[:, :], 0.0, 2.0, ALU.is_ge, ALU.mult))
                        s.link(nc.vector.scalar_tensor_tensor(out=gate_size[:, :], in0=gate[:, :], scalar=-1.0, in1=gate[:, :],
                                                              op0=ALU.mult, op1=ALU.max))
                        s.link(nc.vector.tensor_scalar(gate_size[:, :], gate_size[:, :], 0.25, None, ALU.max))
                        last = nc.vector.scalar_tensor_tensor(out=dst, in0=gate_sign[:, :], scalar=-1.0, in1=gate_size[:, :],
                                                              op0=ALU.add, op1=ALU.mult)
                    last.then_inc(row_done, 1)
                    dve.wait_ge(row_done, i * UN + u + 1)
                    nc.vector.sem_inc(mod_acc_free, 1)

        @block.tensor
        def _(pe):
            pe.wait_ge(silu_ready, 1)
            with pe.Fori(0, 2) as i:
                for u in range(UN):
                    pe.wait_ge(w_loaded[u % 3], i * 32 + 16 * (u // 3 + 1))
                    pe.wait_ge(mod_acc_free, i * UN + u + 2)
                    for k in range(KC):
                        last = nc.tensor.matmul(acc[:, u % 2], silu[:, k:k + 1], wbuf[:, u % 3, k], start=(k == 0), stop=(k == KC - 1))
                    last.then_inc(mod_acc_ready, 1)


def norm_in(nc, sem, x, mod_rows, identity, hT_hi, hT_lo):
    with ExitStack() as ctx:
        sb = lambda name, shape, dt: ctx.enter_context(nc.sbuf_tensor(name, shape, dt))
        ident = sb("n_ident", [P, P], F32)
        scale_b = sb("n_scale", [P, C], F32)
        shift_b = sb("n_shift", [P, C], F32)
        xt = sb("n_x", [P, TPC, C], F32)
        ht = sb("n_h", [P, TPC, C], F32)
        stats = sb("n_stats", [P, TPC, 2, 6], F32)
        mv = sb("n_mv", [P, TPC, 2], F32)
        std = sb("n_std", [P, TPC], F32)
        rstd = sb("n_rstd", [P, TPC], F32)
        newton = sb("n_newton", [P, TPC], F32)
        turned = ctx.enter_context(nc.psum_tensor("n_turned", [P, KC, CH], F32))
        const_loaded = sem("n_const_loaded")
        x_loaded = [sem(f"n_x_loaded{j}") for j in range(TPC)]
        x_free, h_free, bank_free = sem("n_x_free"), sem("n_h_free"), sem("n_bank_free")
        stat_step, var_ready, std_ready, xn_ready = sem("n_stat_step"), sem("n_var_ready"), sem("n_std_ready"), sem("n_xn_ready")
        stats_in = sem("n_stats_in")
        scaled, h_ready, bank_ready, hi_done = sem("n_scaled"), sem("n_h_ready"), sem("n_bank_ready"), sem("n_hi_done")
        block = ctx.enter_context(nc.Block())

        @block.sync
        def _(sp):
            sp.dma_start(ident[:, :], identity).then_inc(const_loaded, 16)
            sp.dma_start(shift_b[:, :], mod_rows[0:C].rearrange("(a n) -> a n", a=1).broadcast_to([P, C])).then_inc(const_loaded, 16)
            sp.dma_start(scale_b[:, :], mod_rows[C:2 * C].rearrange("(a n) -> a n", a=1).broadcast_to([P, C])).then_inc(const_loaded, 16)
            with sp.Fori(0, NQ) as i:
                for j in range(TPC):
                    sp.wait_ge(x_free, i * TPC + j + 1)
                    sp.dma_start(xt[:, j], x[ds((i * TPC + j) * P, P), :]).then_inc(x_loaded[j], 16)

        @block.vector
        def _(dve):
            dve.sem_inc(bank_free, KC)
            with dve.Fori(0, NQ) as i:
                s = Steps(dve, stat_step, i * (2 * TPC + 6))
                for j in range(TPC):
                    dve.wait_ge(x_loaded[j], i * 16 + 16)
                    nc.vector.bn_stats(stats[:, j, 0], xt[:, j, 0:CH])
                    s.link(nc.vector.bn_stats(stats[:, j, 1], xt[:, j, CH:C]))
                    nc.vector.sem_inc(stats_in, 1)
                    s.link(nc.vector.bn_aggr(mv[:, j], stats[:, j].rearrange("p a b -> p (a b)")))
                s.link(nc.vector.tensor_scalar(mv[:, :, 1], mv[:, :, 1], EPS, None, ALU.add))
                nc.vector.sem_inc(var_ready, 1)
                dve.wait_ge(std_ready, i + 1)
                s.link(nc.vector.reciprocal(rstd[:, :], std[:, :]))
                s.link(nc.vector.tensor_tensor(newton[:, :], rstd[:, :], rstd[:, :], ALU.mult))
                s.link(nc.vector.tensor_tensor(newton[:, :], newton[:, :], mv[:, :, 1], ALU.mult))
                s.link(nc.vector.tensor_scalar(newton[:, :], newton[:, :], -0.5, 1.5, ALU.mult, ALU.add))
                s.link(nc.vector.tensor_tensor(rstd[:, :], rstd[:, :], newton[:, :], ALU.mult))
                for j in range(TPC):
                    nc.vector.tensor_scalar(xt[:, j], xt[:, j], mv[:, j, 0:1], rstd[:, j:j + 1], ALU.subtract, ALU.mult).then_inc(xn_ready, 1)
                for k in range(KC):
                    dve.wait_ge(hi_done, i * KC + k + 1)
                    col = ds(i * CH, CH)
                    nc.vector.tensor_tensor(hT_lo[:, k, col], turned[:, k], hT_hi[:, k, col], ALU.subtract).then_inc(bank_free, 1)

        @block.gpsimd
        def _(pool):
            pool.sem_inc(x_free, TPC)
            pool.sem_inc(h_free, TPC)
            pool.wait_ge(const_loaded, 48)
            with pool.Fori(0, NQ) as i:
                for j in range(TPC):
                    pool.wait_ge(xn_ready, i * TPC + j + 1)
                    pool.wait_ge(h_free, i * TPC + j + 1)
                    nc.gpsimd.tensor_tensor(ht[:, j], xt[:, j], scale_b[:, :], ALU.mult).then_inc(scaled, 1)
                    pool.wait_ge(scaled, i * TPC + j + 1)
                    nc.gpsimd.tensor_tensor(ht[:, j], ht[:, j], shift_b[:, :], ALU.add).then_inc(h_ready, 1)
                    nc.gpsimd.sem_inc(x_free, 1)

        @block.tensor
        def _(pe):
            pe.wait_ge(const_loaded, 48)
            with pe.Fori(0, NQ) as i:
                for j in range(TPC):
                    pe.wait_ge(h_ready, i * TPC + j + 1)
                    for k in range(KC):
                        if j == 0:
                            pe.wait_ge(bank_free, i * KC + k + 1)
                        last = nc.tensor.transpose(turned[:, k, j * P:(j + 1) * P], ht[:, j, k * P:(k + 1) * P], ident[:, :])
                        if j == TPC - 1:
                            last.then_inc(bank_ready, 1)
                    if j < TPC - 1:
                        last.then_inc(h_free, 1)
                    else:
                        pe.wait_ge(bank_ready, i * KC + KC)
                        nc.tensor.sem_inc(h_free, 1)

        @block.scalar
        def _(act):
            nc.scalar.preload_act_table(ACT.Sqrt)
            with act.Fori(0, NQ) as i:
                act.wait_ge(var_ready, i + 1)
                nc.scalar.activation(std[:, :], mv[:, :, 1], ACT.Sqrt).then_inc(std_ready, 1)
                for k in range(KC):
                    act.wait_ge(bank_ready, i * KC + k + 1)
                    nc.scalar.activation(hT_hi[:, k, ds(i * CH, CH)], turned[:, k], ACT.Copy).then_inc(hi_done, 1)

BODY = 2 * NQ


def product(nc, acc, lhs, rhs):
    for k in range(KC):
        nc.tensor.matmul(acc, lhs(0, k), rhs(0, k), start=(k == 0), stop=False)
        nc.tensor.matmul(acc, lhs(0, k), rhs(1, k), start=False, stop=False)
        last = nc.tensor.matmul(acc, lhs(1, k), rhs(0, k), start=False, stop=(k == KC - 1))
    return last


def project(nc, sem, kind, w_tiles, first, hT, consts, ad, outs, rows_d=None):
    rope, adapted = kind != "v", kind != "q"
    with ExitStack() as ctx:
        sb = lambda name, shape, dt=F32: ctx.enter_context(nc.sbuf_tensor(f"{kind}_{name}", shape, dt))
        pb = lambda name, shape: ctx.enter_context(nc.psum_tensor(f"{kind}_{name}_psum", shape, F32))
        sm = lambda name: sem(f"{kind}_{name}")
        w_raw = sb("w_raw", [P, 2, C])
        w_hi = sb("w_hi", [P, 2, C], F32R)
        w_lo = sb("w_lo", [P, 2, C], F32R)
        acc = pb("acc", [P, 2, CH])
        if rope:
            cos = sb("cos", [P, T])
            sin = sb("sin", [P, T])
            x_cos = sb("x_cos", [P, CH])
            x_rot = sb("x_rot", [P, CH])
            y = sb("y", [P, 2, CH])
            y_hi = sb("y_hi", [P, 2, CH], F32R)
            y_lo = sb("y_lo", [P, 2, CH], F32R)
        else:
            zeros = sb("zeros", [P, C])
            ident = sb("ident", [P, P])
            vT = sb("vT", [P, 2, CH])
            v_out = sb("v_out", [P, 2, CH])
            turned = pb("turned", [P, 2, CH])
        if adapted:
            a_rep = sb("a_rep", [P, KC, HG, D])
            block_mask = sb("block_mask", [P, P])
            a_acc = pb("a_acc", [P, P])

        consts_loaded, w_raw_free = sm("consts_loaded"), sm("w_raw_free")
        w_loaded = [sm("w_loaded0"), sm("w_loaded1")]
        w_hi_done, w_ready, w_free = sm("w_hi_done"), sm("w_ready"), sm("w_free")
        acc_ready, acc_free = sm("acc_ready"), sm("acc_free")
        stored = [sm("stored0"), sm("stored1")]
        rep_cleared, rep_loaded, a_acc_ready, a_kept = sm("rep_cleared"), sm("rep_loaded"), sm("a_acc_ready"), sm("a_kept")
        rot_step, y_ready, y_hi_done, y_lo_done = sm("rot_step"), sm("y_ready"), sm("y_hi_done"), sm("y_lo_done")
        marks, zeros_set, zeroed = sm("marks"), sm("zeros_set"), sm("zeroed")
        FILLS = rows_d.shape[0] // P // G if rows_d is not None else 0
        vT_ready, turned_ready, v_out_ready = sm("vT_ready"), sm("turned_ready"), sm("v_out_ready")
        n_const = {"k": 3, "v": 2, "q": 2}[kind]
        STORES = 32 if rope else 16
        block = ctx.enter_context(nc.Block())

        @block.sync
        def _(sp):
            with sp.Fori(0, G // 2) as i:
                for v in range(2):
                    sp.wait_ge(w_raw_free, i * 2 + v + 1)
                    sp.dma_start(w_raw[:, v], w_tiles[ds(i * 2 + (first + v))].rearrange("a p n -> (a p) n")).then_inc(w_loaded[v], 16)

        @block.gpsimd
        def _(pool):
            pool.sem_inc(w_raw_free, 2)
            if adapted:
                nc.gpsimd.memset(a_rep[:, :, :, :], 0.0).then_inc(rep_cleared, 1)
            if FILLS:
                nc.gpsimd.memset(zeros[:, :], 0.0).then_inc(zeros_set, 1)
                pool.wait_ge(zeros_set, 1)
            with pool.Fori(0, G // 2) as i:
                for v in range(2):
                    pool.wait_ge(w_free, i * 2 + v + 1)
                    pool.wait_ge(w_loaded[v], i * 16 + 16)
                    pool.sem_inc(marks, 1)
                    nc.gpsimd.tensor_copy(w_hi[:, v], w_raw[:, v]).then_inc(w_hi_done, 1)
                    pool.wait_ge(w_hi_done, i * 2 + v + 1)
                    nc.gpsimd.tensor_tensor(w_lo[:, v], w_raw[:, v], w_hi[:, v], ALU.subtract).then_inc(w_ready, 1)
                    if not adapted:
                        pool.wait_ge(w_ready, i * 2 + v + 1)
                        pool.sem_inc(w_raw_free, 1)
                    for m in range(FILLS):
                        pool.dma_start(rows_d[ds(((i * 2 + v) * FILLS + m) * P, P), :], zeros[:, :]).then_inc(zeroed, 16)
            if FILLS:
                pool.wait_ge(zeroed, 16 * G * FILLS)

        @block.tensor
        def _(pe):
            pe.sem_inc(w_free, 2)

            def turn_v(i, u):
                pe.wait_ge(consts_loaded, 16 * n_const)
                pe.wait_ge(vT_ready, i * BODY + u + 1)
                pe.wait_ge(v_out_ready, i * BODY + u + 1)
                for j in range(TPC):
                    last = nc.tensor.transpose(turned[:, u % 2, j * P:(j + 1) * P], vT[:, u % 2, j * P:(j + 1) * P], ident[:, :])
                last.then_inc(turned_ready, 1)

            def adapter_too(i, v):
                pe.wait_ge(rep_loaded, 16 * HG)
                pe.wait_ge(a_kept, i * 2 + v + 1)
                for k in range(KC):
                    rep = a_rep[:, k].rearrange("p h a -> p (h a)")
                    w = w_raw[:, v, k * P:(k + 1) * P]
                    last = nc.tensor.matmul(a_acc[:, :], *((w, rep) if kind == "k" else (rep, w)), start=(k == 0), stop=(k == KC - 1))
                last.then_inc(a_acc_ready, 1)
                pe.wait_ge(a_acc_ready, i * 2 + v + 1)
                pe.sem_inc(w_raw_free, 1)

            with pe.Fori(0, G // 2) as i:
                for u in range(BODY):
                    v = u // NQ
                    if u % NQ == 0:
                        pe.wait_ge(w_ready, i * 2 + v + 1)
                    pe.wait_ge(acc_free, i * BODY + u + 1)
                    col = slice(u % NQ * CH, (u % NQ + 1) * CH)
                    product(nc, acc[:, u % 2],
                            lambda part, k: (w_hi, w_lo)[part][:, v, k * P:(k + 1) * P],
                            lambda part, k: hT[part][:, k, col]).then_inc(acc_ready, 1)
                    if adapted and u % NQ == 0:
                        adapter_too(i, v)
                    if kind == "v" and u >= 1:
                        turn_v(i, u - 1)
                    if u % NQ == NQ - 1:
                        pe.wait_ge(acc_ready, i * BODY + u + 1)
                        pe.sem_inc(w_free, 1)
                if kind == "v":
                    turn_v(i, BODY - 1)

        @block.scalar
        def _(act):
            nc.scalar.preload_act_table(ACT.Exp)
            act.wait_ge(w_loaded[0], 16)
            if adapted:
                act.wait_ge(rep_cleared, 1)
                for h in range(HG):
                    act.dma_start(a_rep[:, :, h, 0:A], consts["adapter"]).then_inc(rep_loaded, 16)
                act.dma_start(block_mask[:, :], consts["block_mask"]).then_inc(consts_loaded, 16)
            if rope:
                act.dma_start(cos[:, :], consts["cos"]).then_inc(consts_loaded, 16)
                act.dma_start(sin[:, :], consts["sin"]).then_inc(consts_loaded, 16)
            else:
                act.dma_start(ident[:, :], consts["ident"]).then_inc(consts_loaded, 16)
            with act.Fori(0, G // 2) as i:
                for u in range(BODY):
                    v, rows, n = u // NQ, ds((i * 2 + u // NQ)), i * BODY + u
                    if kind == "v":
                        act.wait_ge(acc_ready, n + 1)
                        act.wait_ge(turned_ready, n + 1)
                        nc.scalar.activation(vT[:, u % 2], acc[:, u % 2], ACT.Copy).then_inc(vT_ready, 1)
                        act.wait_ge(vT_ready, n + 1)
                        act.sem_inc(acc_free, 1)
                    else:
                        act.wait_ge(y_ready, n + 1)
                        act.wait_ge(stored[u % 2], i * (STORES * NQ) + STORES * (u // 2 + 1))
                        nc.scalar.activation(y_hi[:, u % 2], y[:, u % 2], ACT.Copy).then_inc(y_hi_done, 1)
                    for b in ([u - 1] if u else []) + ([u] if u == BODY - 1 else []):
                        g = ds(i * 2 + b // NQ)
                        if kind == "v":
                            act.wait_ge(v_out_ready, i * BODY + b + 3)
                            t0 = b % NQ * TPC
                            act.dma_start(outs[0][g, :, t0:t0 + TPC, :].rearrange("g p k n -> (g p) (k n)"), v_out[:, b % 2]).then_inc(stored[b % 2], 16)
                        else:
                            col = slice(b % NQ * CH, (b % NQ + 1) * CH)
                            act.wait_ge(y_lo_done, i * BODY + b + 1)
                            for part, src in ((0, y_hi), (1, y_lo)):
                                act.dma_start(outs[part][g, :, col].rearrange("g p n -> (g p) n"), src[:, b % 2].bitcast(F32)).then_inc(stored[b % 2], 16)
            for b in range(2):
                act.wait_ge(stored[b], STORES * (G * NQ // 2 + 1))

        @block.vector
        def _(dve):
            dve.sem_inc(acc_free, 2)
            for b in range(2):
                dve.sem_inc(stored[b], STORES)
            if kind == "v":
                dve.sem_inc(turned_ready, 2)
                dve.sem_inc(v_out_ready, 2)
            if adapted:
                dve.sem_inc(a_kept, 1)
            dve.wait_ge(consts_loaded, 16 * n_const)
            swap = [(d + D // 2) % D for d in range(D)]

            def keep_adapter(i, v):
                dve.wait_ge(a_acc_ready, i * 2 + v + 1)
                nc.vector.tensor_tensor(ad[:, ds(i * 2 + v)].rearrange("p a n -> p (a n)"), a_acc[:, :], block_mask[:, :],
                                        ALU.mult).then_inc(a_kept, 1)

            def rotate(i, u):
                s = Steps(dve, rot_step, i * (3 * BODY) + 3 * u)
                col = slice(u % NQ * CH, (u % NQ + 1) * CH)
                dve.wait_ge(acc_ready, i * BODY + u + 1)
                dve.sem_inc(marks, 1)
                nc.vector.stream_shuffle(x_rot[:, :], acc[:, u % 2], swap)
                s.link(nc.vector.tensor_tensor(x_cos[:, :], acc[:, u % 2], cos[:, col], ALU.mult))
                dve.sem_inc(acc_free, 1)
                s.link(nc.vector.tensor_tensor(x_rot[:, :], x_rot[:, :], sin[:, col], ALU.mult))
                dve.wait_ge(stored[u % 2], i * (STORES * NQ) + STORES * (u // 2 + 1))
                s.link(nc.vector.tensor_tensor(y[:, u % 2], x_cos[:, :], x_rot[:, :], ALU.add))
                dve.sem_inc(y_ready, 1)

            def split(i, u):
                dve.wait_ge(y_hi_done, i * BODY + u + 1)
                nc.vector.tensor_tensor(y_lo[:, u % 2], y[:, u % 2], y_hi[:, u % 2], ALU.subtract).then_inc(y_lo_done, 1)

            def out_v(i, u):
                dve.wait_ge(turned_ready, i * BODY + u + 3)
                dve.wait_ge(stored[u % 2], i * (STORES * NQ) + STORES * (u // 2 + 1))
                nc.vector.tensor_copy(v_out[:, u % 2], turned[:, u % 2]).then_inc(v_out_ready, 1)

            with dve.Fori(0, G // 2) as i:
                for u in range(BODY):
                    if rope:
                        rotate(i, u)
                    if adapted and u % NQ == 0:
                        keep_adapter(i, u // NQ)
                    if u >= 1:
                        (split if rope else out_v)(i, u - 1)
                (split if rope else out_v)(i, BODY - 1)


def adapter_attention(nc, sem, consts, ak, av, q_hi_d, q_lo_d, out):
    UN = 2 * NQ
    with ExitStack() as ctx:
        sb = lambda name, shape, dt=F32: ctx.enter_context(nc.sbuf_tensor(f"a_{name}", shape, dt))
        pb = lambda name, shape: ctx.enter_context(nc.psum_tensor(f"a_{name}_psum", shape, F32))
        sm = lambda name: sem(f"a_{name}")
        M = TPC * HG
        ident = sb("ident", [P, P])
        gating = sb("gating", [P, 1])
        q_hi, q_lo, q = sb("q_hi", [P, UN, CH]), sb("q_lo", [P, UN, CH]), sb("q", [P, UN, CH])
        av_cur = sb("av_cur", [P, 2, P])
        top, total, inv = sb("top", [P, M]), sb("total", [P, M]), sb("inv", [P, M])
        weight = sb("weight", [P, UN, M, A])
        prob = sb("prob", [P, UN, M, D])
        probT = sb("probT", [P, 2, CH])
        y = sb("y", [P, UN, CH])
        scores, turned, acc = pb("scores", [P, 2, CH]), pb("turned", [P, 2, CH]), pb("acc", [P, 2, CH])
        consts_loaded, cleared = sm("consts_loaded"), sm("cleared")
        q_loaded = [sm(f"q_loaded{u}") for u in range(UN)]
        q_ready, q_used, scores_ready, step, shifted, exp_done = sm("q_ready"), sm("q_used"), sm("scores_ready"), sm("step"), sm("shifted"), sm("exp_done")
        prob_ready, turned_ready, probT_ready, av_ready, acc_ready, y_ready = (
            sm("prob_ready"), sm("turned_ready"), sm("probT_ready"), sm("av_ready"), sm("acc_ready"), sm("y_ready"))
        stored, marks = [sm(f"stored{u}") for u in range(UN)], sm("marks")
        block = ctx.enter_context(nc.Block())

        @block.sync
        def _(sp):
            sp.dma_start(ident[:, :], consts["ident"]).then_inc(consts_loaded, 16)
            sp.dma_start(gating[:, :], consts["gating"].rearrange("(a n) -> a n", a=1).broadcast_to([P, 1])).then_inc(consts_loaded, 16)
            with sp.Fori(0, G // 2) as i:
                for u in range(UN):
                    sp.wait_ge(q_ready, i * UN + u + 1)
                    for src, dst in ((q_hi_d, q_hi), (q_lo_d, q_lo)):
                        sp.dma_start(dst[:, u], src[ds(i * 2 + u // NQ), :, u % NQ * CH:(u % NQ + 1) * CH].rearrange("g p n -> (g p) n")).then_inc(q_loaded[u], 16)

        @block.gpsimd
        def _(pool):
            pool.sem_inc(q_ready, UN)
            pool.sem_inc(acc_ready, UN)
            nc.gpsimd.memset(prob[:, :, :, :], 0.0).then_inc(cleared, 1)
            with pool.Fori(0, G // 2) as i:
                pool.wait_ge(acc_ready, i * UN + UN)
                pool.sem_inc(marks, 1)
                nc.gpsimd.tensor_copy(av_cur[:, :, :], av[:, ds(i * 2, 2)]).then_inc(av_ready, 1)
                for u in range(UN):
                    pool.wait_ge(q_loaded[u], i * 32 + 32)
                    pool.wait_ge(q_used, i * UN + u + 1)
                    nc.gpsimd.tensor_tensor(q[:, u], q_hi[:, u], q_lo[:, u], ALU.add).then_inc(q_ready, 1)

        @block.tensor
        def _(pe):
            pe.sem_inc(q_used, UN)
            pe.wait_ge(consts_loaded, 32)

            def score(i, u):
                pe.wait_ge(q_ready, i * UN + u + 1 + UN)
                pe.wait_ge(shifted, i * UN + u + 1)
                for j in range(TPC):
                    last = nc.tensor.matmul(scores[:, u % 2, j * P:(j + 1) * P], q[:, u, j * P:(j + 1) * P],
                                            ak[:, ds(i * 2 + u // NQ)].rearrange("p a n -> p (a n)"), start=True, stop=True)
                last.then_inc(scores_ready, 1)
                pe.wait_ge(scores_ready, i * UN + u + 1)
                pe.sem_inc(q_used, 1)

            def turn(i, u):
                pe.wait_ge(prob_ready, i * UN + u + 1)
                pe.wait_ge(probT_ready, i * UN + u + 1)
                for j in range(TPC):
                    last = nc.tensor.transpose(turned[:, u % 2, j * P:(j + 1) * P],
                                               prob[:, u, j * HG:(j + 1) * HG, :].rearrange("p h a -> p (h a)"), ident[:, :])
                last.then_inc(turned_ready, 1)

            def multiply(i, u):
                pe.wait_ge(probT_ready, i * UN + u + 3)
                pe.wait_ge(av_ready, i + 1)
                pe.wait_ge(y_ready, i * UN + u + 1)
                nc.tensor.matmul(acc[:, u % 2], av_cur[:, u // NQ], probT[:, u % 2], start=True, stop=True).then_inc(acc_ready, 1)

            with pe.Fori(0, G // 2) as i:
                for u in range(UN + 3):
                    if u < UN:
                        score(i, u)
                    if 2 <= u <= UN + 1:
                        turn(i, u - 2)
                    if u >= 3:
                        multiply(i, u - 3)

        @block.vector
        def _(dve):
            dve.sem_inc(shifted, 2)
            dve.wait_ge(consts_loaded, 32)
            dve.wait_ge(cleared, 1)

            def shift(i, u, s):
                dve.wait_ge(scores_ready, i * UN + u + 1)
                dve.wait_ge(shifted, i * UN + u + 2)
                view = scores[:, u % 2].rearrange("p (m a) -> p m a", a=D)[:, :, 0:A]
                s.link(nc.vector.tensor_reduce(top[:, :], view, AX.X, ALU.max))
                nc.vector.tensor_tensor(weight[:, u], view, top[:, :].rearrange("p (m a) -> p m a", a=1).broadcast_to([P, M, A]),
                                        ALU.subtract).then_inc(shifted, 1)

            def norm(i, u, s):
                dve.wait_ge(exp_done, i * UN + u + 1)
                s.link(nc.vector.tensor_reduce(total[:, :], weight[:, u], AX.X, ALU.add))
                s.link(nc.vector.reciprocal(inv[:, :], total[:, :]))
                s.link(nc.vector.tensor_scalar(inv[:, :], inv[:, :], gating[:, 0:1], None, ALU.mult))
                s.link(nc.vector.tensor_tensor(prob[:, u, :, 0:A], weight[:, u],
                                               inv[:, :].rearrange("p (m a) -> p m a", a=1).broadcast_to([P, M, A]), ALU.mult))
                dve.sem_inc(prob_ready, 1)

            with dve.Fori(0, G // 2) as i:
                s = Steps(dve, step, i * (5 * UN))
                for u in range(UN + 1):
                    if u < UN:
                        shift(i, u, s)
                    if u >= 1:
                        norm(i, u - 1, s)

        @block.scalar
        def _(act):
            nc.scalar.preload_act_table(ACT.Exp)
            act.sem_inc(probT_ready, 2)
            act.sem_inc(y_ready, 2)
            for u in range(UN):
                act.sem_inc(stored[u], 16)
            with act.Fori(0, G // 2) as i:
                for u in range(UN + 3):
                    if u < UN:
                        act.wait_ge(shifted, i * UN + u + 3)
                        nc.scalar.activation(weight[:, u], weight[:, u], ACT.Exp, scale=1.0 / math.sqrt(C)).then_inc(exp_done, 1)
                    if 2 <= u <= UN + 1:
                        b = u - 2
                        act.wait_ge(turned_ready, i * UN + b + 1)
                        act.wait_ge(acc_ready, i * UN + b + UN - 1)
                        nc.scalar.activation(probT[:, b % 2], turned[:, b % 2], ACT.Copy).then_inc(probT_ready, 1)
                    if u >= 3:
                        b = u - 3
                        act.wait_ge(acc_ready, i * UN + b + UN + 1)
                        act.wait_ge(stored[b], i * 16 + 16)
                        nc.scalar.activation(y[:, b], acc[:, b % 2], ACT.Copy).then_inc(y_ready, 1)
                        act.wait_ge(y_ready, i * UN + b + 3)
                        act.dma_start(out[ds(i * 2 + b // NQ), :, b % NQ * CH:(b % NQ + 1) * CH].rearrange("g p n -> (g p) n"), y[:, b]).then_inc(stored[b], 16)
            for u in range(UN):
                act.wait_ge(stored[u], 16 * (G // 2 + 1))

MASKED = -1.0e38
BF16 = mybir.dt.bfloat16
HALF = HG // 2
STACK = 3 * D


def attention(nc, sem, consts, q_parts, k_parts, v_d, a_d, out_parts):
    UNITS = [(par, qc) for par in range(2) for qc in range(NQ)]
    W = len(UNITS)
    steps_of = lambda qc: TPC * (qc + 1)
    STEPS = sum(steps_of(qc) for _, qc in UNITS)
    items_of = lambda qc: HG * TPC * (qc + 1)
    ITEMS = sum(items_of(qc) for _, qc in UNITS) + W
    PAIRS = STEPS // 2
    RING = 4
    Y_LAG, A_LAG, TOTAL_LAG, NORM_LAG, SPLIT_LAG, STORE_LAG = 2, 2, 3, 4, 6, 7
    LOADS = 7 * 16
    ROW = HG * 16
    with ExitStack() as ctx:
        sb = lambda name, shape, dt=F32: ctx.enter_context(nc.sbuf_tensor(f"t_{name}", shape, dt))
        pb = lambda name, shape: ctx.enter_context(nc.psum_tensor(f"t_{name}_psum", shape, F32))
        sm = lambda name: sem(f"t_{name}")
        q_stack = [sb(f"q_stack{b}", [P, HG, T], F32R) for b in range(2)]
        k_stack = [sb(f"k_stack{b}", [P, HG, T], F32R) for b in range(2)]
        v = [sb(f"v{b}", [P, NT, P]) for b in range(2)]
        ident = sb("ident", [P, P])
        causal = sb("causal", [P, CH])
        after = sb("after", [P, P])
        ident_b, after_b = sb("ident_b", [P, P], BF16), sb("after_b", [P, P], BF16)
        ones = sb("ones", [P, D])
        part = sb("part", [P, HG * TPC, NQ])
        top = sb("top", [P, HG * TPC])
        minus_top = sb("minus_top", [HG * TPC, 2, P], F32R)
        prob, two = sb("prob", [P, RING, 2, HALF, CH]), sb("two", [P, 2, 2, HALF, CH])
        y_own, whole = sb("y_own", [P, CH]), sb("whole", [P, CH])
        y = sb("y", [P, CH])
        y_hi, y_lo = sb("y_hi", [P, CH], F32R), sb("y_lo", [P, CH], F32R)
        seen = pb("seen", [P, 2, CH])
        scores = pb("scores", [P, 2, HALF, CH])
        y_acc, total = pb("y_acc", [P, CH]), pb("total", [P, CH])

        consts_loaded, ones_set = sm("consts_loaded"), sm("ones_set")
        loaded = [sm("loaded0"), sm("loaded1")]
        seen_ready, seen_free, top_ready, minus_ready = sm("seen_ready"), sm("seen_free"), sm("top_ready"), sm("minus_ready")
        row_loaded = [sm("row_loaded0"), sm("row_loaded1")]
        scores_ready, exp_done, sums_set, cleared = sm("scores_ready"), sm("exp_done"), sm("sums_set"), sm("cleared")
        y_done, two_ready, total_done, y_free, total_free = sm("y_done"), sm("two_ready"), sm("total_done"), sm("y_free"), sm("total_free")
        a_loaded, stored = sm("a_loaded"), sm("stored")
        norm_step, y_ready, y_hi_done, y_lo_done = sm("norm_step"), sm("y_ready"), sm("y_hi_done"), sm("y_lo_done")
        marks = sm("marks")
        block = ctx.enter_context(nc.Block())

        def first_step(wi):
            return sum(steps_of(UNITS[w][1]) for w in range(wi))

        def last_step(wi):
            return first_step(wi + 1) - 1

        steps = [(wi, s) for wi, (_, qc) in enumerate(UNITS) for s in range(steps_of(qc))]

        def ended(i, step, lag):
            return [wi for wi in range(-1, 0 if isinstance(i, int) else W) if last_step(wi) == step - lag]

        def first_column(step):
            wi, kt = steps[step]
            return max(kt - UNITS[wi][1] * TPC, 0) * P

        def group_of(i, wi):
            par = UNITS[wi][0]
            return ds(i * 2 + par) if wi >= 0 else ds((i * 2 + (G - 2 + par)) % G)

        order = []
        for dg in range(3):
            for qc in range(NQ):
                order += [("see", dg, qc, c, h, j) for c in range(qc + 1) for h in range(HG) for j in range(TPC)]
                order.append(("turn", dg, qc, 0, 0, 0))
        for n in [n for n, entry in enumerate(order) if entry[0] == "turn"][-2::-1]:
            order.insert(n + 2, order.pop(n))
        AHEAD = items_of(NQ - 1) + 3 * HG
        PACE = HG

        def until(banks):
            seen_so_far = 0
            for n, entry in enumerate(order):
                if entry[0] == "see":
                    if seen_so_far == banks:
                        return n
                    seen_so_far += 1

        HEAD = until(AHEAD)
        upto = lambda step: until(AHEAD + PACE * step + step % 2)
        entries_of = lambda step: range(upto(step), upto(step + 1))
        assert STEPS % RING == 0

        def share(step, quarter):
            entries = entries_of(step)
            ends = [0, 1, 2, 4, 5] if step % 2 == 0 else [0, 1, 2, 3, 3]
            return entries[len(entries) * ends[quarter] // ends[4]:len(entries) * ends[quarter + 1] // ends[4]]
        unit_of = lambda entry: entry[1] * NQ + entry[2]
        assert until(AHEAD + PACE * STEPS) - HEAD == ITEMS and ITEMS % 2 == 0
        ends_unit = {n for n, entry in enumerate(order) if entry[0] == "see" and
                     unit_of(entry) != unit_of(next((x for x in order[n + 1:] if x[0] == "see"), (0, -1, 0)))}

        def load_group(eng, par, g):
            for src, dst, rows in ((q_parts[0], q_stack, 0), (q_parts[1], q_stack, 1), (q_parts[0], q_stack, 2),
                                   (k_parts[0], k_stack, 0), (k_parts[0], k_stack, 1), (k_parts[1], k_stack, 2)):
                eng.dma_start(dst[par][rows * D:(rows + 1) * D, :, :].bitcast(F32),
                              src[g].rearrange("g (h d) n -> d (g h) n", d=D)).then_inc(loaded[par], 16)
            eng.dma_start(v[par][:, :, :], v_d[g].rearrange("g p k n -> (g p) k n")).then_inc(loaded[par], 16)

        def load_row(eng, par, qc, b):
            for h in range(HG):
                dst = q_stack[par][STACK:STACK + 1, h, qc * CH:(qc + 1) * CH].bitcast(F32)
                eng.dma_start(dst.rearrange("a (j c) -> a j c", c=P), minus_top[h * TPC:(h + 1) * TPC, b].bitcast(F32)).then_inc(row_loaded[b], 16)

        def store(eng, i, wi):
            qc = UNITS[wi][1]
            eng.wait_ge(y_lo_done, i * W + wi + 3)
            for dst, src in zip(out_parts, (y_hi, y_lo)):
                eng.dma_start(dst[group_of(i, wi), :, qc * CH:(qc + 1) * CH].rearrange("g p n -> (g p) n"),
                              src[:, :].bitcast(F32)).then_inc(stored, 16)

        @block.sync
        def _(sp):
            sp.dma_start(ident[:, :], consts["ident"]).then_inc(consts_loaded, 16)
            sp.dma_start(causal[:, :], consts["causal"]).then_inc(consts_loaded, 16)
            sp.dma_start(after[:, :], consts["after"]).then_inc(consts_loaded, 16)
            load_group(sp, 0, ds(0))
            for entry in order[:HEAD]:
                if entry[0] == "turn":
                    sp.wait_ge(minus_ready, unit_of(entry) + 1)
                    load_row(sp, entry[1] % 2, entry[2], unit_of(entry) % 2)

            def finish(i, step):
                for wi in ended(i, step, A_LAG):
                    qc = UNITS[wi][1]
                    sp.wait_ge(y_lo_done, i * W + wi + 2)
                    sp.dma_start(y[:, :], a_d[group_of(i, wi), :, qc * CH:(qc + 1) * CH].rearrange("g p n -> (g p) n")).then_inc(a_loaded, 16)
                for wi in ended(i, step, STORE_LAG):
                    store(sp, i, wi)

            with sp.Fori(0, G // 2) as i:
                for step in range(STEPS):
                    finish(i, step)
                    for n in entries_of(step):
                        if order[n][0] == "turn":
                            sp.wait_ge(minus_ready, i * W + unit_of(order[n]) + 1)
                            load_row(sp, order[n][1] % 2, order[n][2], unit_of(order[n]) % 2)
            for step in range(STORE_LAG):
                finish(G // 2, step)
            sp.wait_ge(stored, 32 * (G * NQ + 2))
            for b in range(2):
                sp.wait_ge(row_loaded[b], ROW * (G * NQ // 2 + 1 + sum(e[0] == "turn" and unit_of(e) % 2 == b for e in order[:HEAD])))

        @block.tensor
        def _(pe):
            def see(base, n, par, qc, c, h, j):
                width = CH if c < qc else (j + 1) * P
                pe.wait_ge(seen_free, base + n + 1)
                t0 = qc * CH + j * P
                nc.tensor.matmul(seen[:, n % 2, 0:width], q_stack[par][0:STACK, h, t0:t0 + P],
                                 k_stack[par][0:STACK, h, c * CH:c * CH + width], start=True, stop=True).then_inc(seen_ready, 1)

            def turn_top(base, n, w):
                pe.wait_ge(top_ready, w + 1)
                pe.wait_ge(seen_free, base + n + 1)
                nc.tensor.transpose(seen[0:HG * TPC, n % 2, 0:P], top[:, :], ident[:, :]).then_inc(seen_ready, 1)

            def advance(i, n):
                what, dg, qc, c, h, j = order[n]
                if what == "see":
                    see(i * ITEMS, n, dg % 2, qc, c, h, j)
                else:
                    turn_top(i * ITEMS, n, i * W + unit_of(order[n]))

            def score(i, step, pair):
                wi, kt = steps[step]
                par, qc = UNITS[wi]
                c0, r = first_column(step), kt - qc * TPC
                pe.wait_ge(exp_done, (i * STEPS + step) * 2 + pair + 1)
                for x in range(HALF):
                    h = pair * HALF + x
                    last = nc.tensor.matmul(scores[:, pair, x, c0:CH], k_stack[par][0:STACK + 1, h, kt * P:(kt + 1) * P],
                                            q_stack[par][0:STACK + 1, h, qc * CH + c0:(qc + 1) * CH], start=True, stop=(r < 0))
                    if r >= 0:
                        last = nc.tensor.matmul(scores[:, pair, x, c0:c0 + P], ident_b[:, :], after_b[:, :],
                                                start=False, stop=True)
                last.then_inc(scores_ready, 1)

            def multiply(i, step):
                wi, kt = steps[step]
                par, qc = UNITS[wi]
                c0 = first_column(step)
                if step >= 0 or isinstance(i, int):
                    pe.wait_ge(exp_done, (i * STEPS + step) * 2 + 4)
                if kt == 0:
                    pe.wait_ge(y_free, i * W + wi + 1)
                for h in range(HG):
                    last = nc.tensor.matmul(y_acc[h * D:(h + 1) * D, c0:CH], v[par][:, kt, h * D:(h + 1) * D],
                                            prob[:, step % RING, h // HALF, h % HALF, c0:CH],
                                            start=(kt == 0), stop=(kt == steps_of(qc) - 1))
                last.then_inc(y_done, 1)

            def add_up(i, pair):
                wi, kt = steps[2 * pair]
                c0 = first_column(2 * pair)
                pe.wait_ge(two_ready, (i * PAIRS + pair) * 2 + 6)
                if kt == 0:
                    pe.wait_ge(total_free, i * W + wi + 1)
                for h in range(HG):
                    last = nc.tensor.matmul(total[h * D:(h + 1) * D, c0:CH], ones[:, :], two[:, pair % 2, h // HALF, h % HALF, c0:CH],
                                            start=(kt == 0), stop=(kt == steps_of(UNITS[wi][1]) - 2))
                last.then_inc(total_done, 1)

            pe.wait_ge(consts_loaded, 48)
            pe.wait_ge(ones_set, 6)
            pe.wait_ge(sums_set, 2)
            pe.wait_ge(loaded[0], LOADS)
            for n in range(HEAD):
                advance(0, n)
            for acc, lhs in ((y_acc, v[1][:, NT - 1, 0:D]), (total, ones[:, :])):
                for h in range(HG):
                    nc.tensor.matmul(acc[h * D:(h + 1) * D, :], lhs, prob[:, 0, 0, 0], start=True, stop=False)

            def add_step(i, step):
                if step % 2 == 0:
                    add_up(i, (step - TOTAL_LAG - 1) // 2)

            with pe.Fori(0, G // 2) as i:
                for step in range(STEPS):
                    wi = steps[step][0]
                    if steps[step][1] == 0:
                        pe.wait_ge(row_loaded[wi % 2], i * (ROW * W // 2) + ROW * (wi // 2 + 2))
                    for quarter in range(4):
                        if quarter < 2:
                            score(i, step, quarter)
                        elif quarter == 2:
                            multiply(i, step - Y_LAG)
                        else:
                            add_step(i, step)
                        for n in share(step, quarter):
                            if order[n][1] > 0 and order[n - 1][1:] != order[n][1:] and order[n][:1] + order[n][2:] == ("see", 0, 0, 0, 0):
                                pe.wait_ge(loaded[order[n][1] % 2], i * LOADS + LOADS * (1 + (order[n][1] == 2)))
                            advance(i, n)
            for step in range(TOTAL_LAG):
                if step < Y_LAG:
                    multiply(G // 2, step - Y_LAG)
                add_step(G // 2, step)

        @block.scalar
        def _(act):
            nc.scalar.preload_act_table(ACT.Exp)
            act.sem_inc(exp_done, 2)
            act.wait_ge(sums_set, 2)

            def take_y(i, wi):
                act.wait_ge(y_done, i * STEPS + last_step(wi) + 1 + RING)
                act.wait_ge(y_ready, i * W + wi + 2)
                nc.scalar.activation(y_own[:, :], y_acc[:, :], ACT.Copy).then_inc(y_free, 1)

            def take_total(i, wi):
                act.wait_ge(total_done, i * PAIRS + last_step(wi) // 2 + 3)
                act.wait_ge(y_ready, i * W + wi + 2)
                nc.scalar.activation(whole[:, :], total[:, :], ACT.Copy).then_inc(total_free, 1)

            def finish(i, step):
                for wi in ended(i, step, Y_LAG):
                    take_y(i, wi)
                    if not isinstance(i, int) and wi in (-1, NQ - 1):
                        load_group(act, 1 if wi == -1 else 0, ds(i * 2 + 1) if wi == -1 else ds((i * 2 + 2) % G))
                for wi in ended(i, step, TOTAL_LAG):
                    take_total(i, wi)

            with act.Fori(0, G // 2) as i:
                for step in range(STEPS):
                    c0 = first_column(step)
                    act.wait_ge(y_done, i * STEPS + step + 1)
                    if step % 2 == 0:
                        act.wait_ge(two_ready, (i * PAIRS + step // 2) * 2 + 2)
                    for pair in range(2):
                        act.wait_ge(scores_ready, (i * STEPS + step) * 2 + pair + 1)
                        nc.scalar.activation(prob[:, step % RING, pair, :, c0:CH], scores[:, pair, :, c0:CH], ACT.Exp,
                                             scale=1.0 / math.sqrt(D)).then_inc(exp_done, 1)
                    finish(i, step)
            for step in range(TOTAL_LAG + 1):
                finish(G // 2, step)

        @block.vector
        def _(dve):
            dve.sem_inc(seen_free, 2)
            dve.sem_inc(y_ready, 1)
            dve.sem_inc(y_done, RING - Y_LAG)
            dve.sem_inc(stored, 32)
            for b in range(2):
                dve.sem_inc(row_loaded[b], ROW)
            nc.vector.memset(ones[:, :], 1.0).then_inc(ones_set, 1)
            for b in range(2):
                nc.vector.memset(k_stack[b][STACK:STACK + 1, :, :].bitcast(F32), 1.0).then_inc(ones_set, 1)
            nc.vector.memset(v[1][:, NT - 2:NT], 1.0).then_inc(ones_set, 1)
            dve.wait_ge(consts_loaded, 48)
            nc.vector.tensor_copy(ident_b[:, :], ident[:, :]).then_inc(ones_set, 1)
            nc.vector.tensor_copy(after_b[:, :], after[:, :]).then_inc(ones_set, 1)

            def largest(base, n, qc, c, h, j):
                dve.wait_ge(seen_ready, base + n + 1)
                dst = part[:, h * TPC + j, c:c + 1]
                if c < qc:
                    nc.vector.tensor_reduce(dst, seen[:, n % 2], AX.X, ALU.max).then_inc(seen_free, 1)
                else:
                    dve.sem_inc(marks, 1)
                    width = (j + 1) * P
                    nc.vector.tensor_tensor_reduce(out=seen[:, n % 2, 0:width], in0=seen[:, n % 2, 0:width], in1=causal[:, CH - width:CH],
                                                   scale=1.0, scalar=MASKED, op0=ALU.add, op1=ALU.max, accum_out=dst).then_inc(seen_free, 1)

            def gather(base, n, w, qc):
                dve.wait_ge(seen_free, base + n + 3)
                nc.vector.tensor_reduce(top[:, :], part[:, :, 0:qc + 1], AX.X, ALU.max).then_inc(top_ready, 1)
                dve.wait_ge(top_ready, w + 1)

            def negate(base, n, w, rows, b):
                dve.wait_ge(seen_ready, base + n + 1)
                dve.wait_ge(row_loaded[b], rows * ROW + ROW)
                nc.vector.tensor_scalar(minus_top[:, b], seen[0:HG * TPC, n % 2, 0:P], -1.0, None, ALU.mult).then_inc(minus_ready, 1)
                dve.wait_ge(minus_ready, w + 1)
                dve.sem_inc(seen_free, 1)

            def advance(i, n):
                what, dg, qc, c, h, j = order[n]
                w = unit_of(order[n])
                if what == "see":
                    largest(i * ITEMS, n, qc, c, h, j)
                    if n in ends_unit:
                        gather(i * ITEMS, n, i * W + w, qc)
                else:
                    negate(i * ITEMS, n, i * W + w, i * (W // 2) + w // 2, w % 2)

            def invert(i, wi, piece):
                if piece == 0:
                    dve.wait_ge(total_free, i * W + wi + 2)
                col = slice(piece * P, (piece + 1) * P)
                nc.vector.reciprocal(whole[:, col], whole[:, col]).then_inc(norm_step, 1)

            def divide(i, wi):
                at = (i * W + wi + 1) * (TPC + 1) + TPC
                dve.wait_ge(norm_step, at)
                dve.wait_ge(y_free, i * W + wi + 2)
                nc.vector.tensor_tensor(y_own[:, :], y_own[:, :], whole[:, :], ALU.mult).then_inc(norm_step, 1)
                dve.wait_ge(norm_step, at + 1)
                dve.wait_ge(a_loaded, (i * W + wi + 2) * 16)
                nc.vector.tensor_tensor(y[:, :], y[:, :], y_own[:, :], ALU.add).then_inc(y_ready, 1)

            for n in range(HEAD):
                advance(0, n)

            def finish(i, step, quarter):
                for wi in ended(i, step, NORM_LAG):
                    invert(i, wi, quarter)
                for wi in ended(i, step, NORM_LAG + 1):
                    if quarter == 1:
                        divide(i, wi)

            with dve.Fori(0, G // 2) as i:
                for step in range(STEPS):
                    for quarter in range(TPC):
                        for n in share(step, quarter):
                            advance(i, n)
                        finish(i, step, quarter)
            for step in range(NORM_LAG + 1):
                for quarter in range(TPC):
                    finish(G // 2, step, quarter)

        @block.gpsimd
        def _(pool):
            pool.sem_inc(y_lo_done, 1)
            pool.sem_inc(two_ready, 3)
            nc.gpsimd.memset(prob[:, :, :, :, :], 1.0).then_inc(sums_set, 1)
            nc.gpsimd.memset(two[:, :, :, :, :], 1.0).then_inc(sums_set, 1)
            pool.wait_ge(sums_set, 2)

            def add_two(i, pair, half):
                c0 = first_column(2 * pair)
                if half == 0:
                    pool.wait_ge(exp_done, (i * STEPS + 2 * pair + 1) * 2 + 4)
                    pool.wait_ge(total_done, i * PAIRS + pair + 1)
                    c1 = first_column(2 * pair + 1)
                    if c1 > c0:
                        pool.sem_inc(marks, 1)
                        nc.gpsimd.memset(prob[:, (2 * pair + 1) % RING, :, :, c0:c1], 0.0).then_inc(cleared, 1)
                        pool.wait_ge(cleared, (i * W + steps[2 * pair][0]) * (TPC // 2) + (c0 > 0) + 1)
                a, b = (prob[:, (2 * pair + x) % RING, half, :, c0:CH] for x in range(2))
                nc.gpsimd.tensor_tensor(two[:, pair % 2, half, :, c0:CH], a, b, ALU.add).then_inc(two_ready, 1)

            def split(i, wi):
                pool.wait_ge(y_ready, i * W + wi + 3)
                pool.wait_ge(stored, (i * W + wi + 2) * 32)
                pool.sem_inc(marks, 1)
                nc.gpsimd.tensor_copy(y_hi[:, :], y[:, :]).then_inc(y_hi_done, 1)
                pool.wait_ge(y_hi_done, i * W + wi + 2)
                nc.gpsimd.tensor_tensor(y_lo[:, :], y[:, :], y_hi[:, :], ALU.subtract).then_inc(y_lo_done, 1)

            def finish(i, step):
                if step % 2 == 0:
                    add_two(i, step // 2 - 1, 1)
                for wi in ended(i, step, SPLIT_LAG):
                    split(i, wi)

            with pool.Fori(0, G // 2) as i:
                for step in range(STEPS):
                    finish(i, step)
                    if step % 2 == 1:
                        add_two(i, step // 2, 0)
            for step in range(SPLIT_LAG):
                if step == 0:
                    add_two(G // 2, -1, 1)
                for wi in ended(i, step, SPLIT_LAG):
                    split(G // 2, wi)

MT = 2
MROWS = MT * P
MAX_MACRO = 2 * T // MROWS + E - 1
LAG = 2


def proj_out(nc, sem, consts, mod_rows, w_proj, y_parts, x, x1_d, h2, logitsT):
    with ExitStack() as ctx:
        sb = lambda name, shape, dt=F32: ctx.enter_context(nc.sbuf_tensor(f"o_{name}", shape, dt))
        pb = lambda name, shape: ctx.enter_context(nc.psum_tensor(f"o_{name}_psum", shape, F32))
        sm = lambda name: sem(f"o_{name}")
        w_raw = sb("w_raw", [P, 2, C])
        w_hi, w_lo = sb("w_hi", [P, KC, C], F32R), sb("w_lo", [P, KC, C], F32R)
        ident = sb("ident", [P, P])
        gate_w = sb("gate_w", [P, KC, E])
        ga, shift_b, scale_b = sb("ga", [P, C]), sb("shift", [P, C]), sb("scale", [P, C])
        y_hi, y_lo = sb("y_hi", [P, 2, G, P], F32R), sb("y_lo", [P, 2, G, P], F32R)
        xt, x1, xn = sb("x", [P, 2, C]), sb("x1", [P, 2, C]), sb("xn", [P, C])
        stats, mv = sb("stats", [P, 2, 6]), sb("mv", [P, 2])
        std, rstd, newton = sb("std", [P, 1]), sb("rstd", [P, 1]), sb("newton", [P, 1])
        h = sb("h", [P, 2, C])
        h2T = sb("h2T", [P, KC, P])
        acc, turned, logits = pb("acc", [P, 2, C]), pb("turned", [P, KC, P]), pb("logits", [E, P])
        consts_loaded, w_hi_done, w_ready = sm("consts_loaded"), sm("w_hi_done"), sm("w_ready")
        w_loaded = [sm("w_loaded0"), sm("w_loaded1")]
        y_loaded, x_loaded = [sm("y_loaded0"), sm("y_loaded1")], [sm("x_loaded0"), sm("x_loaded1")]
        acc_ready, x1_ready, step, var_ready, std_ready, xn_ready, scaled, h_ready = (
            sm("acc_ready"), sm("x1_ready"), sm("step"), sm("var_ready"), sm("std_ready"), sm("xn_ready"), sm("scaled"), sm("h_ready"))
        turned_ready, h2T_ready, logits_ready, logits_kept = sm("turned_ready"), sm("h2T_ready"), sm("logits_ready"), sm("logits_kept")
        stored, kept, marks = [sm("stored0"), sm("stored1")], [sm("kept0"), sm("kept1")], sm("marks")
        block = ctx.enter_context(nc.Block())

        @block.sync
        def _(sp):
            sp.dma_start(ident[:, :], consts["ident"]).then_inc(consts_loaded, 16)
            sp.dma_start(gate_w[:, :, :], consts["gate_w"].rearrange("(k p) e -> p k e", p=P)).then_inc(consts_loaded, 16)
            for j, dst in ((2, ga), (3, shift_b), (4, scale_b)):
                sp.dma_start(dst[:, :], mod_rows[j * C:(j + 1) * C].rearrange("(a n) -> a n", a=1).broadcast_to([P, C])).then_inc(consts_loaded, 16)
            for k in range(KC):
                if k >= 2:
                    sp.wait_ge(w_ready, k - 1)
                sp.dma_start(w_raw[:, k % 2], w_proj[k * P:(k + 1) * P, :]).then_inc(w_loaded[k % 2], 16)
            with sp.Fori(0, NT // 2) as i:
                for b in range(2):
                    n = i * 2 + b
                    sp.wait_ge(acc_ready, n + 1)
                    for src, dst in zip(y_parts, (y_hi, y_lo)):
                        sp.dma_start(dst[:, b].bitcast(F32), src[:, :, ds(n * P, P)].rearrange("g p n -> p g n")).then_inc(y_loaded[b], 16)
                    sp.wait_ge(x1_ready, n + 1)
                    sp.dma_start(xt[:, b], x[ds(n * P, P), :]).then_inc(x_loaded[b], 16)

        @block.tensor
        def _(pe):
            pe.sem_inc(acc_ready, 2)
            pe.wait_ge(consts_loaded, 16 * 5)
            pe.wait_ge(w_ready, KC)

            def turn(n, b):
                pe.wait_ge(h_ready, n + 1)
                pe.wait_ge(h2T_ready, n + 1)
                for k in range(KC):
                    last = nc.tensor.transpose(turned[:, k], h[:, b, k * P:(k + 1) * P], ident[:, :])
                last.then_inc(turned_ready, 1)

            def gate(n):
                pe.wait_ge(h2T_ready, n + 2)
                pe.wait_ge(logits_kept, n + 1)
                for k in range(KC):
                    last = nc.tensor.matmul(logits[:, :], gate_w[:, k], h2T[:, k], start=(k == 0), stop=(k == KC - 1))
                last.then_inc(logits_ready, 1)

            def project(i, b):
                pe.wait_ge(y_loaded[b], i * 32 + 32)
                pe.wait_ge(x1_ready, i * 2 + b + 1)
                for o in range(2):
                    col = slice(o * CH, (o + 1) * CH)
                    last = product(nc, acc[:, b, col], lambda part, k: (y_hi, y_lo)[part][:, b, k],
                                   lambda part, k: (w_hi, w_lo)[part][:, k, col])
                last.then_inc(acc_ready, 1)

            with pe.Fori(0, NT // 2) as i:
                for b in range(2):
                    turn(i * 2 + b, b)
                    project(i, b)
                    gate(i * 2 + b)
            for n in range(NT, NT + LAG):
                turn(n, n % 2)
                gate(n)

        @block.scalar
        def _(act):
            nc.scalar.preload_act_table(ACT.Sqrt)
            act.sem_inc(h2T_ready, 1)
            act.sem_inc(logits_kept, 1)
            for k in range(KC):
                act.wait_ge(w_loaded[k % 2], 16 * (k // 2 + 1))
                nc.scalar.activation(w_hi[:, k], w_raw[:, k % 2], ACT.Copy).then_inc(w_hi_done, 1)

            def keep(n, col):
                act.wait_ge(turned_ready, n + 1)
                act.wait_ge(logits_ready, n + 1)
                nc.scalar.activation(h2T[:, :, :], turned[:, :, :], ACT.Copy).then_inc(h2T_ready, 1)
                act.wait_ge(logits_ready, n + 2)
                nc.scalar.activation(logitsT[:, col], logits[:, :], ACT.Copy).then_inc(logits_kept, 1)

            act.sem_inc(logits_ready, 1)
            with act.Fori(0, NT // 2) as i:
                for b in range(2):
                    keep(i * 2 + b, ds((i * 2 + b) * P, P))
                    act.wait_ge(var_ready, i * 2 + b + 1)
                    nc.scalar.activation(std[:, :], mv[:, 1:2], ACT.Sqrt).then_inc(std_ready, 1)
                    n = i * 2 + b
                    act.wait_ge(h_ready, n + LAG + 1)
                    act.dma_start(h2[:, ds(n)].rearrange("p a n -> p (a n)"), h[:, b]).then_inc(kept[b], 16)
                    act.dma_start(x1_d[ds(n * P, P), :], x1[:, b]).then_inc(stored[b], 16)
            for n in range(NT, NT + LAG):
                keep(n, slice(n * P, (n + 1) * P))
            for b in range(2):
                act.wait_ge(kept[b], 16 * (NT // 2 + 1))
                act.wait_ge(stored[b], 16 * (NT // 2 + 1))

        @block.vector
        def _(dve):
            dve.sem_inc(x1_ready, 2)
            for b in range(2):
                dve.sem_inc(stored[b], 16)
            for k in range(KC):
                dve.wait_ge(w_hi_done, k + 1)
                nc.vector.tensor_tensor(w_lo[:, k], w_raw[:, k % 2], w_hi[:, k], ALU.subtract).then_inc(w_ready, 1)
            dve.wait_ge(consts_loaded, 16 * 5)
            with dve.Fori(0, NT // 2) as i:
                s = Steps(dve, step, i * (2 * 9))
                for b in range(2):
                    n = i * 2 + b
                    dve.wait_ge(acc_ready, n + 3)
                    dve.wait_ge(stored[b], i * 16 + 16)
                    dve.wait_ge(xn_ready, n + 1)
                    s.link(nc.vector.tensor_tensor(x1[:, b], acc[:, b], ga[:, :], ALU.mult))
                    dve.wait_ge(x_loaded[b], i * 16 + 16)
                    s.link(nc.vector.tensor_tensor(x1[:, b], x1[:, b], xt[:, b], ALU.add))
                    dve.sem_inc(x1_ready, 1)
                    nc.vector.bn_stats(stats[:, 0], x1[:, b, 0:CH])
                    s.link(nc.vector.bn_stats(stats[:, 1], x1[:, b, CH:C]))
                    dve.sem_inc(marks, 1)
                    s.link(nc.vector.bn_aggr(mv[:, :], stats[:, :, :].rearrange("p a b -> p (a b)")))
                    nc.vector.tensor_scalar(mv[:, 1:2], mv[:, 1:2], EPS, None, ALU.add).then_inc(var_ready, 1)
                    dve.wait_ge(std_ready, n + 1)
                    s.link(nc.vector.reciprocal(rstd[:, :], std[:, :]))
                    s.link(nc.vector.tensor_tensor(newton[:, :], rstd[:, :], rstd[:, :], ALU.mult))
                    s.link(nc.vector.tensor_tensor(newton[:, :], newton[:, :], mv[:, 1:2], ALU.mult))
                    s.link(nc.vector.tensor_scalar(newton[:, :], newton[:, :], -0.5, 1.5, ALU.mult, ALU.add))
                    s.link(nc.vector.tensor_tensor(rstd[:, :], rstd[:, :], newton[:, :], ALU.mult))
                    dve.wait_ge(scaled, n + 1)
                    nc.vector.tensor_scalar(xn[:, :], x1[:, b], mv[:, 0:1], rstd[:, 0:1], ALU.subtract, ALU.mult).then_inc(xn_ready, 1)

        @block.gpsimd
        def _(pool):
            pool.sem_inc(scaled, 1)
            pool.sem_inc(xn_ready, 1)
            nc.gpsimd.memset(h[:, :, :], 0.0).then_inc(h_ready, LAG)
            for b in range(2):
                pool.sem_inc(kept[b], 16)
            pool.wait_ge(consts_loaded, 16 * 5)
            with pool.Fori(0, NT // 2) as i:
                for b in range(2):
                    n = i * 2 + b
                    pool.wait_ge(turned_ready, n + 1)
                    pool.wait_ge(kept[b], i * 16 + 16)
                    pool.wait_ge(xn_ready, n + 2)
                    nc.gpsimd.tensor_tensor(h[:, b], xn[:, :], scale_b[:, :], ALU.mult).then_inc(scaled, 1)
                    pool.wait_ge(scaled, n + 2)
                    nc.gpsimd.tensor_tensor(h[:, b], h[:, b], shift_b[:, :], ALU.add).then_inc(h_ready, 1)


def route(nc, sem, consts, h2, logitsT, slots, weights, bounds, rows_d):
    NTH = T // MROWS - 1
    with ExitStack() as ctx:
        sb = lambda name, shape, dt=F32: ctx.enter_context(nc.sbuf_tensor(f"r_{name}", shape, dt))
        pb = lambda name, shape: ctx.enter_context(nc.psum_tensor(f"r_{name}_psum", shape, F32))
        sm = lambda name: sem(f"r_{name}")
        ident, before, ones = sb("ident", [P, P]), sb("before", [P, P]), sb("ones", [P, P])
        numbers, limits = sb("numbers", [P, E]), sb("limits", [P, NTH])
        logits, best, index = sb("logits", [P, NT, E]), sb("best", [P, NT, 8]), sb("index", [P, NT, 8], U32)
        indexf = sb("indexf", [P, NT, 8])
        first, second, both = sb("first", [P, NT, E]), sb("second", [P, NT, E]), sb("both", [P, NT, E])
        gap, denom = sb("gap", [P, NT]), sb("denom", [P, NT])
        ahead, over = sb("ahead", [P, NT + 1, E]), sb("over", [P, E, NTH])
        macros, start = sb("macros", [P, E]), sb("start", [P, E + 1])
        row, picked, slotf = sb("row", [P, NT, E]), sb("picked", [P, NT, E]), sb("slotf", [P, 2, NT])
        p_logits, p_rank, p_count = pb("logits", [P, CH]), pb("rank", [P, CH]), pb("count", [P, CH])
        consts_loaded, turned_ready, both_ready, ranks_ready = sm("consts_loaded"), sm("turned_ready"), sm("both_ready"), sm("ranks_ready")
        step, gap_ready, exp_done, slots_ready, scattered = sm("step"), sm("gap_ready"), sm("exp_done"), sm("slots_ready"), sm("scattered")
        block = ctx.enter_context(nc.Block())

        @block.sync
        def _(sp):
            for dst, name in ((ident[:, :], "ident"), (before[:, :], "before"), (numbers[:, :], "numbers"), (limits[:, :], "limits")):
                sp.dma_start(dst, consts[name]).then_inc(consts_loaded, 16)

        @block.tensor
        def _(pe):
            pe.wait_ge(consts_loaded, 64)
            for i in range(NT):
                last = nc.tensor.transpose(p_logits[:, i * E:(i + 1) * E], logitsT[:, (i + LAG) * P:(i + LAG + 1) * P], ident[0:E, 0:E])
            last.then_inc(turned_ready, 1)
            pe.wait_ge(both_ready, 1)
            m = both[:, :, :].rearrange("p i e -> p (i e)")
            nc.tensor.matmul(p_rank[:, 0:P], before[:, :], m, start=True, stop=True)
            nc.tensor.matmul(p_count[:, 0:P], ones[:, :], m, start=True, stop=True).then_inc(ranks_ready, 1)

        @block.scalar
        def _(act):
            nc.scalar.preload_act_table(ACT.Exp)
            act.wait_ge(gap_ready, 1)
            nc.scalar.activation(gap[:, :], gap[:, :], ACT.Exp).then_inc(exp_done, 1)

        @block.vector
        def _(dve):
            s = Steps(dve, step)
            wide = lambda ap, shape: ap.broadcast_to(shape)
            s.link(nc.vector.memset(ones[:, :], 1.0))
            s.link(nc.vector.memset(ahead[:, 0], 0.0))
            s.link(nc.vector.memset(start[:, 0:1], 0.0))
            dve.wait_ge(consts_loaded, 64)
            dve.wait_ge(turned_ready, 1)
            s.link(nc.vector.tensor_copy(logits[:, :, :].rearrange("p i e -> p (i e)"), p_logits[:, 0:NT * E]))
            for i in range(NT):
                last = nc.vector.max(best[:, i], logits[:, i])
            s.link(last)
            for i in range(NT):
                last = nc.vector.max_index(index[:, i], best[:, i], logits[:, i])
            s.link(last)
            s.link(nc.vector.tensor_copy(indexf[:, :, :], index[:, :, :]))
            numbers_w = wide(numbers[:, :].rearrange("p (a e) -> p a e", a=1), [P, NT, E])
            for c, mask in ((0, first), (1, second)):
                s.link(nc.vector.tensor_tensor(mask[:, :, :], wide(indexf[:, :, c:c + 1], [P, NT, E]), numbers_w, ALU.is_equal))
            nc.vector.tensor_tensor(both[:, :, :], first[:, :, :], second[:, :, :], ALU.add).then_inc(both_ready, 1)
            nc.vector.tensor_tensor(gap[:, :], best[:, :, 1], best[:, :, 0], ALU.subtract).then_inc(gap_ready, 1)
            dve.wait_ge(exp_done, 1)
            s.link(nc.vector.tensor_scalar(denom[:, :], gap[:, :], 1.0, None, ALU.add))
            s.link(nc.vector.reciprocal(weights[:, 0], denom[:, :]))
            s.link(nc.vector.tensor_tensor(weights[:, 1], gap[:, :], weights[:, 0], ALU.mult))
            dve.wait_ge(ranks_ready, 1)
            for i in range(NT):
                s.link(nc.vector.tensor_tensor(ahead[:, i + 1], p_count[:, i * E:(i + 1) * E], ahead[:, i], ALU.add))
            s.link(nc.vector.tensor_tensor(over[:, :, :], wide(ahead[:, NT].rearrange("p (e a) -> p e a", a=1), [P, E, NTH]),
                                           wide(limits[:, :].rearrange("p (a l) -> p a l", a=1), [P, E, NTH]), ALU.is_gt))
            s.link(nc.vector.tensor_reduce(macros[:, :], over[:, :, :], AX.X, ALU.add))
            s.link(nc.vector.tensor_scalar(macros[:, :], macros[:, :], 1.0, None, ALU.add))
            for e in range(E):
                s.link(nc.vector.tensor_tensor(start[:, e + 1:e + 2], start[:, e:e + 1], macros[:, e:e + 1], ALU.add))
            s.link(nc.vector.tensor_copy(bounds[:, :], start[0:1, :]))
            s.link(nc.vector.tensor_tensor(row[:, :, :].rearrange("p i e -> p (i e)"), p_rank[:, 0:P],
                                           ahead[:, 0:NT].rearrange("p i e -> p (i e)"), ALU.add))
            s.link(nc.vector.tensor_scalar(macros[:, :], start[:, 0:E], float(MROWS), None, ALU.mult))
            s.link(nc.vector.tensor_tensor(row[:, :, :], row[:, :, :], wide(macros[:, :].rearrange("p (a e) -> p a e", a=1), [P, NT, E]), ALU.add))
            for c, mask in ((0, first), (1, second)):
                s.link(nc.vector.tensor_tensor(picked[:, :, :], mask[:, :, :], row[:, :, :], ALU.mult))
                s.link(nc.vector.tensor_reduce(slotf[:, c], picked[:, :, :], AX.X, ALU.add))
            nc.vector.tensor_copy(slots[:, :, :], slotf[:, :, :]).then_inc(slots_ready, 1)

        @block.gpsimd
        def _(pool):
            pool.wait_ge(slots_ready, 1)
            for i in range(NT):
                for c in range(2):
                    nc.gpsimd.indirect_dma_start(rows_d, bass.IndirectOffsetOnAxis(ap=slots[:, c, i:i + 1], axis=0),
                                                 h2[:, i], None).then_inc(scattered, 16)
            pool.wait_ge(scattered, 16 * 2 * NT)


def experts(nc, sem, consts, mod_rows, expert_w, bounds, rows_d):
    RAWS = 4
    with ExitStack() as ctx:
        sb = lambda name, shape, dt=F32: ctx.enter_context(nc.sbuf_tensor(f"e_{name}", shape, dt))
        pb = lambda name, shape: ctx.enter_context(nc.psum_tensor(f"e_{name}_psum", shape, F32))
        sm = lambda name: sem(f"e_{name}")
        ident, gb = sb("ident", [P, P]), sb("gb", [P, C])
        w_raw = sb("w_raw", [P, RAWS, C])
        w_hi = [sb(f"w_hi{b}", [P, KC, C], F32R) for b in range(2)]
        w_lo = [sb(f"w_lo{b}", [P, KC, C], F32R) for b in range(2)]
        xt = sb("x", [P, MT, C])
        x_hi, x_lo = sb("x_hi", [P, MT, KC, P], F32R), sb("x_lo", [P, MT, KC, P], F32R)
        y = sb("y", [P, MT, C])
        turned, acc = pb("turned", [P, C]), pb("acc", [P, MT, C])
        consts_loaded = sm("consts_loaded")
        w_loaded, w_hi_done, w_ready, w_free = [sm(f"w_loaded{r}") for r in range(RAWS)], sm("w_hi_done"), sm("w_ready"), sm("w_free")
        x_loaded, turned_ready, x_hi_done, x_ready = [sm(f"x_loaded{s}") for s in range(MT)], sm("turned_ready"), sm("x_hi_done"), sm("x_ready")
        acc_ready, y_ready, stored, marks = sm("acc_ready"), sm("y_ready"), [sm(f"stored{s}") for s in range(MT)], sm("marks")
        block = ctx.enter_context(nc.Block())

        def bound(eng, e):
            return eng.value_load(bounds[0:1, e:e + 1], min_val=0, max_val=MAX_MACRO) if isinstance(e, int) else eng.value_load(bounds[0:1, ds(e)], min_val=0, max_val=MAX_MACRO)

        @block.sync
        def _(sp):
            sp.dma_start(ident[:, :], consts["ident"]).then_inc(consts_loaded, 16)
            sp.dma_start(gb[:, :], mod_rows[5 * C:6 * C].rearrange("(a n) -> a n", a=1).broadcast_to([P, C])).then_inc(consts_loaded, 16)
            for s in range(MT):
                sp.dma_start(xt[:, s], rows_d[s * P:(s + 1) * P, :]).then_inc(x_loaded[s], 16)
            total = bound(sp, E)
            with sp.Fori(0, total) as g:
                for s in range(MT):
                    sp.wait_ge(turned_ready, g * MT + s + 2)
                    sp.dma_start(xt[:, s], rows_d[ds((g * MT + (s + MT)) * P, P), :]).then_inc(x_loaded[s], 16)
            for s in range(MT):
                sp.wait_ge(x_loaded[s], total * 16 + 16)
            sp.sem_inc(marks, 1)

        @block.gpsimd
        def _(pool):
            def load(e, c):
                src = expert_w[ds(e), c * P:(c + 1) * P, :].rearrange("a p n -> (a p) n")
                pool.dma_start(w_raw[:, c % RAWS], src).then_inc(w_loaded[c % RAWS], 16)

            def load_ahead(e, c):
                pool.wait_ge(w_ready, e * KC + c + 1)
                ahead = c + RAWS
                if ahead < KC:
                    load(e, ahead)
                elif not (isinstance(e, int) and e == E - 1):
                    load(e + 1, ahead - KC)

            def split(e, b):
                pool.wait_ge(w_free, e + 1)
                for c in range(KC):
                    pool.wait_ge(w_loaded[c % RAWS], e * (16 * KC // RAWS) + 16 * (c // RAWS + 1))
                    pool.sem_inc(marks, 1)
                    nc.gpsimd.tensor_copy(w_hi[b][:, c], w_raw[:, c % RAWS]).then_inc(w_hi_done, 1)
                    pool.wait_ge(w_hi_done, e * KC + c + 1)
                    nc.gpsimd.tensor_tensor(w_lo[b][:, c], w_raw[:, c % RAWS], w_hi[b][:, c], ALU.subtract).then_inc(w_ready, 1)
                    load_ahead(e, c)

            for c in range(RAWS):
                load(0, c)
            for c in range(KC):
                load_ahead(0, c)
            with pool.Fori(0, E // 2 - 1) as j:
                for b in range(2):
                    split(j * 2 + (b + 1), 1 - b)
            split(E - 1, 1)

        @block.tensor
        def _(pe):
            pe.sem_inc(w_free, 2)
            pe.sem_inc(turned_ready, 1)
            pe.sem_inc(acc_ready, 1)
            pe.wait_ge(consts_loaded, 32)

            def turn(n, s, loads):
                pe.wait_ge(x_loaded[s], loads)
                pe.wait_ge(x_ready, n + 1)
                for k in range(KC):
                    last = nc.tensor.transpose(turned[:, k * P:(k + 1) * P], xt[:, s, k * P:(k + 1) * P], ident[:, :])
                last.then_inc(turned_ready, 1)

            turn(0, 0, 16)
            with pe.Fori(0, E // 2) as j:
                for b in range(2):
                    lo, hi = bound(pe, j * 2 + b), bound(pe, j * 2 + (b + 1))
                    pe.wait_ge(w_ready, (j * 2 + b) * KC + KC)
                    pe.sem_inc(marks, 1)
                    with pe.Fori(lo, hi) as g:
                        for s in range(MT):
                            turn(g * MT + (s + 1), (s + 1) % MT, g * 16 + 16 * (1 + s))
                            pe.wait_ge(x_ready, g * MT + s + 2)
                            pe.wait_ge(y_ready, g * MT + s + 1)
                            for o in range(2):
                                col = slice(o * CH, (o + 1) * CH)
                                last = product(nc, acc[:, s, col], lambda part, k: (x_hi, x_lo)[part][:, s, k],
                                               lambda part, k: (w_hi, w_lo)[part][b][:, k, col])
                            last.then_inc(acc_ready, 1)
                    pe.wait_ge(acc_ready, hi * MT + 1)
                    pe.sem_inc(w_free, 1)

        @block.scalar
        def _(act):
            nc.scalar.preload_act_table(ACT.Exp)
            total = bound(act, E)
            for c in range(KC):
                act.wait_ge(w_loaded[c % RAWS], 16 * (c // RAWS + 1))
                nc.scalar.activation(w_hi[0][:, c], w_raw[:, c % RAWS], ACT.Copy).then_inc(w_hi_done, 1)
            act.wait_ge(turned_ready, 2)
            nc.scalar.activation(x_hi[:, 0].rearrange("p k n -> p (k n)"), turned[:, :], ACT.Copy).then_inc(x_hi_done, 1)
            with act.Fori(0, total) as g:
                for s in range(MT):
                    act.wait_ge(turned_ready, g * MT + s + 3)
                    act.wait_ge(acc_ready, g * MT + s + 1)
                    nc.scalar.activation(x_hi[:, (s + 1) % MT].rearrange("p k n -> p (k n)"), turned[:, :], ACT.Copy).then_inc(x_hi_done, 1)
                    act.wait_ge(y_ready, g * MT + s + 3)
                    act.dma_start(rows_d[ds((g * MT + s) * P, P), :], y[:, s]).then_inc(stored[s], 16)
            for s in range(MT):
                act.wait_ge(stored[s], total * 16 + 16)
            act.sem_inc(marks, 1)

        @block.vector
        def _(dve):
            dve.sem_inc(x_ready, 1)
            dve.sem_inc(y_ready, 2)
            for s in range(MT):
                dve.sem_inc(stored[s], 16)
            dve.wait_ge(consts_loaded, 32)
            total = bound(dve, E)
            for c in range(KC):
                dve.wait_ge(w_hi_done, c + 1)
                nc.vector.tensor_tensor(w_lo[0][:, c], w_raw[:, c % RAWS], w_hi[0][:, c], ALU.subtract).then_inc(w_ready, 1)

            def split(n, s):
                dve.wait_ge(x_hi_done, n + 1)
                nc.vector.tensor_tensor(x_lo[:, s].rearrange("p k n -> p (k n)"), turned[:, :],
                                        x_hi[:, s].rearrange("p k n -> p (k n)"), ALU.subtract).then_inc(x_ready, 1)

            split(0, 0)
            with dve.Fori(0, total) as g:
                for s in range(MT):
                    split(g * MT + (s + 1), (s + 1) % MT)
                    dve.wait_ge(acc_ready, g * MT + s + 2)
                    dve.wait_ge(stored[s], g * 16 + 16)
                    nc.vector.tensor_tensor(y[:, s], acc[:, s], gb[:, :], ALU.mult).then_inc(y_ready, 1)


def combine(nc, sem, slots, weights, out_rows_d, x1_d, out):
    with ExitStack() as ctx:
        sb = lambda name, shape, dt=F32: ctx.enter_context(nc.sbuf_tensor(f"c_{name}", shape, dt))
        sm = lambda name: sem(f"c_{name}")
        B = 4
        rows, x1, res = sb("rows", [P, B, 2, C]), sb("x1", [P, B, C]), sb("res", [P, B, C])
        gathered, x1_loaded = [sm(f"gathered{b}") for b in range(B)], [sm(f"x1_loaded{b}") for b in range(B)]
        half, done, stored = sm("half"), sm("done"), [sm(f"stored{b}") for b in range(B)]
        block = ctx.enter_context(nc.Block())

        @block.gpsimd
        def _(pool):
            for i in range(NT):
                b = i % B
                if i >= B:
                    pool.wait_ge(done, i - B + 1)
                for c in range(2):
                    nc.gpsimd.indirect_dma_start(rows[:, b, c], None, out_rows_d,
                                                 bass.IndirectOffsetOnAxis(ap=slots[:, c, i:i + 1], axis=0)).then_inc(gathered[b], 16)

        @block.sync
        def _(sp):
            for i in range(NT + 2):
                if i < NT:
                    if i >= B:
                        sp.wait_ge(done, i - B + 1)
                    sp.dma_start(x1[:, i % B], x1_d[i * P:(i + 1) * P, :]).then_inc(x1_loaded[i % B], 16)
                if i >= 2:
                    n = i - 2
                    sp.wait_ge(done, n + 1)
                    sp.dma_start(out[n * P:(n + 1) * P, :], res[:, n % B]).then_inc(stored[n % B], 16)
            for b in range(B):
                sp.wait_ge(stored[b], 16 * (NT // B))

        @block.vector
        def _(dve):
            for i in range(NT):
                b = i % B
                dve.wait_ge(gathered[b], 32 * (i // B + 1))
                dve.wait_ge(x1_loaded[b], 16 * (i // B + 1))
                if i >= B:
                    dve.wait_ge(stored[b], 16 * (i // B))
                nc.vector.scalar_tensor_tensor(out=res[:, b], in0=rows[:, b, 0], scalar=weights[:, 0, i:i + 1], in1=x1[:, b],
                                               op0=ALU.mult, op1=ALU.add).then_inc(half, 1)
                dve.wait_ge(half, i + 1)
                nc.vector.scalar_tensor_tensor(out=res[:, b], in0=rows[:, b, 1], scalar=weights[:, 1, i:i + 1], in1=res[:, b],
                                               op0=ALU.mult, op1=ALU.add).then_inc(done, 1)


@contextmanager
def semaphores(nc):
    taken = []

    def sem(name):
        taken.append(nc.alloc_semaphore(name=name))
        return taken[-1]

    yield sem
    nc.clear_and_free_semaphores(taken)
    nc.all_engine_barrier()


def adaln_block(nc, x, w_attn, w_proj, adapter, gating, gate_w, expert_w, c, wmod, consts, out):
    def scratch(name, shape):
        return nc.dram_tensor(f"scratch_{name}", shape, F32).ap()

    mod_rows = scratch("mod_rows", [6 * C])
    q_hi, q_lo, k_hi, k_lo = (scratch(n, [G, P, T]) for n in ("q_hi", "q_lo", "k_hi", "k_lo"))
    v, a_y = scratch("v", [G, P, NT, P]), scratch("a_y", [G, P, T])
    y_hi, y_lo = scratch("y_hi", [G, P, T]), scratch("y_lo", [G, P, T])
    x1 = scratch("x1", [T, C])
    rows = scratch("rows", [(MAX_MACRO + 1) * MROWS, C])
    consts = dict(consts, adapter=adapter, gating=gating, gate_w=gate_w)
    with ExitStack() as ctx:
        with semaphores(nc) as sem:
            modulation(nc, sem, c, wmod, mod_rows)
        with semaphores(nc) as sem, ExitStack() as stage:
            ak = stage.enter_context(nc.sbuf_tensor("ak", [P, G, P], F32))
            av = stage.enter_context(nc.sbuf_tensor("av", [P, G, P], F32))
            with ExitStack() as inner:
                hT = [inner.enter_context(nc.sbuf_tensor(n, [P, KC, T], F32R)) for n in ("hT_hi", "hT_lo")]
                norm_in(nc, sem, x, mod_rows, consts["ident"], *hT)
                project(nc, sem, "k", w_attn, G, hT, consts, ak, (k_hi, k_lo))
                project(nc, sem, "v", w_attn, 2 * G, hT, consts, av, (v,), rows)
                project(nc, sem, "q", w_attn, 0, hT, consts, None, (q_hi, q_lo))
            adapter_attention(nc, sem, consts, ak, av, q_hi, q_lo, a_y)
        with semaphores(nc) as sem:
            attention(nc, sem, consts, (q_hi, q_lo), (k_hi, k_lo), v, a_y, (y_hi, y_lo))
        slots = ctx.enter_context(nc.sbuf_tensor("slots", [P, 2, NT], I32))
        weights = ctx.enter_context(nc.sbuf_tensor("weights", [P, 2, NT], F32))
        bounds = ctx.enter_context(nc.sbuf_tensor("bounds", [1, E + 1], I32))
        with semaphores(nc) as sem, ExitStack() as stage:
            h2 = stage.enter_context(nc.sbuf_tensor("h2", [P, NT, C], F32))
            logitsT = stage.enter_context(nc.sbuf_tensor("logitsT", [E, (NT + LAG) * P], F32))
            proj_out(nc, sem, consts, mod_rows, w_proj, (y_hi, y_lo), x, x1, h2, logitsT)
            route(nc, sem, consts, h2, logitsT, slots, weights, bounds, rows)
        with semaphores(nc) as sem:
            experts(nc, sem, consts, mod_rows, expert_w, bounds, rows)
            combine(nc, sem, slots, weights, rows, x1, out)


def _constants():
    import numpy as np

    theta = np.float32(1.0) / np.float32(10000.0) ** (np.arange(0, D, 2, dtype=np.float32) / np.float32(D))
    angle = np.outer(np.arange(T, dtype=np.float32), theta.astype(np.float32)).astype(np.float32)
    d = np.arange(P) % D
    sign = np.where(d < D // 2, np.float32(-1), np.float32(1))[:, None]
    p = np.arange(P)
    causal = np.zeros((P, CH), np.float32)
    causal[:, CH - P:] = np.where(p[None, :] > p[:, None], np.float32(MASKED), np.float32(0))
    return {
        "ident": np.eye(P, dtype=np.float32),
        "block_mask": np.kron(np.eye(HG, dtype=np.float32), np.ones((D, D), np.float32)),
        "cos": np.ascontiguousarray(np.cos(angle).astype(np.float32).T[d % (D // 2)]),
        "sin": np.ascontiguousarray(np.sin(angle).astype(np.float32).T[d % (D // 2)] * sign),
        "causal": causal,
        "after": np.where(p[:, None] > p[None, :], np.float32(-1e30), np.float32(0)),
        "before": np.ascontiguousarray((p[:, None] < p[None, :]).astype(np.float32)),
        "numbers": np.tile(np.arange(E, dtype=np.float32), (P, 1)),
        "limits": np.tile(np.arange(1, T // MROWS, dtype=np.float32) * MROWS, (P, 1)),
    }


def kernel(**inputs):
    import numpy as np
    import concourse.bacc as bacc
    from concourse.bass_utils import run_bass_kernel_spmd

    a = {k: np.asarray(v) for k, v in inputs.items()}
    lay = {
        "x": a["L0_attn_x"].reshape(T, C),
        "w_attn": a["L0_attn_w_attn"].reshape(3 * G, P, KC, P).transpose(0, 3, 2, 1).reshape(3 * G, P, C),
        "w_proj": a["L0_attn_w_proj"].T,
        "adapter": a["L0_attn_adapter_wte"].T.reshape(KC, P, A).transpose(1, 0, 2),
        "gating": a["L0_attn_gating"],
        "gate_w": a["L0_ffn_gate_w"],
        "expert_w": a["L0_ffn_expert_w"],
        "c": a["L0_c"].reshape(KC, P).T,
        "wmod": a["L0_wmod"],
    }
    nc = bacc.Bacc("TRN2", target_bir_lowering=False, num_devices=1)
    arrays, aps = {}, {}
    for name, value in {**lay, **_constants()}.items():
        arrays[f"in_{name}"] = np.ascontiguousarray(value)
        aps[name] = nc.dram_tensor(f"in_{name}", list(value.shape), F32, kind="ExternalInput").ap()
    out = nc.dram_tensor("out", [T, C], F32, kind="ExternalOutput").ap()
    adaln_block(nc, *(aps[name] for name in lay), {name: aps[name] for name in _constants()}, out)
    r = run_bass_kernel_spmd(nc, [arrays], core_ids=[0])
    return r.results[0]["out"].reshape(1, T, C)
```

```python
import math
from contextlib import ExitStack, contextmanager

import concourse.bass as bass
from concourse import mybir

ALU = mybir.AluOpType
ACT = mybir.ActivationFunctionType
AX = mybir.AxisListType
F32 = mybir.dt.float32
F32R = mybir.dt.float32r
I32 = mybir.dt.int32
U32 = mybir.dt.uint32

P = 128
T, C = 2048, 1024
H, D = 32, 32
E = 8
A = 10
CH = 512
KC = C // P
NT = T // P
NQ = T // CH
TPC = CH // P
HG = P // D
G = H // HG
EPS = 1e-5


def ds(i, n=1):
    return bass.ds(i, n)


class Steps:

    def __init__(self, eng, sem, base=0):
        self.eng, self.sem, self.base, self.n = eng, sem, base, 0

    def link(self, ins):
        self.n += 1
        ins.then_inc(self.sem, 1)
        self.eng.wait_ge(self.sem, self.base + self.n)


def modulated_norm(nc, sem, x, c, wmod, identity, raw_d, mod_rows, hT_hi, hT_lo):
    VC = C // CH
    NORM_STEPS = 2 * TPC + 6
    with ExitStack() as ctx:
        sb = lambda name, shape, dt=F32: ctx.enter_context(nc.sbuf_tensor(f"n_{name}", shape, dt))
        sm = lambda name: sem(f"n_{name}")
        c_col, c_sig, silu = sb("c_col", [P, KC]), sb("c_sig", [P, KC]), sb("silu", [P, KC])
        wbuf = sb("wmod", [P, 2, KC, CH])
        rows = sb("rows", [KC, 8, P])
        row = [rows[0:1, b * TPC:(b + 1) * TPC].rearrange("a n p -> a (n p)") for b in range(2)]
        vectors, gate_sign, gate_size = rows[:, 0:6], rows[:, 6], rows[:, 7]
        shift_c, scale_c = sb("shift", [P, KC]), sb("scale", [P, KC])
        first_two = sb("first_two", [KC, 2, P])
        ident = sb("ident", [P, P])
        xt = sb("x", [P, 2, TPC, C])
        stats, mv = sb("stats", [P, TPC, 2, 6]), sb("mv", [P, TPC, 2])
        std, rstd, newton = sb("std", [P, TPC]), sb("rstd", [P, TPC]), sb("newton", [P, TPC])
        BANKS = 4
        turned = ctx.enter_context(nc.psum_tensor("n_turned", [P, BANKS, CH], F32))
        acc = ctx.enter_context(nc.psum_tensor("n_acc", [1, 2, CH], F32))
        columns = ctx.enter_context(nc.psum_tensor("n_columns", [P, 2, KC], F32))
        c_loaded, sig_ready, silu_step, silu_ready = sm("c_loaded"), sm("sig_ready"), sm("silu_step"), sm("silu_ready")
        w_loaded, acc_ready, row_ready = [sm("w_loaded0"), sm("w_loaded1")], sm("acc_ready"), sm("row_ready")
        row_stored = [sm("row_stored0"), sm("row_stored1")]
        first_loaded, columns_turned, columns_taken = sm("first_loaded"), sm("columns_turned"), sm("columns_taken")
        columns_ready, ident_loaded = sm("columns_ready"), sm("ident_loaded")
        x_loaded = [sm("x_loaded0"), sm("x_loaded1")]
        stat_step, var_ready, std_ready, xn_ready, stats_in = sm("stat_step"), sm("var_ready"), sm("std_ready"), sm("xn_ready"), sm("stats_in")
        bank_ready, h_ready, hi_done, lo_done = sm("bank_ready"), sm("h_ready"), sm("hi_done"), sm("lo_done")
        vectors_loaded, vector_step, vectors_ready, vectors_stored = sm("vectors_loaded"), sm("vector_step"), sm("vectors_ready"), sm("vectors_stored")
        w_view = wmod.rearrange("(k p) (n j) -> n p k j", p=P, j=CH)
        block = ctx.enter_context(nc.Block())

        def load_x(eng, q, g):
            for j in range(TPC):
                eng.dma_start(xt[:, g, j], x[ds((q * TPC + j) * P, P), :]).then_inc(x_loaded[g], 16)

        @block.sync
        def _(sp):
            sp.dma_start(c_col[:, :], c).then_inc(c_loaded, 16)

            def load_w(n, b):
                sp.wait_ge(acc_ready, n + 1)
                sp.dma_start(wbuf[:, b], w_view[ds(n)].rearrange("a p k j -> (a p) k j")).then_inc(w_loaded[b], 16)

            for n in range(2 * VC):
                load_w(n, n % 2)
                if n == 0:
                    sp.dma_start(ident[:, :], identity).then_inc(ident_loaded, 16)
                    load_x(sp, 0, 0)
            with sp.Fori(0, NQ // 2) as i:
                for g in range(2):
                    for b in range(2):
                        load_w((i * 2 + g) * 2 + (2 * VC + b), b)
            for g in range(2):
                sp.wait_ge(x_loaded[g], 16 * TPC * (NQ // 2 + (g == 0)))

        @block.scalar
        def _(act):
            nc.scalar.preload_act_table(ACT.Exp)
            act.wait_ge(c_loaded, 16)
            nc.scalar.activation(c_sig[:, :], c_col[:, :], ACT.Exp, scale=-1.0).then_inc(sig_ready, 1)

            def store(n, b):
                act.wait_ge(row_ready, n + 3)
                act.dma_start(raw_d[ds(n * CH, CH)].rearrange("(a n) -> a n", a=1), row[b]).then_inc(row_stored[b], 16)

            for n in range(2 * VC):
                store(n, n % 2)
            for b in range(2):
                act.wait_ge(row_stored[b], 16 * (VC + 1))
            act.dma_start(first_two[:, :, :], raw_d[0:2 * C].rearrange("(v k p) -> k v p", p=P, k=KC)).then_inc(first_loaded, 16)
            act.wait_ge(columns_turned, 1)
            nc.scalar.activation(shift_c[:, :], columns[:, 0], ACT.Copy).then_inc(columns_taken, 1)
            nc.scalar.activation(scale_c[:, :], columns[:, 1], ACT.Copy).then_inc(columns_taken, 1)
            nc.scalar.preload_act_table(ACT.Sqrt)
            with act.Fori(0, NQ // 2) as i:
                for g in range(2):
                    q = i * 2 + g
                    act.wait_ge(bank_ready, q * KC + 1)
                    load_x(act, (q + 1) % NQ, 1 - g)
                    act.wait_ge(var_ready, q + 1)
                    nc.scalar.activation(std[:, :], mv[:, :, 1], ACT.Sqrt).then_inc(std_ready, 1)
                    for b in range(2):
                        store(q * 2 + (2 * VC + b), b)
                    for k in range(KC):
                        act.wait_ge(h_ready, q * KC + k + 1 + BANKS)
                        col = ds(q * CH, CH)
                        nc.scalar.activation(hT_hi[:, k, col], hT_lo[:, k, col].bitcast(F32), ACT.Copy).then_inc(hi_done, 1)
            for b in range(2):
                act.wait_ge(row_stored[b], 16 * (3 * VC + 1))
            act.dma_start(vectors, raw_d.rearrange("(v k p) -> k v p", p=P, k=KC)).then_inc(vectors_loaded, 16)
            act.wait_ge(vectors_ready, 1)
            act.dma_start(mod_rows.rearrange("(v k p) -> k v p", p=P, k=KC), vectors).then_inc(vectors_stored, 16)
            act.wait_ge(vectors_stored, 16)

        @block.vector
        def _(dve):
            dve.sem_inc(acc_ready, 2)
            dve.sem_inc(row_ready, 2)
            dve.sem_inc(h_ready, BANKS)
            dve.sem_inc(bank_ready, 1)
            for b in range(2):
                dve.sem_inc(row_stored[b], 16)
            dve.wait_ge(sig_ready, 1)
            s = Steps(dve, silu_step)
            s.link(nc.vector.tensor_scalar(silu[:, :], c_sig[:, :], 1.0, None, ALU.add))
            s.link(nc.vector.reciprocal(c_sig[:, :], silu[:, :]))
            nc.vector.tensor_tensor(silu[:, :], c_col[:, :], c_sig[:, :], ALU.mult).then_inc(silu_ready, 1)

            def take_row(n, half, b):
                dve.wait_ge(acc_ready, n + 3)
                dve.wait_ge(row_stored[b], half * 16 + 16)
                nc.vector.tensor_copy(row[b], acc[:, b]).then_inc(row_ready, 1)

            def normalise(q, g, half):
                s = Steps(dve, stat_step, q * NORM_STEPS)
                dve.wait_ge(x_loaded[g], half * (16 * TPC) + 16 * TPC)
                for j in range(TPC):
                    nc.vector.bn_stats(stats[:, j, 0], xt[:, g, j, 0:CH])
                    s.link(nc.vector.bn_stats(stats[:, j, 1], xt[:, g, j, CH:C]))
                    dve.sem_inc(stats_in, 1)
                    s.link(nc.vector.bn_aggr(mv[:, j], stats[:, j].rearrange("p a b -> p (a b)")))
                s.link(nc.vector.tensor_scalar(mv[:, :, 1], mv[:, :, 1], EPS, None, ALU.add))
                dve.sem_inc(var_ready, 1)
                dve.wait_ge(std_ready, q + 1)
                s.link(nc.vector.reciprocal(rstd[:, :], std[:, :]))
                s.link(nc.vector.tensor_tensor(newton[:, :], rstd[:, :], rstd[:, :], ALU.mult))
                s.link(nc.vector.tensor_tensor(newton[:, :], newton[:, :], mv[:, :, 1], ALU.mult))
                s.link(nc.vector.tensor_scalar(newton[:, :], newton[:, :], -0.5, 1.5, ALU.mult, ALU.add))
                s.link(nc.vector.tensor_tensor(rstd[:, :], rstd[:, :], newton[:, :], ALU.mult))
                for j in range(TPC):
                    nc.vector.tensor_scalar(xt[:, g, j], xt[:, g, j], mv[:, j, 0:1], rstd[:, j:j + 1], ALU.subtract, ALU.mult).then_inc(xn_ready, 1)

            for n in range(2 * VC):
                take_row(n, n // 2, n % 2)
            with dve.Fori(0, NQ // 2) as i:
                for g in range(2):
                    q = i * 2 + g
                    normalise(q, g, i)
                    for b in range(2):
                        take_row(q * 2 + (2 * VC + b), q + VC, b)
                    for k in range(KC):
                        dve.wait_ge(bank_ready, q * KC + k + 2)
                        dve.wait_ge(columns_ready, 1)
                        nc.vector.tensor_scalar(hT_lo[:, k, ds(q * CH, CH)].bitcast(F32), turned[:, k % BANKS], scale_c[:, k:k + 1], shift_c[:, k:k + 1],
                                                ALU.mult, ALU.add).then_inc(h_ready, 1)
            dve.wait_ge(vectors_loaded, 16)
            s = Steps(dve, vector_step)
            for v in (1, 4):
                s.link(nc.vector.tensor_scalar(vectors[:, v], vectors[:, v], 1.0, None, ALU.add))
            for v in (2, 5):
                s.link(nc.vector.tensor_scalar(gate_sign, vectors[:, v], 0.0, 2.0, ALU.is_ge, ALU.mult))
                s.link(nc.vector.scalar_tensor_tensor(out=gate_size, in0=vectors[:, v], scalar=-1.0, in1=vectors[:, v],
                                                      op0=ALU.mult, op1=ALU.max))
                s.link(nc.vector.tensor_scalar(gate_size, gate_size, 0.25, None, ALU.max))
                s.link(nc.vector.scalar_tensor_tensor(out=vectors[:, v], in0=gate_sign, scalar=-1.0, in1=gate_size,
                                                      op0=ALU.add, op1=ALU.mult))
            dve.sem_inc(vectors_ready, 1)

        @block.gpsimd
        def _(pool):
            pool.wait_ge(columns_taken, 2)
            nc.gpsimd.tensor_scalar(scale_c[:, :], scale_c[:, :], 1.0, None, ALU.add).then_inc(columns_ready, 1)
            with pool.Fori(0, NQ // 2) as i:
                for g in range(2):
                    for k in range(KC):
                        pool.wait_ge(hi_done, (i * 2 + g) * KC + k + 1)
                        col = ds((i * 2 + g) * CH, CH)
                        nc.gpsimd.tensor_tensor(hT_lo[:, k, col], hT_lo[:, k, col].bitcast(F32), hT_hi[:, k, col], ALU.subtract).then_inc(lo_done, 1)

        @block.tensor
        def _(pe):
            def multiply(n, half, b):
                pe.wait_ge(w_loaded[b], half * 16 + 16)
                pe.wait_ge(row_ready, n + 1)
                for k in range(KC):
                    last = nc.tensor.matmul(acc[:, b], silu[:, k:k + 1], wbuf[:, b, k], start=(k == 0), stop=(k == KC - 1))
                last.then_inc(acc_ready, 1)

            pe.wait_ge(silu_ready, 1)
            for n in range(2 * VC):
                multiply(n, n // 2, n % 2)
            pe.wait_ge(ident_loaded, 16)
            pe.wait_ge(first_loaded, 16)
            for j in range(2):
                last = nc.tensor.transpose(columns[:, j], first_two[:, j], ident[0:KC, 0:KC])
            last.then_inc(columns_turned, 1)
            with pe.Fori(0, NQ // 2) as i:
                for g in range(2):
                    q = i * 2 + g
                    for b in range(2):
                        multiply(q * 2 + (2 * VC + b), q + VC, b)
                    pe.wait_ge(xn_ready, q * TPC + TPC)
                    for k in range(KC):
                        pe.wait_ge(h_ready, q * KC + k + 1)
                        for j in range(TPC):
                            last = nc.tensor.transpose(turned[:, k % BANKS, j * P:(j + 1) * P], xt[:, g, j, k * P:(k + 1) * P], ident[:, :])
                        last.then_inc(bank_ready, 1)

BODY = 2 * NQ


def product(nc, acc, lhs, rhs):
    for k in range(KC):
        nc.tensor.matmul(acc, lhs(0, k), rhs(0, k), start=(k == 0), stop=False)
        nc.tensor.matmul(acc, lhs(0, k), rhs(1, k), start=False, stop=False)
        last = nc.tensor.matmul(acc, lhs(1, k), rhs(0, k), start=False, stop=(k == KC - 1))
    return last


def project(nc, sem, kind, w_tiles, first, hT, consts, ad, outs, rows_d=None):
    rope, adapted = kind != "v", kind != "q"
    with ExitStack() as ctx:
        sb = lambda name, shape, dt=F32: ctx.enter_context(nc.sbuf_tensor(f"{kind}_{name}", shape, dt))
        pb = lambda name, shape: ctx.enter_context(nc.psum_tensor(f"{kind}_{name}_psum", shape, F32))
        sm = lambda name: sem(f"{kind}_{name}")
        w_raw = sb("w_raw", [P, 2, C])
        w_hi = sb("w_hi", [P, 2, C], F32R)
        w_lo = sb("w_lo", [P, 2, C], F32R)
        acc = pb("acc", [P, 2, CH])
        if rope:
            cos = sb("cos", [P, T])
            sin = sb("sin", [P, T])
            x_cos = sb("x_cos", [P, CH])
            x_rot = sb("x_rot", [P, CH])
            y = sb("y", [P, 2, CH])
            y_hi = sb("y_hi", [P, 2, CH], F32R)
            y_lo = sb("y_lo", [P, 2, CH], F32R)
        else:
            zeros = sb("zeros", [P, C])
            ident = sb("ident", [P, P])
            vT = sb("vT", [P, 2, CH])
            v_out = sb("v_out", [P, 2, CH])
            turned = pb("turned", [P, 2, CH])
        if adapted:
            a_rep = sb("a_rep", [P, KC, HG, D])
            block_mask = sb("block_mask", [P, P])
            a_acc = pb("a_acc", [P, P])

        consts_loaded, w_raw_free = sm("consts_loaded"), sm("w_raw_free")
        w_loaded = [sm("w_loaded0"), sm("w_loaded1")]
        w_hi_done, w_ready, w_free = sm("w_hi_done"), sm("w_ready"), sm("w_free")
        acc_ready, acc_free = sm("acc_ready"), sm("acc_free")
        stored = [sm("stored0"), sm("stored1")]
        rep_cleared, rep_loaded, a_acc_ready, a_kept = sm("rep_cleared"), sm("rep_loaded"), sm("a_acc_ready"), sm("a_kept")
        rot_step, y_ready, y_hi_done, y_lo_done = sm("rot_step"), sm("y_ready"), sm("y_hi_done"), sm("y_lo_done")
        marks, zeros_set, zeroed = sm("marks"), sm("zeros_set"), sm("zeroed")
        FILLS = rows_d.shape[0] // P // G if rows_d is not None else 0
        vT_ready, turned_ready, v_out_ready = sm("vT_ready"), sm("turned_ready"), sm("v_out_ready")
        n_const = {"k": 3, "v": 2, "q": 2}[kind]
        STORES = 32 if rope else 16
        block = ctx.enter_context(nc.Block())

        @block.sync
        def _(sp):
            with sp.Fori(0, G // 2) as i:
                for v in range(2):
                    sp.wait_ge(w_raw_free, i * 2 + v + 1)
                    sp.dma_start(w_raw[:, v], w_tiles[ds(i * 2 + (first + v))].rearrange("a p n -> (a p) n")).then_inc(w_loaded[v], 16)

        @block.gpsimd
        def _(pool):
            pool.sem_inc(w_raw_free, 2)
            if adapted:
                nc.gpsimd.memset(a_rep[:, :, :, :], 0.0).then_inc(rep_cleared, 1)
            if FILLS:
                nc.gpsimd.memset(zeros[:, :], 0.0).then_inc(zeros_set, 1)
                pool.wait_ge(zeros_set, 1)
            with pool.Fori(0, G // 2) as i:
                for v in range(2):
                    pool.wait_ge(w_free, i * 2 + v + 1)
                    pool.wait_ge(w_loaded[v], i * 16 + 16)
                    pool.sem_inc(marks, 1)
                    nc.gpsimd.tensor_copy(w_hi[:, v], w_raw[:, v]).then_inc(w_hi_done, 1)
                    pool.wait_ge(w_hi_done, i * 2 + v + 1)
                    nc.gpsimd.tensor_tensor(w_lo[:, v], w_raw[:, v], w_hi[:, v], ALU.subtract).then_inc(w_ready, 1)
                    if not adapted:
                        pool.wait_ge(w_ready, i * 2 + v + 1)
                        pool.sem_inc(w_raw_free, 1)
                    for m in range(FILLS):
                        pool.dma_start(rows_d[ds(((i * 2 + v) * FILLS + m) * P, P), :], zeros[:, :]).then_inc(zeroed, 16)
            if FILLS:
                pool.wait_ge(zeroed, 16 * G * FILLS)

        @block.tensor
        def _(pe):
            pe.sem_inc(w_free, 2)

            def turn_v(i, u):
                pe.wait_ge(consts_loaded, 16 * n_const)
                pe.wait_ge(vT_ready, i * BODY + u + 1)
                pe.wait_ge(v_out_ready, i * BODY + u + 1)
                for j in range(TPC):
                    last = nc.tensor.transpose(turned[:, u % 2, j * P:(j + 1) * P], vT[:, u % 2, j * P:(j + 1) * P], ident[:, :])
                last.then_inc(turned_ready, 1)

            def adapter_too(i, v):
                pe.wait_ge(rep_loaded, 16 * HG)
                pe.wait_ge(a_kept, i * 2 + v + 1)
                for k in range(KC):
                    rep = a_rep[:, k].rearrange("p h a -> p (h a)")
                    w = w_raw[:, v, k * P:(k + 1) * P]
                    last = nc.tensor.matmul(a_acc[:, :], *((w, rep) if kind == "k" else (rep, w)), start=(k == 0), stop=(k == KC - 1))
                last.then_inc(a_acc_ready, 1)
                pe.wait_ge(a_acc_ready, i * 2 + v + 1)
                pe.sem_inc(w_raw_free, 1)

            with pe.Fori(0, G // 2) as i:
                for u in range(BODY):
                    v = u // NQ
                    if u % NQ == 0:
                        pe.wait_ge(w_ready, i * 2 + v + 1)
                    pe.wait_ge(acc_free, i * BODY + u + 1)
                    col = slice(u % NQ * CH, (u % NQ + 1) * CH)
                    product(nc, acc[:, u % 2],
                            lambda part, k: (w_hi, w_lo)[part][:, v, k * P:(k + 1) * P],
                            lambda part, k: hT[part][:, k, col]).then_inc(acc_ready, 1)
                    if adapted and u % NQ == 0:
                        adapter_too(i, v)
                    if kind == "v" and u >= 1:
                        turn_v(i, u - 1)
                    if u % NQ == NQ - 1:
                        pe.wait_ge(acc_ready, i * BODY + u + 1)
                        pe.sem_inc(w_free, 1)
                if kind == "v":
                    turn_v(i, BODY - 1)

        @block.scalar
        def _(act):
            nc.scalar.preload_act_table(ACT.Exp)
            act.wait_ge(w_loaded[0], 16)
            if adapted:
                act.wait_ge(rep_cleared, 1)
                for h in range(HG):
                    act.dma_start(a_rep[:, :, h, 0:A], consts["adapter"]).then_inc(rep_loaded, 16)
                act.dma_start(block_mask[:, :], consts["block_mask"]).then_inc(consts_loaded, 16)
            if rope:
                act.dma_start(cos[:, :], consts["cos"]).then_inc(consts_loaded, 16)
                act.dma_start(sin[:, :], consts["sin"]).then_inc(consts_loaded, 16)
            else:
                act.dma_start(ident[:, :], consts["ident"]).then_inc(consts_loaded, 16)
            with act.Fori(0, G // 2) as i:
                for u in range(BODY):
                    v, rows, n = u // NQ, ds((i * 2 + u // NQ)), i * BODY + u
                    if kind == "v":
                        act.wait_ge(acc_ready, n + 1)
                        act.wait_ge(turned_ready, n + 1)
                        nc.scalar.activation(vT[:, u % 2], acc[:, u % 2], ACT.Copy).then_inc(vT_ready, 1)
                        act.wait_ge(vT_ready, n + 1)
                        act.sem_inc(acc_free, 1)
                    else:
                        act.wait_ge(y_ready, n + 1)
                        act.wait_ge(stored[u % 2], i * (STORES * NQ) + STORES * (u // 2 + 1))
                        nc.scalar.activation(y_hi[:, u % 2], y[:, u % 2], ACT.Copy).then_inc(y_hi_done, 1)
                    for b in ([u - 1] if u else []) + ([u] if u == BODY - 1 else []):
                        g = ds(i * 2 + b // NQ)
                        if kind == "v":
                            act.wait_ge(v_out_ready, i * BODY + b + 3)
                            t0 = b % NQ * TPC
                            act.dma_start(outs[0][g, :, t0:t0 + TPC, :].rearrange("g p k n -> (g p) (k n)"), v_out[:, b % 2]).then_inc(stored[b % 2], 16)
                        else:
                            col = slice(b % NQ * CH, (b % NQ + 1) * CH)
                            act.wait_ge(y_lo_done, i * BODY + b + 1)
                            for part, src in ((0, y_hi), (1, y_lo)):
                                act.dma_start(outs[part][g, :, col].rearrange("g p n -> (g p) n"), src[:, b % 2].bitcast(F32)).then_inc(stored[b % 2], 16)
            for b in range(2):
                act.wait_ge(stored[b], STORES * (G * NQ // 2 + 1))

        @block.vector
        def _(dve):
            dve.sem_inc(acc_free, 2)
            for b in range(2):
                dve.sem_inc(stored[b], STORES)
            if kind == "v":
                dve.sem_inc(turned_ready, 2)
                dve.sem_inc(v_out_ready, 2)
            if adapted:
                dve.sem_inc(a_kept, 1)
            dve.wait_ge(consts_loaded, 16 * n_const)
            swap = [(d + D // 2) % D for d in range(D)]

            def keep_adapter(i, v):
                dve.wait_ge(a_acc_ready, i * 2 + v + 1)
                nc.vector.tensor_tensor(ad[:, ds(i * 2 + v)].rearrange("p a n -> p (a n)"), a_acc[:, :], block_mask[:, :],
                                        ALU.mult).then_inc(a_kept, 1)

            def rotate(i, u):
                s = Steps(dve, rot_step, i * (3 * BODY) + 3 * u)
                col = slice(u % NQ * CH, (u % NQ + 1) * CH)
                dve.wait_ge(acc_ready, i * BODY + u + 1)
                dve.sem_inc(marks, 1)
                nc.vector.stream_shuffle(x_rot[:, :], acc[:, u % 2], swap)
                s.link(nc.vector.tensor_tensor(x_cos[:, :], acc[:, u % 2], cos[:, col], ALU.mult))
                dve.sem_inc(acc_free, 1)
                s.link(nc.vector.tensor_tensor(x_rot[:, :], x_rot[:, :], sin[:, col], ALU.mult))
                dve.wait_ge(stored[u % 2], i * (STORES * NQ) + STORES * (u // 2 + 1))
                s.link(nc.vector.tensor_tensor(y[:, u % 2], x_cos[:, :], x_rot[:, :], ALU.add))
                dve.sem_inc(y_ready, 1)

            def split(i, u):
                dve.wait_ge(y_hi_done, i * BODY + u + 1)
                nc.vector.tensor_tensor(y_lo[:, u % 2], y[:, u % 2], y_hi[:, u % 2], ALU.subtract).then_inc(y_lo_done, 1)

            def out_v(i, u):
                dve.wait_ge(turned_ready, i * BODY + u + 3)
                dve.wait_ge(stored[u % 2], i * (STORES * NQ) + STORES * (u // 2 + 1))
                nc.vector.tensor_copy(v_out[:, u % 2], turned[:, u % 2]).then_inc(v_out_ready, 1)

            with dve.Fori(0, G // 2) as i:
                for u in range(BODY):
                    if rope:
                        rotate(i, u)
                    if adapted and u % NQ == 0:
                        keep_adapter(i, u // NQ)
                    if u >= 1:
                        (split if rope else out_v)(i, u - 1)
                (split if rope else out_v)(i, BODY - 1)


def adapter_attention(nc, sem, consts, ak, av, q_hi_d, q_lo_d, out):
    UN = 2 * NQ
    with ExitStack() as ctx:
        sb = lambda name, shape, dt=F32: ctx.enter_context(nc.sbuf_tensor(f"a_{name}", shape, dt))
        pb = lambda name, shape: ctx.enter_context(nc.psum_tensor(f"a_{name}_psum", shape, F32))
        sm = lambda name: sem(f"a_{name}")
        M = TPC * HG
        ident = sb("ident", [P, P])
        gating = sb("gating", [P, 1])
        q_hi, q_lo, q = sb("q_hi", [P, UN, CH]), sb("q_lo", [P, UN, CH]), sb("q", [P, UN, CH])
        av_cur = sb("av_cur", [P, 2, P])
        top, total, inv = sb("top", [P, M]), sb("total", [P, M]), sb("inv", [P, M])
        weight = sb("weight", [P, UN, M, A])
        prob = sb("prob", [P, UN, M, D])
        probT = sb("probT", [P, 2, CH])
        y = sb("y", [P, UN, CH])
        scores, turned, acc = pb("scores", [P, 2, CH]), pb("turned", [P, 2, CH]), pb("acc", [P, 2, CH])
        consts_loaded, cleared = sm("consts_loaded"), sm("cleared")
        q_loaded = [sm(f"q_loaded{u}") for u in range(UN)]
        q_ready, q_used, scores_ready, step, shifted, exp_done = sm("q_ready"), sm("q_used"), sm("scores_ready"), sm("step"), sm("shifted"), sm("exp_done")
        prob_ready, turned_ready, probT_ready, av_ready, acc_ready, y_ready = (
            sm("prob_ready"), sm("turned_ready"), sm("probT_ready"), sm("av_ready"), sm("acc_ready"), sm("y_ready"))
        stored, marks = [sm(f"stored{u}") for u in range(UN)], sm("marks")
        block = ctx.enter_context(nc.Block())

        @block.sync
        def _(sp):
            sp.dma_start(ident[:, :], consts["ident"]).then_inc(consts_loaded, 16)
            sp.dma_start(gating[:, :], consts["gating"].rearrange("(a n) -> a n", a=1).broadcast_to([P, 1])).then_inc(consts_loaded, 16)
            with sp.Fori(0, G // 2) as i:
                for u in range(UN):
                    sp.wait_ge(q_ready, i * UN + u + 1)
                    for src, dst in ((q_hi_d, q_hi), (q_lo_d, q_lo)):
                        sp.dma_start(dst[:, u], src[ds(i * 2 + u // NQ), :, u % NQ * CH:(u % NQ + 1) * CH].rearrange("g p n -> (g p) n")).then_inc(q_loaded[u], 16)

        @block.gpsimd
        def _(pool):
            pool.sem_inc(q_ready, UN)
            pool.sem_inc(acc_ready, UN)
            nc.gpsimd.memset(prob[:, :, :, :], 0.0).then_inc(cleared, 1)
            with pool.Fori(0, G // 2) as i:
                pool.wait_ge(acc_ready, i * UN + UN)
                pool.sem_inc(marks, 1)
                nc.gpsimd.tensor_copy(av_cur[:, :, :], av[:, ds(i * 2, 2)]).then_inc(av_ready, 1)
                for u in range(UN):
                    pool.wait_ge(q_loaded[u], i * 32 + 32)
                    pool.wait_ge(q_used, i * UN + u + 1)
                    nc.gpsimd.tensor_tensor(q[:, u], q_hi[:, u], q_lo[:, u], ALU.add).then_inc(q_ready, 1)

        @block.tensor
        def _(pe):
            pe.sem_inc(q_used, UN)
            pe.wait_ge(consts_loaded, 32)

            def score(i, u):
                pe.wait_ge(q_ready, i * UN + u + 1 + UN)
                pe.wait_ge(shifted, i * UN + u + 1)
                for j in range(TPC):
                    last = nc.tensor.matmul(scores[:, u % 2, j * P:(j + 1) * P], q[:, u, j * P:(j + 1) * P],
                                            ak[:, ds(i * 2 + u // NQ)].rearrange("p a n -> p (a n)"), start=True, stop=True)
                last.then_inc(scores_ready, 1)
                pe.wait_ge(scores_ready, i * UN + u + 1)
                pe.sem_inc(q_used, 1)

            def turn(i, u):
                pe.wait_ge(prob_ready, i * UN + u + 1)
                pe.wait_ge(probT_ready, i * UN + u + 1)
                for j in range(TPC):
                    last = nc.tensor.transpose(turned[:, u % 2, j * P:(j + 1) * P],
                                               prob[:, u, j * HG:(j + 1) * HG, :].rearrange("p h a -> p (h a)"), ident[:, :])
                last.then_inc(turned_ready, 1)

            def multiply(i, u):
                pe.wait_ge(probT_ready, i * UN + u + 3)
                pe.wait_ge(av_ready, i + 1)
                pe.wait_ge(y_ready, i * UN + u + 1)
                nc.tensor.matmul(acc[:, u % 2], av_cur[:, u // NQ], probT[:, u % 2], start=True, stop=True).then_inc(acc_ready, 1)

            with pe.Fori(0, G // 2) as i:
                for u in range(UN + 3):
                    if u < UN:
                        score(i, u)
                    if 2 <= u <= UN + 1:
                        turn(i, u - 2)
                    if u >= 3:
                        multiply(i, u - 3)

        @block.vector
        def _(dve):
            dve.sem_inc(shifted, 2)
            dve.wait_ge(consts_loaded, 32)
            dve.wait_ge(cleared, 1)

            def shift(i, u, s):
                dve.wait_ge(scores_ready, i * UN + u + 1)
                dve.wait_ge(shifted, i * UN + u + 2)
                view = scores[:, u % 2].rearrange("p (m a) -> p m a", a=D)[:, :, 0:A]
                s.link(nc.vector.tensor_reduce(top[:, :], view, AX.X, ALU.max))
                nc.vector.tensor_tensor(weight[:, u], view, top[:, :].rearrange("p (m a) -> p m a", a=1).broadcast_to([P, M, A]),
                                        ALU.subtract).then_inc(shifted, 1)

            def norm(i, u, s):
                dve.wait_ge(exp_done, i * UN + u + 1)
                s.link(nc.vector.tensor_reduce(total[:, :], weight[:, u], AX.X, ALU.add))
                s.link(nc.vector.reciprocal(inv[:, :], total[:, :]))
                s.link(nc.vector.tensor_scalar(inv[:, :], inv[:, :], gating[:, 0:1], None, ALU.mult))
                s.link(nc.vector.tensor_tensor(prob[:, u, :, 0:A], weight[:, u],
                                               inv[:, :].rearrange("p (m a) -> p m a", a=1).broadcast_to([P, M, A]), ALU.mult))
                dve.sem_inc(prob_ready, 1)

            with dve.Fori(0, G // 2) as i:
                s = Steps(dve, step, i * (5 * UN))
                for u in range(UN + 1):
                    if u < UN:
                        shift(i, u, s)
                    if u >= 1:
                        norm(i, u - 1, s)

        @block.scalar
        def _(act):
            nc.scalar.preload_act_table(ACT.Exp)
            act.sem_inc(probT_ready, 2)
            act.sem_inc(y_ready, 2)
            for u in range(UN):
                act.sem_inc(stored[u], 16)
            with act.Fori(0, G // 2) as i:
                for u in range(UN + 3):
                    if u < UN:
                        act.wait_ge(shifted, i * UN + u + 3)
                        nc.scalar.activation(weight[:, u], weight[:, u], ACT.Exp, scale=1.0 / math.sqrt(C)).then_inc(exp_done, 1)
                    if 2 <= u <= UN + 1:
                        b = u - 2
                        act.wait_ge(turned_ready, i * UN + b + 1)
                        act.wait_ge(acc_ready, i * UN + b + UN - 1)
                        nc.scalar.activation(probT[:, b % 2], turned[:, b % 2], ACT.Copy).then_inc(probT_ready, 1)
                    if u >= 3:
                        b = u - 3
                        act.wait_ge(acc_ready, i * UN + b + UN + 1)
                        act.wait_ge(stored[b], i * 16 + 16)
                        nc.scalar.activation(y[:, b], acc[:, b % 2], ACT.Copy).then_inc(y_ready, 1)
                        act.wait_ge(y_ready, i * UN + b + 3)
                        act.dma_start(out[ds(i * 2 + b // NQ), :, b % NQ * CH:(b % NQ + 1) * CH].rearrange("g p n -> (g p) n"), y[:, b]).then_inc(stored[b], 16)
            for u in range(UN):
                act.wait_ge(stored[u], 16 * (G // 2 + 1))

MASKED = -1.0e38
BF16 = mybir.dt.bfloat16
HALF = HG // 2
STACK = 3 * D


def attention(nc, sem, consts, q_parts, k_parts, v_d, a_d, out_parts):
    UNITS = [(par, qc) for par in range(2) for qc in range(NQ)]
    W = len(UNITS)
    steps_of = lambda qc: TPC * (qc + 1)
    STEPS = sum(steps_of(qc) for _, qc in UNITS)
    items_of = lambda qc: HG * TPC * (qc + 1)
    ITEMS = sum(items_of(qc) for _, qc in UNITS) + W
    PAIRS = STEPS // 2
    RING = 4
    Y_LAG, A_LAG, TOTAL_LAG, NORM_LAG, SPLIT_LAG, STORE_LAG = 2, 2, 3, 4, 6, 7
    LOADS = 7 * 16
    ROW = HG * 16
    with ExitStack() as ctx:
        sb = lambda name, shape, dt=F32: ctx.enter_context(nc.sbuf_tensor(f"t_{name}", shape, dt))
        pb = lambda name, shape: ctx.enter_context(nc.psum_tensor(f"t_{name}_psum", shape, F32))
        sm = lambda name: sem(f"t_{name}")
        q_stack = [sb(f"q_stack{b}", [P, HG, T], F32R) for b in range(2)]
        k_stack = [sb(f"k_stack{b}", [P, HG, T], F32R) for b in range(2)]
        v = [sb(f"v{b}", [P, NT, P]) for b in range(2)]
        ident = sb("ident", [P, P])
        causal = sb("causal", [P, CH])
        after = sb("after", [P, P])
        ident_b, after_b = sb("ident_b", [P, P], BF16), sb("after_b", [P, P], BF16)
        ones = sb("ones", [P, D])
        part = sb("part", [P, HG * TPC, NQ])
        top = sb("top", [P, HG * TPC])
        minus_top = sb("minus_top", [HG * TPC, 2, P], F32R)
        prob, two = sb("prob", [P, RING, 2, HALF, CH]), sb("two", [P, 2, 2, HALF, CH])
        y_own, whole = sb("y_own", [P, CH]), sb("whole", [P, CH])
        y = sb("y", [P, CH])
        y_hi, y_lo = sb("y_hi", [P, CH], F32R), sb("y_lo", [P, CH], F32R)
        seen = pb("seen", [P, 2, CH])
        scores = pb("scores", [P, 2, HALF, CH])
        y_acc, total = pb("y_acc", [P, CH]), pb("total", [P, CH])

        consts_loaded, ones_set, rows_set = sm("consts_loaded"), sm("ones_set"), sm("rows_set")
        first_loaded = [sm(f"first_loaded{c}") for c in range(NQ + 1)]
        loaded = [sm("loaded0"), sm("loaded1")]
        seen_ready, seen_free, top_ready, minus_ready = sm("seen_ready"), sm("seen_free"), sm("top_ready"), sm("minus_ready")
        row_loaded = [sm("row_loaded0"), sm("row_loaded1")]
        scores_ready, exp_done, sums_set, cleared = sm("scores_ready"), sm("exp_done"), sm("sums_set"), sm("cleared")
        y_done, two_ready, total_done, y_free, total_free = sm("y_done"), sm("two_ready"), sm("total_done"), sm("y_free"), sm("total_free")
        a_loaded, stored = sm("a_loaded"), sm("stored")
        norm_step, y_ready, y_hi_done, y_lo_done = sm("norm_step"), sm("y_ready"), sm("y_hi_done"), sm("y_lo_done")
        marks = sm("marks")
        block = ctx.enter_context(nc.Block())

        def first_step(wi):
            return sum(steps_of(UNITS[w][1]) for w in range(wi))

        def last_step(wi):
            return first_step(wi + 1) - 1

        steps = [(wi, s) for wi, (_, qc) in enumerate(UNITS) for s in range(steps_of(qc))]

        def ended(i, step, lag):
            return [wi for wi in range(-1, 0 if isinstance(i, int) else W) if last_step(wi) == step - lag]

        def first_column(step):
            wi, kt = steps[step]
            return max(kt - UNITS[wi][1] * TPC, 0) * P

        def group_of(i, wi):
            par = UNITS[wi][0]
            return ds(i * 2 + par) if wi >= 0 else ds((i * 2 + (G - 2 + par)) % G)

        order = []
        for dg in range(3):
            for qc in range(NQ):
                order += [("see", dg, qc, c, h, j) for c in range(qc + 1) for h in range(HG) for j in range(TPC)]
                order.append(("turn", dg, qc, 0, 0, 0))
        for n in [n for n, entry in enumerate(order) if entry[0] == "turn"][-2::-1]:
            order.insert(n + 2, order.pop(n))
        AHEAD = items_of(NQ - 1) + 3 * HG
        PACE = HG

        def until(banks):
            seen_so_far = 0
            for n, entry in enumerate(order):
                if entry[0] == "see":
                    if seen_so_far == banks:
                        return n
                    seen_so_far += 1

        HEAD = until(AHEAD)
        upto = lambda step: until(AHEAD + PACE * step + step % 2)
        entries_of = lambda step: range(upto(step), upto(step + 1))
        assert STEPS % RING == 0

        def share(step, quarter):
            entries = entries_of(step)
            ends = [0, 1, 2, 4, 5] if step % 2 == 0 else [0, 1, 1, 2, 3]
            return entries[len(entries) * ends[quarter] // ends[4]:len(entries) * ends[quarter + 1] // ends[4]]
        unit_of = lambda entry: entry[1] * NQ + entry[2]
        assert until(AHEAD + PACE * STEPS) - HEAD == ITEMS and ITEMS % 2 == 0
        ends_unit = {n for n, entry in enumerate(order) if entry[0] == "see" and
                     unit_of(entry) != unit_of(next((x for x in order[n + 1:] if x[0] == "see"), (0, -1, 0)))}

        def load_parts(eng, par, g, col, done):
            for src, dst, rows in ((q_parts[0], q_stack, 0), (q_parts[1], q_stack, 1), (q_parts[0], q_stack, 2),
                                   (k_parts[0], k_stack, 0), (k_parts[0], k_stack, 1), (k_parts[1], k_stack, 2)):
                eng.dma_start(dst[par][rows * D:(rows + 1) * D, :, col].bitcast(F32),
                              src[g, :, col].rearrange("g (h d) n -> d (g h) n", d=D)).then_inc(done, 16)

        def load_group(eng, par, g):
            load_parts(eng, par, g, slice(0, T), loaded[par])
            eng.dma_start(v[par][:, :, :], v_d[g].rearrange("g p k n -> (g p) k n")).then_inc(loaded[par], 16)

        def load_row(eng, par, qc, b):
            for h in range(HG):
                dst = q_stack[par][STACK:STACK + 1, h, qc * CH:(qc + 1) * CH].bitcast(F32)
                eng.dma_start(dst.rearrange("a (j c) -> a j c", c=P), minus_top[h * TPC:(h + 1) * TPC, b].bitcast(F32)).then_inc(row_loaded[b], 16)

        def store(eng, i, wi):
            qc = UNITS[wi][1]
            eng.wait_ge(y_lo_done, i * W + wi + 3)
            for dst, src in zip(out_parts, (y_hi, y_lo)):
                eng.dma_start(dst[group_of(i, wi), :, qc * CH:(qc + 1) * CH].rearrange("g p n -> (g p) n"),
                              src[:, :].bitcast(F32)).then_inc(stored, 16)

        @block.sync
        def _(sp):
            def load_consts():
                for dst, name in ((ident, "ident"), (causal, "causal"), (after, "after")):
                    sp.dma_start(dst[:, :], consts[name]).then_inc(consts_loaded, 16)

            for c in range(NQ):
                load_parts(sp, 0, ds(0), slice(c * CH, (c + 1) * CH), first_loaded[c])
                if c == 0:
                    load_consts()
            sp.dma_start(v[0][:, :, :], v_d[0]).then_inc(first_loaded[NQ], 16)
            for entry in order[:HEAD]:
                if entry[0] == "turn":
                    sp.wait_ge(minus_ready, unit_of(entry) + 1)
                    load_row(sp, entry[1] % 2, entry[2], unit_of(entry) % 2)

            def finish(i, step):
                for wi in ended(i, step, A_LAG):
                    qc = UNITS[wi][1]
                    sp.wait_ge(y_lo_done, i * W + wi + 2)
                    sp.dma_start(y[:, :], a_d[group_of(i, wi), :, qc * CH:(qc + 1) * CH].rearrange("g p n -> (g p) n")).then_inc(a_loaded, 16)
                for wi in ended(i, step, STORE_LAG):
                    store(sp, i, wi)

            with sp.Fori(0, G // 2) as i:
                for step in range(STEPS):
                    finish(i, step)
                    for n in entries_of(step):
                        if order[n][0] == "turn":
                            sp.wait_ge(minus_ready, i * W + unit_of(order[n]) + 1)
                            load_row(sp, order[n][1] % 2, order[n][2], unit_of(order[n]) % 2)
            for step in range(STORE_LAG):
                finish(G // 2, step)
            sp.wait_ge(stored, 32 * (G * NQ + 2))
            for b in range(2):
                sp.wait_ge(row_loaded[b], ROW * (G * NQ // 2 + 1 + sum(e[0] == "turn" and unit_of(e) % 2 == b for e in order[:HEAD])))

        @block.tensor
        def _(pe):
            def see(base, n, par, qc, c, h, j):
                width = CH if c < qc else (j + 1) * P
                pe.wait_ge(seen_free, base + n + 1)
                t0 = qc * CH + j * P
                nc.tensor.matmul(seen[:, n % 2, 0:width], q_stack[par][0:STACK, h, t0:t0 + P],
                                 k_stack[par][0:STACK, h, c * CH:c * CH + width], start=True, stop=True).then_inc(seen_ready, 1)

            def turn_top(base, n, w):
                pe.wait_ge(consts_loaded, 48)
                pe.wait_ge(top_ready, w + 1)
                pe.wait_ge(seen_free, base + n + 1)
                nc.tensor.transpose(seen[0:HG * TPC, n % 2, 0:P], top[:, :], ident[:, :]).then_inc(seen_ready, 1)

            def advance(i, n):
                what, dg, qc, c, h, j = order[n]
                if what == "see":
                    see(i * ITEMS, n, dg % 2, qc, c, h, j)
                else:
                    turn_top(i * ITEMS, n, i * W + unit_of(order[n]))

            def score(i, step, pair):
                wi, kt = steps[step]
                par, qc = UNITS[wi]
                c0, r = first_column(step), kt - qc * TPC
                pe.wait_ge(exp_done, (i * STEPS + step) * 2 + pair + 1)
                for x in range(HALF):
                    h = pair * HALF + x
                    last = nc.tensor.matmul(scores[:, pair, x, c0:CH], k_stack[par][0:STACK + 1, h, kt * P:(kt + 1) * P],
                                            q_stack[par][0:STACK + 1, h, qc * CH + c0:(qc + 1) * CH], start=True, stop=(r < 0))
                    if r >= 0:
                        last = nc.tensor.matmul(scores[:, pair, x, c0:c0 + P], ident_b[:, :], after_b[:, :],
                                                start=False, stop=True)
                last.then_inc(scores_ready, 1)

            def multiply(i, step):
                wi, kt = steps[step]
                par, qc = UNITS[wi]
                c0 = first_column(step)
                if step >= 0 or isinstance(i, int):
                    pe.wait_ge(exp_done, (i * STEPS + step) * 2 + 4)
                if kt == 0:
                    pe.wait_ge(y_free, i * W + wi + 1)
                for h in range(HG):
                    last = nc.tensor.matmul(y_acc[h * D:(h + 1) * D, c0:CH], v[par][:, kt, h * D:(h + 1) * D],
                                            prob[:, step % RING, h // HALF, h % HALF, c0:CH],
                                            start=(kt == 0), stop=(kt == steps_of(qc) - 1))
                last.then_inc(y_done, 1)

            def add_up(i, pair):
                wi, kt = steps[2 * pair]
                c0 = first_column(2 * pair)
                pe.wait_ge(two_ready, (i * PAIRS + pair) * 2 + 6)
                if kt == 0:
                    pe.wait_ge(total_free, i * W + wi + 1)
                for h in range(HG):
                    last = nc.tensor.matmul(total[h * D:(h + 1) * D, c0:CH], ones[:, :], two[:, pair % 2, h // HALF, h % HALF, c0:CH],
                                            start=(kt == 0), stop=(kt == steps_of(UNITS[wi][1]) - 2))
                last.then_inc(total_done, 1)

            for n in range(HEAD):
                if order[n][0] == "see" and order[n][3:] == (0, 0, 0):
                    pe.wait_ge(first_loaded[order[n][2]], LOADS - 16)
                advance(0, n)
            for c in range(NQ):
                pe.wait_ge(first_loaded[c], LOADS - 16)
            pe.wait_ge(first_loaded[NQ], 16)
            pe.wait_ge(ones_set, 4)
            pe.wait_ge(rows_set, 2)
            pe.wait_ge(sums_set, 2)
            for acc, lhs in ((y_acc, v[1][:, NT - 1, 0:D]), (total, ones[:, :])):
                for h in range(HG):
                    nc.tensor.matmul(acc[h * D:(h + 1) * D, :], lhs, prob[:, 0, 0, 0], start=True, stop=False)

            def add_step(i, step):
                if step % 2 == 0:
                    add_up(i, (step - TOTAL_LAG - 1) // 2)

            with pe.Fori(0, G // 2) as i:
                for step in range(STEPS):
                    wi = steps[step][0]
                    if steps[step][1] == 0:
                        pe.wait_ge(row_loaded[wi % 2], i * (ROW * W // 2) + ROW * (wi // 2 + 2))
                    for quarter in range(4):
                        if quarter < 2:
                            score(i, step, quarter)
                        elif quarter == 2:
                            multiply(i, step - Y_LAG)
                        else:
                            add_step(i, step)
                        for n in share(step, quarter):
                            if order[n][1] > 0 and order[n - 1][1:] != order[n][1:] and order[n][:1] + order[n][2:] == ("see", 0, 0, 0, 0):
                                pe.wait_ge(loaded[order[n][1] % 2], i * LOADS + LOADS)
                            advance(i, n)
            for step in range(TOTAL_LAG):
                if step < Y_LAG:
                    multiply(G // 2, step - Y_LAG)
                add_step(G // 2, step)

        @block.scalar
        def _(act):
            nc.scalar.preload_act_table(ACT.Exp)
            act.sem_inc(exp_done, 2)
            act.wait_ge(sums_set, 2)

            def take_y(i, wi):
                act.wait_ge(y_done, i * STEPS + last_step(wi) + 1 + RING)
                act.wait_ge(y_ready, i * W + wi + 2)
                nc.scalar.activation(y_own[:, :], y_acc[:, :], ACT.Copy).then_inc(y_free, 1)

            def take_total(i, wi):
                act.wait_ge(total_done, i * PAIRS + last_step(wi) // 2 + 3)
                act.wait_ge(y_ready, i * W + wi + 2)
                nc.scalar.activation(whole[:, :], total[:, :], ACT.Copy).then_inc(total_free, 1)

            def finish(i, step):
                for wi in ended(i, step, Y_LAG):
                    take_y(i, wi)
                    if not isinstance(i, int) and wi in (-1, NQ - 1):
                        load_group(act, 1 if wi == -1 else 0, ds(i * 2 + 1) if wi == -1 else ds((i * 2 + 2) % G))
                for wi in ended(i, step, TOTAL_LAG):
                    take_total(i, wi)

            with act.Fori(0, G // 2) as i:
                for step in range(STEPS):
                    c0 = first_column(step)
                    act.wait_ge(y_done, i * STEPS + step + 1)
                    if step % 2 == 0:
                        act.wait_ge(two_ready, (i * PAIRS + step // 2) * 2 + 2)
                    for pair in range(2):
                        act.wait_ge(scores_ready, (i * STEPS + step) * 2 + pair + 1)
                        nc.scalar.activation(prob[:, step % RING, pair, :, c0:CH], scores[:, pair, :, c0:CH], ACT.Exp,
                                             scale=1.0 / math.sqrt(D)).then_inc(exp_done, 1)
                    finish(i, step)
            for step in range(TOTAL_LAG + 1):
                finish(G // 2, step)

        @block.vector
        def _(dve):
            dve.sem_inc(seen_free, 2)
            dve.sem_inc(y_ready, 1)
            dve.sem_inc(y_done, RING - Y_LAG)
            dve.sem_inc(stored, 32)
            for b in range(2):
                dve.sem_inc(row_loaded[b], ROW)
            nc.vector.memset(ones[:, :], 1.0).then_inc(ones_set, 1)
            nc.vector.memset(v[1][:, NT - 2:NT], 1.0).then_inc(ones_set, 1)
            dve.wait_ge(consts_loaded, 48)
            nc.vector.tensor_copy(ident_b[:, :], ident[:, :]).then_inc(ones_set, 1)
            nc.vector.tensor_copy(after_b[:, :], after[:, :]).then_inc(ones_set, 1)

            def largest(base, n, qc, c, h, j):
                dve.wait_ge(seen_ready, base + n + 1)
                dst = part[:, h * TPC + j, c:c + 1]
                if c < qc:
                    nc.vector.tensor_reduce(dst, seen[:, n % 2], AX.X, ALU.max).then_inc(seen_free, 1)
                else:
                    dve.sem_inc(marks, 1)
                    width = (j + 1) * P
                    nc.vector.tensor_tensor_reduce(out=seen[:, n % 2, 0:width], in0=seen[:, n % 2, 0:width], in1=causal[:, CH - width:CH],
                                                   scale=1.0, scalar=MASKED, op0=ALU.add, op1=ALU.max, accum_out=dst).then_inc(seen_free, 1)

            def gather(base, n, w, qc):
                dve.wait_ge(seen_free, base + n + 3)
                nc.vector.tensor_reduce(top[:, :], part[:, :, 0:qc + 1], AX.X, ALU.max).then_inc(top_ready, 1)
                dve.wait_ge(top_ready, w + 1)

            def negate(base, n, w, rows, b):
                dve.wait_ge(seen_ready, base + n + 1)
                dve.wait_ge(row_loaded[b], rows * ROW + ROW)
                nc.vector.tensor_scalar(minus_top[:, b], seen[0:HG * TPC, n % 2, 0:P], -1.0, None, ALU.mult).then_inc(minus_ready, 1)
                dve.wait_ge(minus_ready, w + 1)
                dve.sem_inc(seen_free, 1)

            def advance(i, n):
                what, dg, qc, c, h, j = order[n]
                w = unit_of(order[n])
                if what == "see":
                    largest(i * ITEMS, n, qc, c, h, j)
                    if n in ends_unit:
                        gather(i * ITEMS, n, i * W + w, qc)
                else:
                    negate(i * ITEMS, n, i * W + w, i * (W // 2) + w // 2, w % 2)

            def invert(i, wi, piece):
                if piece == 0:
                    dve.wait_ge(total_free, i * W + wi + 2)
                col = slice(piece * P, (piece + 1) * P)
                nc.vector.reciprocal(whole[:, col], whole[:, col]).then_inc(norm_step, 1)

            def divide(i, wi):
                at = (i * W + wi + 1) * (TPC + 1) + TPC
                dve.wait_ge(norm_step, at)
                dve.wait_ge(y_free, i * W + wi + 2)
                nc.vector.tensor_tensor(y_own[:, :], y_own[:, :], whole[:, :], ALU.mult).then_inc(norm_step, 1)
                dve.wait_ge(norm_step, at + 1)
                dve.wait_ge(a_loaded, (i * W + wi + 2) * 16)
                nc.vector.tensor_tensor(y[:, :], y[:, :], y_own[:, :], ALU.add).then_inc(y_ready, 1)

            for n in range(HEAD):
                advance(0, n)

            def finish(i, step, quarter):
                for wi in ended(i, step, NORM_LAG):
                    invert(i, wi, quarter)
                for wi in ended(i, step, NORM_LAG + 1):
                    if quarter == 1:
                        divide(i, wi)

            with dve.Fori(0, G // 2) as i:
                for step in range(STEPS):
                    for quarter in range(TPC):
                        for n in share(step, quarter):
                            advance(i, n)
                        finish(i, step, quarter)
            for step in range(NORM_LAG + 1):
                for quarter in range(TPC):
                    finish(G // 2, step, quarter)

        @block.gpsimd
        def _(pool):
            pool.sem_inc(y_lo_done, 1)
            pool.sem_inc(two_ready, 3)
            for b in range(2):
                nc.gpsimd.memset(k_stack[b][STACK:STACK + 1, :, :].bitcast(F32), 1.0).then_inc(rows_set, 1)
                pool.wait_ge(rows_set, b + 1)
            nc.gpsimd.memset(prob[:, :, :, :, :], 1.0).then_inc(sums_set, 1)
            nc.gpsimd.memset(two[:, :, :, :, :], 1.0).then_inc(sums_set, 1)
            pool.wait_ge(sums_set, 2)

            def add_two(i, pair, half):
                c0 = first_column(2 * pair)
                if half == 0:
                    pool.wait_ge(exp_done, (i * STEPS + 2 * pair + 1) * 2 + 4)
                    pool.wait_ge(total_done, i * PAIRS + pair + 1)
                    c1 = first_column(2 * pair + 1)
                    if c1 > c0:
                        pool.sem_inc(marks, 1)
                        nc.gpsimd.memset(prob[:, (2 * pair + 1) % RING, :, :, c0:c1], 0.0).then_inc(cleared, 1)
                        pool.wait_ge(cleared, (i * W + steps[2 * pair][0]) * (TPC // 2) + (c0 > 0) + 1)
                a, b = (prob[:, (2 * pair + x) % RING, half, :, c0:CH] for x in range(2))
                nc.gpsimd.tensor_tensor(two[:, pair % 2, half, :, c0:CH], a, b, ALU.add).then_inc(two_ready, 1)

            def split(i, wi):
                pool.wait_ge(y_ready, i * W + wi + 3)
                pool.wait_ge(stored, (i * W + wi + 2) * 32)
                pool.sem_inc(marks, 1)
                nc.gpsimd.tensor_copy(y_hi[:, :], y[:, :]).then_inc(y_hi_done, 1)
                pool.wait_ge(y_hi_done, i * W + wi + 2)
                nc.gpsimd.tensor_tensor(y_lo[:, :], y[:, :], y_hi[:, :], ALU.subtract).then_inc(y_lo_done, 1)

            def finish(i, step):
                if step % 2 == 0:
                    add_two(i, step // 2 - 1, 1)
                for wi in ended(i, step, SPLIT_LAG):
                    split(i, wi)

            with pool.Fori(0, G // 2) as i:
                for step in range(STEPS):
                    finish(i, step)
                    if step % 2 == 1:
                        add_two(i, step // 2, 0)
            for step in range(SPLIT_LAG):
                if step == 0:
                    add_two(G // 2, -1, 1)
                for wi in ended(i, step, SPLIT_LAG):
                    split(G // 2, wi)

MT = 2
MROWS = MT * P
MAX_MACRO = 2 * T // MROWS + E - 1
LAG = 2


def proj_out(nc, sem, consts, mod_rows, w_proj, y_parts, x, x1_d, h2, logitsT):
    RING = 4
    with ExitStack() as ctx:
        sb = lambda name, shape, dt=F32: ctx.enter_context(nc.sbuf_tensor(f"o_{name}", shape, dt))
        pb = lambda name, shape: ctx.enter_context(nc.psum_tensor(f"o_{name}_psum", shape, F32))
        sm = lambda name: sem(f"o_{name}")
        w_raw = sb("w_raw", [P, RING - 2, C])
        w_hi, w_lo = sb("w_hi", [P, KC, C], F32R), sb("w_lo", [P, KC, C], F32R)
        ident = sb("ident", [P, P])
        gate_w = sb("gate_w", [P, KC, E])
        ga, shift_b, scale_b = sb("ga", [P, C]), sb("shift", [P, C]), sb("scale", [P, C])
        y_hi, y_lo = sb("y_hi", [P, 2, G, P], F32R), sb("y_lo", [P, 2, G, P], F32R)
        xt, x1, xn = sb("x", [P, 2, C]), sb("x1", [P, 2, C]), sb("xn", [P, C])
        stats, mv = sb("stats", [P, 2, 6]), sb("mv", [P, 2])
        std, rstd, newton = sb("std", [P, 1]), sb("rstd", [P, 1]), sb("newton", [P, 1])
        h = sb("h", [P, 2, C])
        h2T = sb("h2T", [P, KC, P])
        acc, turned, logits = pb("acc", [P, 2, C]), pb("turned", [P, KC, P]), pb("logits", [E, P])
        consts_loaded, w_hi_done, w_ready = sm("consts_loaded"), sm("w_hi_done"), sm("w_ready")
        w_loaded = [sm(f"w_loaded{r}") for r in range(RING)]
        y_loaded, x_loaded = [sm("y_loaded0"), sm("y_loaded1")], [sm("x_loaded0"), sm("x_loaded1")]
        acc_ready, x1_ready, step, var_ready, std_ready, xn_ready, scaled, h_ready = (
            sm("acc_ready"), sm("x1_ready"), sm("step"), sm("var_ready"), sm("std_ready"), sm("xn_ready"), sm("scaled"), sm("h_ready"))
        turned_ready, h2T_ready, logits_ready, logits_kept = sm("turned_ready"), sm("h2T_ready"), sm("logits_ready"), sm("logits_kept")
        stored, kept, marks = [sm("stored0"), sm("stored1")], [sm("kept0"), sm("kept1")], sm("marks")
        raw = lambda k: w_raw[:, k % RING] if k % RING < RING - 2 else x1[:, k % RING - (RING - 2)]
        block = ctx.enter_context(nc.Block())

        @block.sync
        def _(sp):
            for k in range(KC):
                if k >= RING:
                    sp.wait_ge(w_ready, k - RING + 1)
                sp.dma_start(raw(k), w_proj[k * P:(k + 1) * P, :]).then_inc(w_loaded[k % RING], 16)
            sp.dma_start(ident[:, :], consts["ident"]).then_inc(consts_loaded, 16)
            sp.dma_start(gate_w[:, :, :], consts["gate_w"].rearrange("(k p) e -> p k e", p=P)).then_inc(consts_loaded, 16)
            for j, dst in ((2, ga), (3, shift_b), (4, scale_b)):
                sp.dma_start(dst[:, :], mod_rows[j * C:(j + 1) * C].rearrange("(a n) -> a n", a=1).broadcast_to([P, C])).then_inc(consts_loaded, 16)
            with sp.Fori(0, NT // 2) as i:
                for b in range(2):
                    n = i * 2 + b
                    sp.wait_ge(acc_ready, n + 1)
                    for src, dst in zip(y_parts, (y_hi, y_lo)):
                        sp.dma_start(dst[:, b].bitcast(F32), src[:, :, ds(n * P, P)].rearrange("g p n -> p g n")).then_inc(y_loaded[b], 16)
                    sp.wait_ge(x1_ready, n + 1)
                    sp.dma_start(xt[:, b], x[ds(n * P, P), :]).then_inc(x_loaded[b], 16)

        @block.tensor
        def _(pe):
            pe.sem_inc(acc_ready, 2)
            pe.wait_ge(consts_loaded, 16 * 5)
            pe.wait_ge(w_ready, KC)

            def turn(n, b):
                pe.wait_ge(h_ready, n + 1)
                pe.wait_ge(h2T_ready, n + 1)
                for k in range(KC):
                    last = nc.tensor.transpose(turned[:, k], h[:, b, k * P:(k + 1) * P], ident[:, :])
                last.then_inc(turned_ready, 1)

            def gate(n):
                pe.wait_ge(h2T_ready, n + 2)
                pe.wait_ge(logits_kept, n + 1)
                for k in range(KC):
                    last = nc.tensor.matmul(logits[:, :], gate_w[:, k], h2T[:, k], start=(k == 0), stop=(k == KC - 1))
                last.then_inc(logits_ready, 1)

            def project(i, b):
                pe.wait_ge(y_loaded[b], i * 32 + 32)
                pe.wait_ge(x1_ready, i * 2 + b + 1)
                for o in range(2):
                    col = slice(o * CH, (o + 1) * CH)
                    last = product(nc, acc[:, b, col], lambda part, k: (y_hi, y_lo)[part][:, b, k],
                                   lambda part, k: (w_hi, w_lo)[part][:, k, col])
                last.then_inc(acc_ready, 1)

            with pe.Fori(0, NT // 2) as i:
                for b in range(2):
                    turn(i * 2 + b, b)
                    project(i, b)
                    gate(i * 2 + b)
            for n in range(NT, NT + LAG):
                turn(n, n % 2)
                gate(n)

        @block.scalar
        def _(act):
            nc.scalar.preload_act_table(ACT.Sqrt)
            act.sem_inc(h2T_ready, 1)
            act.sem_inc(logits_kept, 1)
            for k in range(KC):
                act.wait_ge(w_loaded[k % RING], 16 * (k // RING + 1))
                nc.scalar.activation(w_hi[:, k], raw(k), ACT.Copy).then_inc(w_hi_done, 1)

            def keep(n, col):
                act.wait_ge(turned_ready, n + 1)
                act.wait_ge(logits_ready, n + 1)
                nc.scalar.activation(h2T[:, :, :], turned[:, :, :], ACT.Copy).then_inc(h2T_ready, 1)
                act.wait_ge(logits_ready, n + 2)
                nc.scalar.activation(logitsT[:, col], logits[:, :], ACT.Copy).then_inc(logits_kept, 1)

            act.sem_inc(logits_ready, 1)
            with act.Fori(0, NT // 2) as i:
                for b in range(2):
                    keep(i * 2 + b, ds((i * 2 + b) * P, P))
                    act.wait_ge(var_ready, i * 2 + b + 1)
                    nc.scalar.activation(std[:, :], mv[:, 1:2], ACT.Sqrt).then_inc(std_ready, 1)
                    n = i * 2 + b
                    act.wait_ge(h_ready, n + LAG + 1)
                    act.dma_start(h2[:, ds(n)].rearrange("p a n -> p (a n)"), h[:, b]).then_inc(kept[b], 16)
                    act.dma_start(x1_d[ds(n * P, P), :], x1[:, b]).then_inc(stored[b], 16)
            for n in range(NT, NT + LAG):
                keep(n, slice(n * P, (n + 1) * P))
            for b in range(2):
                act.wait_ge(kept[b], 16 * (NT // 2 + 1))
                act.wait_ge(stored[b], 16 * (NT // 2 + 1))

        @block.vector
        def _(dve):
            dve.sem_inc(x1_ready, 2)
            for b in range(2):
                dve.sem_inc(stored[b], 16)
            for k in range(KC):
                dve.wait_ge(w_hi_done, k + 1)
                nc.vector.tensor_tensor(w_lo[:, k], raw(k), w_hi[:, k], ALU.subtract).then_inc(w_ready, 1)
            dve.wait_ge(w_ready, KC)
            dve.wait_ge(consts_loaded, 16 * 5)
            with dve.Fori(0, NT // 2) as i:
                s = Steps(dve, step, i * (2 * 9))
                for b in range(2):
                    n = i * 2 + b
                    dve.wait_ge(acc_ready, n + 3)
                    dve.wait_ge(stored[b], i * 16 + 16)
                    dve.wait_ge(xn_ready, n + 1)
                    s.link(nc.vector.tensor_tensor(x1[:, b], acc[:, b], ga[:, :], ALU.mult))
                    dve.wait_ge(x_loaded[b], i * 16 + 16)
                    s.link(nc.vector.tensor_tensor(x1[:, b], x1[:, b], xt[:, b], ALU.add))
                    dve.sem_inc(x1_ready, 1)
                    nc.vector.bn_stats(stats[:, 0], x1[:, b, 0:CH])
                    s.link(nc.vector.bn_stats(stats[:, 1], x1[:, b, CH:C]))
                    dve.sem_inc(marks, 1)
                    s.link(nc.vector.bn_aggr(mv[:, :], stats[:, :, :].rearrange("p a b -> p (a b)")))
                    nc.vector.tensor_scalar(mv[:, 1:2], mv[:, 1:2], EPS, None, ALU.add).then_inc(var_ready, 1)
                    dve.wait_ge(std_ready, n + 1)
                    s.link(nc.vector.reciprocal(rstd[:, :], std[:, :]))
                    s.link(nc.vector.tensor_tensor(newton[:, :], rstd[:, :], rstd[:, :], ALU.mult))
                    s.link(nc.vector.tensor_tensor(newton[:, :], newton[:, :], mv[:, 1:2], ALU.mult))
                    s.link(nc.vector.tensor_scalar(newton[:, :], newton[:, :], -0.5, 1.5, ALU.mult, ALU.add))
                    s.link(nc.vector.tensor_tensor(rstd[:, :], rstd[:, :], newton[:, :], ALU.mult))
                    dve.wait_ge(scaled, n + 1)
                    nc.vector.tensor_scalar(xn[:, :], x1[:, b], mv[:, 0:1], rstd[:, 0:1], ALU.subtract, ALU.mult).then_inc(xn_ready, 1)

        @block.gpsimd
        def _(pool):
            pool.sem_inc(scaled, 1)
            pool.sem_inc(xn_ready, 1)
            nc.gpsimd.memset(h[:, :, :], 0.0).then_inc(h_ready, LAG)
            for b in range(2):
                pool.sem_inc(kept[b], 16)
            pool.wait_ge(consts_loaded, 16 * 5)
            with pool.Fori(0, NT // 2) as i:
                for b in range(2):
                    n = i * 2 + b
                    pool.wait_ge(turned_ready, n + 1)
                    pool.wait_ge(kept[b], i * 16 + 16)
                    pool.wait_ge(xn_ready, n + 2)
                    nc.gpsimd.tensor_tensor(h[:, b], xn[:, :], scale_b[:, :], ALU.mult).then_inc(scaled, 1)
                    pool.wait_ge(scaled, n + 2)
                    nc.gpsimd.tensor_tensor(h[:, b], h[:, b], shift_b[:, :], ALU.add).then_inc(h_ready, 1)


def route(nc, sem, consts, h2, logitsT, slots, weights, bounds, rows_d):
    NTH = T // MROWS - 1
    with ExitStack() as ctx:
        sb = lambda name, shape, dt=F32: ctx.enter_context(nc.sbuf_tensor(f"r_{name}", shape, dt))
        pb = lambda name, shape: ctx.enter_context(nc.psum_tensor(f"r_{name}_psum", shape, F32))
        sm = lambda name: sem(f"r_{name}")
        ident, before, ones = sb("ident", [P, P]), sb("before", [P, P]), sb("ones", [P, P])
        numbers, limits = sb("numbers", [P, E]), sb("limits", [P, NTH])
        logits, best, index = sb("logits", [P, NT, E]), sb("best", [P, NT, 8]), sb("index", [P, NT, 8], U32)
        indexf = sb("indexf", [P, NT, 8])
        first, second, both = sb("first", [P, NT, E]), sb("second", [P, NT, E]), sb("both", [P, NT, E])
        gap, denom = sb("gap", [P, NT]), sb("denom", [P, NT])
        ahead, over = sb("ahead", [P, NT + 1, E]), sb("over", [P, E, NTH])
        macros, start = sb("macros", [P, E]), sb("start", [P, E + 1])
        row, picked, slotf = sb("row", [P, NT, E]), sb("picked", [P, NT, E]), sb("slotf", [P, 2, NT])
        p_logits, p_rank, p_count = pb("logits", [P, CH]), pb("rank", [P, CH]), pb("count", [P, CH])
        consts_loaded, turned_ready, both_ready, ranks_ready = sm("consts_loaded"), sm("turned_ready"), sm("both_ready"), sm("ranks_ready")
        step, gap_ready, exp_done, slots_ready, scattered = sm("step"), sm("gap_ready"), sm("exp_done"), sm("slots_ready"), sm("scattered")
        block = ctx.enter_context(nc.Block())

        @block.sync
        def _(sp):
            for dst, name in ((ident[:, :], "ident"), (before[:, :], "before"), (numbers[:, :], "numbers"), (limits[:, :], "limits")):
                sp.dma_start(dst, consts[name]).then_inc(consts_loaded, 16)

        @block.tensor
        def _(pe):
            pe.wait_ge(consts_loaded, 64)
            for i in range(NT):
                last = nc.tensor.transpose(p_logits[:, i * E:(i + 1) * E], logitsT[:, (i + LAG) * P:(i + LAG + 1) * P], ident[0:E, 0:E])
            last.then_inc(turned_ready, 1)
            pe.wait_ge(both_ready, 1)
            m = both[:, :, :].rearrange("p i e -> p (i e)")
            nc.tensor.matmul(p_rank[:, 0:P], before[:, :], m, start=True, stop=True)
            nc.tensor.matmul(p_count[:, 0:P], ones[:, :], m, start=True, stop=True).then_inc(ranks_ready, 1)

        @block.scalar
        def _(act):
            nc.scalar.preload_act_table(ACT.Exp)
            act.wait_ge(gap_ready, 1)
            nc.scalar.activation(gap[:, :], gap[:, :], ACT.Exp).then_inc(exp_done, 1)

        @block.vector
        def _(dve):
            s = Steps(dve, step)
            wide = lambda ap, shape: ap.broadcast_to(shape)
            s.link(nc.vector.memset(ones[:, :], 1.0))
            s.link(nc.vector.memset(ahead[:, 0], 0.0))
            s.link(nc.vector.memset(start[:, 0:1], 0.0))
            dve.wait_ge(consts_loaded, 64)
            dve.wait_ge(turned_ready, 1)
            s.link(nc.vector.tensor_copy(logits[:, :, :].rearrange("p i e -> p (i e)"), p_logits[:, 0:NT * E]))
            for i in range(NT):
                last = nc.vector.max(best[:, i], logits[:, i])
            s.link(last)
            for i in range(NT):
                last = nc.vector.max_index(index[:, i], best[:, i], logits[:, i])
            s.link(last)
            s.link(nc.vector.tensor_copy(indexf[:, :, :], index[:, :, :]))
            numbers_w = wide(numbers[:, :].rearrange("p (a e) -> p a e", a=1), [P, NT, E])
            for c, mask in ((0, first), (1, second)):
                s.link(nc.vector.tensor_tensor(mask[:, :, :], wide(indexf[:, :, c:c + 1], [P, NT, E]), numbers_w, ALU.is_equal))
            nc.vector.tensor_tensor(both[:, :, :], first[:, :, :], second[:, :, :], ALU.add).then_inc(both_ready, 1)
            nc.vector.tensor_tensor(gap[:, :], best[:, :, 1], best[:, :, 0], ALU.subtract).then_inc(gap_ready, 1)
            dve.wait_ge(exp_done, 1)
            s.link(nc.vector.tensor_scalar(denom[:, :], gap[:, :], 1.0, None, ALU.add))
            s.link(nc.vector.reciprocal(weights[:, 0], denom[:, :]))
            s.link(nc.vector.tensor_tensor(weights[:, 1], gap[:, :], weights[:, 0], ALU.mult))
            dve.wait_ge(ranks_ready, 1)
            for i in range(NT):
                s.link(nc.vector.tensor_tensor(ahead[:, i + 1], p_count[:, i * E:(i + 1) * E], ahead[:, i], ALU.add))
            s.link(nc.vector.tensor_tensor(over[:, :, :], wide(ahead[:, NT].rearrange("p (e a) -> p e a", a=1), [P, E, NTH]),
                                           wide(limits[:, :].rearrange("p (a l) -> p a l", a=1), [P, E, NTH]), ALU.is_gt))
            s.link(nc.vector.tensor_reduce(macros[:, :], over[:, :, :], AX.X, ALU.add))
            s.link(nc.vector.tensor_scalar(macros[:, :], macros[:, :], 1.0, None, ALU.add))
            for e in range(E):
                s.link(nc.vector.tensor_tensor(start[:, e + 1:e + 2], start[:, e:e + 1], macros[:, e:e + 1], ALU.add))
            s.link(nc.vector.tensor_copy(bounds[:, :], start[0:1, :]))
            s.link(nc.vector.tensor_tensor(row[:, :, :].rearrange("p i e -> p (i e)"), p_rank[:, 0:P],
                                           ahead[:, 0:NT].rearrange("p i e -> p (i e)"), ALU.add))
            s.link(nc.vector.tensor_scalar(macros[:, :], start[:, 0:E], float(MROWS), None, ALU.mult))
            s.link(nc.vector.tensor_tensor(row[:, :, :], row[:, :, :], wide(macros[:, :].rearrange("p (a e) -> p a e", a=1), [P, NT, E]), ALU.add))
            for c, mask in ((0, first), (1, second)):
                s.link(nc.vector.tensor_tensor(picked[:, :, :], mask[:, :, :], row[:, :, :], ALU.mult))
                s.link(nc.vector.tensor_reduce(slotf[:, c], picked[:, :, :], AX.X, ALU.add))
            nc.vector.tensor_copy(slots[:, :, :], slotf[:, :, :]).then_inc(slots_ready, 1)

        @block.gpsimd
        def _(pool):
            pool.wait_ge(slots_ready, 1)
            for i in range(NT):
                for c in range(2):
                    nc.gpsimd.indirect_dma_start(rows_d, bass.IndirectOffsetOnAxis(ap=slots[:, c, i:i + 1], axis=0),
                                                 h2[:, i], None).then_inc(scattered, 16)
            pool.wait_ge(scattered, 16 * 2 * NT)


def experts(nc, sem, consts, mod_rows, expert_w, bounds, rows_d):
    RAWS = 4
    with ExitStack() as ctx:
        sb = lambda name, shape, dt=F32: ctx.enter_context(nc.sbuf_tensor(f"e_{name}", shape, dt))
        pb = lambda name, shape: ctx.enter_context(nc.psum_tensor(f"e_{name}_psum", shape, F32))
        sm = lambda name: sem(f"e_{name}")
        ident, gb = sb("ident", [P, P]), sb("gb", [P, C])
        w_raw = sb("w_raw", [P, RAWS, C])
        w_hi = [sb(f"w_hi{b}", [P, KC, C], F32R) for b in range(2)]
        w_lo = [sb(f"w_lo{b}", [P, KC, C], F32R) for b in range(2)]
        xt = sb("x", [P, MT, C])
        x_hi, x_lo = sb("x_hi", [P, MT, KC, P], F32R), sb("x_lo", [P, MT, KC, P], F32R)
        y = sb("y", [P, MT, C])
        turned, acc = pb("turned", [P, C]), pb("acc", [P, MT, C])
        consts_loaded = sm("consts_loaded")
        w_loaded, w_hi_done, w_ready, w_free = [sm(f"w_loaded{r}") for r in range(RAWS)], sm("w_hi_done"), sm("w_ready"), sm("w_free")
        x_loaded, turned_ready, x_hi_done, x_ready = [sm(f"x_loaded{s}") for s in range(MT)], sm("turned_ready"), sm("x_hi_done"), sm("x_ready")
        acc_ready, y_ready, stored, marks = sm("acc_ready"), sm("y_ready"), [sm(f"stored{s}") for s in range(MT)], sm("marks")
        block = ctx.enter_context(nc.Block())

        def bound(eng, e):
            return eng.value_load(bounds[0:1, e:e + 1], min_val=0, max_val=MAX_MACRO) if isinstance(e, int) else eng.value_load(bounds[0:1, ds(e)], min_val=0, max_val=MAX_MACRO)

        @block.sync
        def _(sp):
            sp.dma_start(ident[:, :], consts["ident"]).then_inc(consts_loaded, 16)
            sp.dma_start(gb[:, :], mod_rows[5 * C:6 * C].rearrange("(a n) -> a n", a=1).broadcast_to([P, C])).then_inc(consts_loaded, 16)
            for s in range(MT):
                sp.dma_start(xt[:, s], rows_d[s * P:(s + 1) * P, :]).then_inc(x_loaded[s], 16)
            total = bound(sp, E)
            with sp.Fori(0, total) as g:
                for s in range(MT):
                    sp.wait_ge(turned_ready, g * MT + s + 2)
                    sp.dma_start(xt[:, s], rows_d[ds((g * MT + (s + MT)) * P, P), :]).then_inc(x_loaded[s], 16)
            for s in range(MT):
                sp.wait_ge(x_loaded[s], total * 16 + 16)
            sp.sem_inc(marks, 1)

        @block.gpsimd
        def _(pool):
            def load(e, c):
                src = expert_w[ds(e), c * P:(c + 1) * P, :].rearrange("a p n -> (a p) n")
                pool.dma_start(w_raw[:, c % RAWS], src).then_inc(w_loaded[c % RAWS], 16)

            def load_ahead(e, c):
                pool.wait_ge(w_ready, e * KC + c + 1)
                ahead = c + RAWS
                if ahead < KC:
                    load(e, ahead)
                elif not (isinstance(e, int) and e == E - 1):
                    load(e + 1, ahead - KC)

            def split(e, b):
                pool.wait_ge(w_free, e + 1)
                for c in range(KC):
                    pool.wait_ge(w_loaded[c % RAWS], e * (16 * KC // RAWS) + 16 * (c // RAWS + 1))
                    pool.sem_inc(marks, 1)
                    nc.gpsimd.tensor_copy(w_hi[b][:, c], w_raw[:, c % RAWS]).then_inc(w_hi_done, 1)
                    pool.wait_ge(w_hi_done, e * KC + c + 1)
                    nc.gpsimd.tensor_tensor(w_lo[b][:, c], w_raw[:, c % RAWS], w_hi[b][:, c], ALU.subtract).then_inc(w_ready, 1)
                    load_ahead(e, c)

            for c in range(RAWS):
                load(0, c)
            for c in range(KC):
                load_ahead(0, c)
            with pool.Fori(0, E // 2 - 1) as j:
                for b in range(2):
                    split(j * 2 + (b + 1), 1 - b)
            split(E - 1, 1)

        @block.tensor
        def _(pe):
            pe.sem_inc(w_free, 2)
            pe.sem_inc(turned_ready, 1)
            pe.sem_inc(acc_ready, 1)
            pe.wait_ge(consts_loaded, 32)

            def turn(n, s, loads):
                pe.wait_ge(x_loaded[s], loads)
                pe.wait_ge(x_ready, n + 1)
                for k in range(KC):
                    last = nc.tensor.transpose(turned[:, k * P:(k + 1) * P], xt[:, s, k * P:(k + 1) * P], ident[:, :])
                last.then_inc(turned_ready, 1)

            turn(0, 0, 16)
            with pe.Fori(0, E // 2) as j:
                for b in range(2):
                    lo, hi = bound(pe, j * 2 + b), bound(pe, j * 2 + (b + 1))
                    pe.wait_ge(w_ready, (j * 2 + b) * KC + KC)
                    pe.sem_inc(marks, 1)
                    with pe.Fori(lo, hi) as g:
                        for s in range(MT):
                            turn(g * MT + (s + 1), (s + 1) % MT, g * 16 + 16 * (1 + s))
                            pe.wait_ge(x_ready, g * MT + s + 2)
                            pe.wait_ge(y_ready, g * MT + s + 1)
                            for o in range(2):
                                col = slice(o * CH, (o + 1) * CH)
                                last = product(nc, acc[:, s, col], lambda part, k: (x_hi, x_lo)[part][:, s, k],
                                               lambda part, k: (w_hi, w_lo)[part][b][:, k, col])
                            last.then_inc(acc_ready, 1)
                    pe.wait_ge(acc_ready, hi * MT + 1)
                    pe.sem_inc(w_free, 1)

        @block.scalar
        def _(act):
            nc.scalar.preload_act_table(ACT.Exp)
            total = bound(act, E)
            for c in range(KC):
                act.wait_ge(w_loaded[c % RAWS], 16 * (c // RAWS + 1))
                nc.scalar.activation(w_hi[0][:, c], w_raw[:, c % RAWS], ACT.Copy).then_inc(w_hi_done, 1)
            act.wait_ge(turned_ready, 2)
            nc.scalar.activation(x_hi[:, 0].rearrange("p k n -> p (k n)"), turned[:, :], ACT.Copy).then_inc(x_hi_done, 1)
            with act.Fori(0, total) as g:
                for s in range(MT):
                    act.wait_ge(turned_ready, g * MT + s + 3)
                    act.wait_ge(acc_ready, g * MT + s + 1)
                    nc.scalar.activation(x_hi[:, (s + 1) % MT].rearrange("p k n -> p (k n)"), turned[:, :], ACT.Copy).then_inc(x_hi_done, 1)
                    act.wait_ge(y_ready, g * MT + s + 3)
                    act.dma_start(rows_d[ds((g * MT + s) * P, P), :], y[:, s]).then_inc(stored[s], 16)
            for s in range(MT):
                act.wait_ge(stored[s], total * 16 + 16)
            act.sem_inc(marks, 1)

        @block.vector
        def _(dve):
            dve.sem_inc(x_ready, 1)
            dve.sem_inc(y_ready, 2)
            for s in range(MT):
                dve.sem_inc(stored[s], 16)
            dve.wait_ge(consts_loaded, 32)
            total = bound(dve, E)
            for c in range(KC):
                dve.wait_ge(w_hi_done, c + 1)
                nc.vector.tensor_tensor(w_lo[0][:, c], w_raw[:, c % RAWS], w_hi[0][:, c], ALU.subtract).then_inc(w_ready, 1)

            def split(n, s):
                dve.wait_ge(x_hi_done, n + 1)
                nc.vector.tensor_tensor(x_lo[:, s].rearrange("p k n -> p (k n)"), turned[:, :],
                                        x_hi[:, s].rearrange("p k n -> p (k n)"), ALU.subtract).then_inc(x_ready, 1)

            split(0, 0)
            with dve.Fori(0, total) as g:
                for s in range(MT):
                    split(g * MT + (s + 1), (s + 1) % MT)
                    dve.wait_ge(acc_ready, g * MT + s + 2)
                    dve.wait_ge(stored[s], g * 16 + 16)
                    nc.vector.tensor_tensor(y[:, s], acc[:, s], gb[:, :], ALU.mult).then_inc(y_ready, 1)


def combine(nc, sem, slots, weights, out_rows_d, x1_d, out):
    with ExitStack() as ctx:
        sb = lambda name, shape, dt=F32: ctx.enter_context(nc.sbuf_tensor(f"c_{name}", shape, dt))
        sm = lambda name: sem(f"c_{name}")
        B = 4
        rows, x1, res = sb("rows", [P, B, 2, C]), sb("x1", [P, B, C]), sb("res", [P, B, C])
        gathered, x1_loaded = [sm(f"gathered{b}") for b in range(B)], [sm(f"x1_loaded{b}") for b in range(B)]
        half, done, stored = sm("half"), sm("done"), [sm(f"stored{b}") for b in range(B)]
        block = ctx.enter_context(nc.Block())

        @block.gpsimd
        def _(pool):
            for i in range(NT):
                b = i % B
                if i >= B:
                    pool.wait_ge(done, i - B + 1)
                for c in range(2):
                    nc.gpsimd.indirect_dma_start(rows[:, b, c], None, out_rows_d,
                                                 bass.IndirectOffsetOnAxis(ap=slots[:, c, i:i + 1], axis=0)).then_inc(gathered[b], 16)

        @block.sync
        def _(sp):
            for i in range(NT + 2):
                if i < NT:
                    if i >= B:
                        sp.wait_ge(done, i - B + 1)
                    sp.dma_start(x1[:, i % B], x1_d[i * P:(i + 1) * P, :]).then_inc(x1_loaded[i % B], 16)
                if i >= 2:
                    n = i - 2
                    sp.wait_ge(done, n + 1)
                    sp.dma_start(out[n * P:(n + 1) * P, :], res[:, n % B]).then_inc(stored[n % B], 16)
            for b in range(B):
                sp.wait_ge(stored[b], 16 * (NT // B))

        @block.vector
        def _(dve):
            for i in range(NT):
                b = i % B
                dve.wait_ge(gathered[b], 32 * (i // B + 1))
                dve.wait_ge(x1_loaded[b], 16 * (i // B + 1))
                if i >= B:
                    dve.wait_ge(stored[b], 16 * (i // B))
                nc.vector.scalar_tensor_tensor(out=res[:, b], in0=rows[:, b, 0], scalar=weights[:, 0, i:i + 1], in1=x1[:, b],
                                               op0=ALU.mult, op1=ALU.add).then_inc(half, 1)
                dve.wait_ge(half, i + 1)
                nc.vector.scalar_tensor_tensor(out=res[:, b], in0=rows[:, b, 1], scalar=weights[:, 1, i:i + 1], in1=res[:, b],
                                               op0=ALU.mult, op1=ALU.add).then_inc(done, 1)


@contextmanager
def semaphores(nc):
    taken = []

    def sem(name):
        taken.append(nc.alloc_semaphore(name=name))
        return taken[-1]

    yield sem
    nc.clear_and_free_semaphores(taken)
    nc.all_engine_barrier()


def adaln_block(nc, x, w_attn, w_proj, adapter, gating, gate_w, expert_w, c, wmod, consts, out):
    def scratch(name, shape):
        return nc.dram_tensor(f"scratch_{name}", shape, F32).ap()

    mod_rows = scratch("mod_rows", [6 * C])
    q_hi, q_lo, k_hi, k_lo = (scratch(n, [G, P, T]) for n in ("q_hi", "q_lo", "k_hi", "k_lo"))
    v, a_y = scratch("v", [G, P, NT, P]), scratch("a_y", [G, P, T])
    y_hi, y_lo = scratch("y_hi", [G, P, T]), scratch("y_lo", [G, P, T])
    x1 = scratch("x1", [T, C])
    rows = scratch("rows", [(MAX_MACRO + 1) * MROWS, C])
    consts = dict(consts, adapter=adapter, gating=gating, gate_w=gate_w)
    with ExitStack() as ctx:
        with semaphores(nc) as sem, ExitStack() as stage:
            ak = stage.enter_context(nc.sbuf_tensor("ak", [P, G, P], F32))
            av = stage.enter_context(nc.sbuf_tensor("av", [P, G, P], F32))
            with ExitStack() as inner:
                hT = [inner.enter_context(nc.sbuf_tensor(n, [P, KC, T], F32R)) for n in ("hT_hi", "hT_lo")]
                modulated_norm(nc, sem, x, c, wmod, consts["ident"], scratch("mod_raw", [6 * C]), mod_rows, *hT)
                project(nc, sem, "k", w_attn, G, hT, consts, ak, (k_hi, k_lo))
                project(nc, sem, "v", w_attn, 2 * G, hT, consts, av, (v,), rows)
                project(nc, sem, "q", w_attn, 0, hT, consts, None, (q_hi, q_lo))
            adapter_attention(nc, sem, consts, ak, av, q_hi, q_lo, a_y)
        with semaphores(nc) as sem:
            attention(nc, sem, consts, (q_hi, q_lo), (k_hi, k_lo), v, a_y, (y_hi, y_lo))
        slots = ctx.enter_context(nc.sbuf_tensor("slots", [P, 2, NT], I32))
        weights = ctx.enter_context(nc.sbuf_tensor("weights", [P, 2, NT], F32))
        bounds = ctx.enter_context(nc.sbuf_tensor("bounds", [1, E + 1], I32))
        with semaphores(nc) as sem, ExitStack() as stage:
            h2 = stage.enter_context(nc.sbuf_tensor("h2", [P, NT, C], F32))
            logitsT = stage.enter_context(nc.sbuf_tensor("logitsT", [E, (NT + LAG) * P], F32))
            proj_out(nc, sem, consts, mod_rows, w_proj, (y_hi, y_lo), x, x1, h2, logitsT)
            route(nc, sem, consts, h2, logitsT, slots, weights, bounds, rows)
        with semaphores(nc) as sem:
            experts(nc, sem, consts, mod_rows, expert_w, bounds, rows)
            combine(nc, sem, slots, weights, rows, x1, out)


def _constants():
    import numpy as np

    theta = np.float32(1.0) / np.float32(10000.0) ** (np.arange(0, D, 2, dtype=np.float32) / np.float32(D))
    angle = np.outer(np.arange(T, dtype=np.float32), theta.astype(np.float32)).astype(np.float32)
    d = np.arange(P) % D
    sign = np.where(d < D // 2, np.float32(-1), np.float32(1))[:, None]
    p = np.arange(P)
    causal = np.zeros((P, CH), np.float32)
    causal[:, CH - P:] = np.where(p[None, :] > p[:, None], np.float32(MASKED), np.float32(0))
    return {
        "ident": np.eye(P, dtype=np.float32),
        "block_mask": np.kron(np.eye(HG, dtype=np.float32), np.ones((D, D), np.float32)),
        "cos": np.ascontiguousarray(np.cos(angle).astype(np.float32).T[d % (D // 2)]),
        "sin": np.ascontiguousarray(np.sin(angle).astype(np.float32).T[d % (D // 2)] * sign),
        "causal": causal,
        "after": np.where(p[:, None] > p[None, :], np.float32(-1e30), np.float32(0)),
        "before": np.ascontiguousarray((p[:, None] < p[None, :]).astype(np.float32)),
        "numbers": np.tile(np.arange(E, dtype=np.float32), (P, 1)),
        "limits": np.tile(np.arange(1, T // MROWS, dtype=np.float32) * MROWS, (P, 1)),
    }


def kernel(**inputs):
    import numpy as np
    import concourse.bacc as bacc
    from concourse.bass_utils import run_bass_kernel_spmd

    a = {k: np.asarray(v) for k, v in inputs.items()}
    lay = {
        "x": a["L0_attn_x"].reshape(T, C),
        "w_attn": a["L0_attn_w_attn"].reshape(3 * G, P, KC, P).transpose(0, 3, 2, 1).reshape(3 * G, P, C),
        "w_proj": a["L0_attn_w_proj"].T,
        "adapter": a["L0_attn_adapter_wte"].T.reshape(KC, P, A).transpose(1, 0, 2),
        "gating": a["L0_attn_gating"],
        "gate_w": a["L0_ffn_gate_w"],
        "expert_w": a["L0_ffn_expert_w"],
        "c": a["L0_c"].reshape(KC, P).T,
        "wmod": a["L0_wmod"],
    }
    nc = bacc.Bacc("TRN2", target_bir_lowering=False, num_devices=1)
    arrays, aps = {}, {}
    for name, value in {**lay, **_constants()}.items():
        arrays[f"in_{name}"] = np.ascontiguousarray(value)
        aps[name] = nc.dram_tensor(f"in_{name}", list(value.shape), F32, kind="ExternalInput").ap()
    out = nc.dram_tensor("out", [T, C], F32, kind="ExternalOutput").ap()
    adaln_block(nc, *(aps[name] for name in lay), {name: aps[name] for name in _constants()}, out)
    r = run_bass_kernel_spmd(nc, [arrays], core_ids=[0])
    return r.results[0]["out"].reshape(1, T, C)
```
